# Optimizing a Trainium2 kernel written in Bass

```python
import numpy as np
import jax
import jax.numpy as jnp

def _softmax(x, axis=-1):
    return jax.nn.softmax(x, axis=axis)

def _gelu(x):
    return jax.nn.gelu(x, approximate=True)

def _silu(x):
    return jax.nn.silu(x)

def _sigmoid(x):
    return jax.nn.sigmoid(x)

def _layernorm(x, axis=-1, eps=1e-05):
    m = jnp.mean(x, axis=axis, keepdims=True)
    v = jnp.var(x, axis=axis, keepdims=True)
    return (x - m) / jnp.sqrt(v + eps)

def _scatter_add(tgt, idx, src, axis=0):
    return tgt.at[idx].add(src)

def _segment_sum(src, seg, n):
    return jax.ops.segment_sum(src, seg, n)
kernel_name = 'mk_decoder_postln_d2_seqx_r8_90a72e'

def setup_inputs(seed: int=0):
    np.random.seed(seed)
    _w = jnp.asarray

    def _rec_inputs():
        import jax
        import jax.numpy as jnp
        _rk = jax.random.key(seed)
        x = -7.109e-05 + 0.9999 * jax.random.normal(jax.random.fold_in(_rk, 1), (4, 256, 256), jnp.float32)
        _lenS = 256 - jax.random.randint(jax.random.fold_in(_rk, 7), (4,), 0, max(1, 256 // 4) + 1, jnp.int32)
        _lenS2 = 256 - jax.random.randint(jax.random.fold_in(_rk, 8), (4,), 0, max(1, 256 // 4) + 1, jnp.int32)
        _ctx_512P = jax.random.normal(jax.random.fold_in(_rk, 11), (4, 16, 64), jnp.float32)
        _ctx_512c = jax.random.dirichlet(jax.random.fold_in(_rk, 511), 0.3 * jnp.ones((16,), jnp.float32), (4, 256))
        _ctx_512t = jnp.einsum('bsk,bkd->bsd', _ctx_512c, _ctx_512P)
        _ctx_512t = _ctx_512t * jax.lax.rsqrt(jnp.mean(jnp.square(_ctx_512t)) + 1e-12) * 0.953939
        ctx_512 = 2.81802e-05 + 1.00001 * (_ctx_512t + 0.3 * jax.random.normal(jax.random.fold_in(_rk, 611), (4, 256, 64), jnp.float32))
        return (x, ctx_512)
    x, ctx_512 = _rec_inputs()

    def _L0_attn_setup():
        import jax, jax.numpy as jnp
        import numpy as np
        from jax import lax
        H, P, N, G, K, CHUNK = (64, 64, 128, 1, 4, 32)
        D_MODEL = 256
        D_INNER = H * P
        CONV_DIM = D_INNER + 2 * G * N
        EPS = 1e-05

        def _mamba2_forward(hidden_states, in_proj_w, conv_w, conv_b, dt_bias, A_log, D_param, norm_w, out_proj_w):
            b, l, _ = hidden_states.shape
            c = l // CHUNK
            proj = hidden_states @ in_proj_w
            gate = proj[..., :D_INNER]
            hbc = proj[..., D_INNER:D_INNER + CONV_DIM]
            dt = proj[..., D_INNER + CONV_DIM:]
            xt = hbc.transpose(0, 2, 1)
            y = lax.conv_general_dilated(xt, conv_w[:, None, :], window_strides=(1,), padding=[(K - 1, 0)], feature_group_count=CONV_DIM, dimension_numbers=('NCH', 'OIH', 'NCH'))
            hbc = jax.nn.silu(y + conv_b[None, :, None]).transpose(0, 2, 1)
            per_g = D_INNER // G
            hg = hbc.reshape(b, l, G, per_g + 2 * N)
            x = hg[..., :per_g].reshape(b, l, H, P)
            Bm = hg[..., per_g:per_g + N]
            Cm = hg[..., per_g + N:]
            hpg = H // G
            Bh = jnp.repeat(Bm, hpg, axis=2)
            Ch = jnp.repeat(Cm, hpg, axis=2)
            dt = jax.nn.softplus(dt + dt_bias)
            A = -jnp.exp(A_log)
            x_c = x.reshape(b, c, CHUNK, H, P)
            B_c = Bh.reshape(b, c, CHUNK, H, N)
            C_c = Ch.reshape(b, c, CHUNK, H, N)
            dt_c = dt.reshape(b, c, CHUNK, H)
            dA = dt_c * A[None, None, None, :]
            cum = jnp.cumsum(dA, axis=2)
            diff = cum[:, :, :, None, :] - cum[:, :, None, :, :]
            i = jnp.arange(CHUNK)
            mask = i[:, None] >= i[None, :]
            decay = jnp.exp(jnp.where(mask[None, None, :, :, None], diff, -jnp.inf))
            scores = jnp.einsum('bcihn,bcjhn->bcijh', C_c, B_c) * decay * dt_c[:, :, None, :, :]
            Y_diag = jnp.einsum('bcijh,bcjhp->bcihp', scores, x_c)
            decay_states = jnp.exp(cum[:, :, -1:, :] - cum)
            states = jnp.einsum('bclh,bclhn,bclhp->bchpn', decay_states * dt_c, B_c, x_c)
            chunk_decay = jnp.exp(cum[:, :, -1, :])

            def step(prev, inp):
                st, cd = inp
                new = cd[:, :, None, None] * prev + st
                return (new, prev)
            init = jnp.zeros((b, H, P, N), hidden_states.dtype)
            _, prev_states = lax.scan(step, init, (jnp.moveaxis(states, 1, 0), jnp.moveaxis(chunk_decay, 1, 0)))
            prev_states = jnp.moveaxis(prev_states, 0, 1)
            state_decay_out = jnp.exp(cum)
            Y_off = jnp.einsum('bclhn,bchpn,bclh->bclhp', C_c, prev_states, state_decay_out)
            yh = (Y_diag + Y_off).reshape(b, l, H, P) + D_param[None, None, :, None] * x
            yr = yh.reshape(b, l, D_INNER)
            hidden = yr * jax.nn.silu(gate)
            var = jnp.mean(hidden * hidden, axis=-1, keepdims=True)
            hidden = hidden * lax.rsqrt(var + EPS) * norm_w
            return hidden @ out_proj_w
        key = jax.random.key(seed)
        ks = jax.random.split(key, 6)
        s = lambda k, shape, scale: jax.random.normal(k, shape, jnp.float32) * scale
        return {'hidden_states': s(ks[0], (2, 256, D_MODEL), 1.0), 'in_proj_w': s(ks[1], (D_MODEL, D_INNER + CONV_DIM + H), D_MODEL ** (-0.5)), 'conv_w': s(ks[2], (CONV_DIM, K), K ** (-0.5)), 'conv_b': jnp.zeros((CONV_DIM,), jnp.float32), 'dt_bias': jnp.ones((H,), jnp.float32), 'A_log': jnp.log(jnp.arange(1, H + 1, dtype=jnp.float32)), 'D_param': jnp.ones((H,), jnp.float32), 'norm_w': jnp.ones((D_INNER,), jnp.float32), 'out_proj_w': s(ks[3], (D_INNER, D_MODEL), D_INNER ** (-0.5))}
    _L0_attn_all = _L0_attn_setup()
    _L0_attn_in = {k: v for k, v in _L0_attn_all.items() if k in ('in_proj_w', 'conv_w', 'conv_b', 'dt_bias', 'A_log', 'D_param', 'norm_w', 'out_proj_w')}
    del _L0_attn_all

    def _L0_xattn_setup():
        import jax, jax.numpy as jnp
        import numpy as np
        EPS = 1e-06
        IMAGE_DIMS = 256
        key = jax.random.key(seed)
        k1, k2, k3 = jax.random.split(key, 3)
        B, I, J, D = (16, 256, 256, 64)
        p = jax.random.normal(k1, (B, I, J), dtype=jnp.float32)
        k_v = jax.random.normal(k2, (B, J, D), dtype=jnp.float32)
        W_k = jax.random.normal(k3, (D, D), dtype=jnp.float32) * (1.0 / np.sqrt(D))
        b_k = jnp.zeros((D,), dtype=jnp.float32)
        ln_gamma = jnp.ones((J,), dtype=jnp.float32)
        ln_beta = jnp.zeros((J,), dtype=jnp.float32)
        return {'p': p, 'k_v': k_v, 'W_k': W_k, 'b_k': b_k, 'ln_gamma': ln_gamma, 'ln_beta': ln_beta}
    _L0_xattn_all = _L0_xattn_setup()
    _L0_xattn_in = {k: v for k, v in _L0_xattn_all.items() if k in ('W_k', 'b_k', 'ln_gamma', 'ln_beta')}
    del _L0_xattn_all

    def _L0_ffn_setup():
        import math
        import jax, jax.numpy as jnp
        import numpy as np
        DIM = 256
        RANK = 8
        B, T = (4, 512)

        def _orthogonal(key, n):
            a = jax.random.normal(key, (n, n), dtype=jnp.float32)
            q, r = jnp.linalg.qr(a)
            q = q * jnp.sign(jnp.diagonal(r))[None, :]
            return q
        key = jax.random.key(seed)
        kx, kf = jax.random.split(key)
        x = jax.random.normal(kx, (B, T, DIM), dtype=jnp.float32)
        fkeys = jax.random.split(kf, RANK)
        factors = jnp.stack([_orthogonal(fkeys[r], DIM) * (r + 1) ** (-0.5) for r in range(RANK)])
        bias = jnp.zeros((DIM,), dtype=jnp.float32)
        return {'x': x, 'factors': factors, 'bias': bias}
    _L0_ffn_all = _L0_ffn_setup()
    _L0_ffn_in = {k: v for k, v in _L0_ffn_all.items() if k in ('factors', 'bias')}
    del _L0_ffn_all

    def _L1_attn_setup():
        import jax, jax.numpy as jnp
        import numpy as np
        B, L, FUSED, DIM = (4, 72, 256, 256)
        DI, DS, DCONV, DTR = (2 * DIM, 16, 4, 128)

        def _mamba_params(key, prefix):
            ks = jax.random.split(key, 6)
            s_in = 1.0 / np.sqrt(DIM)
            s_di = 1.0 / np.sqrt(DI)
            s_dt = 1.0 / np.sqrt(DTR)
            A_log = jnp.log(jnp.broadcast_to(jnp.arange(1, DS + 1, dtype=jnp.float32), (DI, DS)))
            return {prefix + '_in_w': jax.random.normal(ks[0], (2 * DI, DIM), jnp.float32) * s_in, prefix + '_conv_w': jax.random.normal(ks[1], (DI, DCONV), jnp.float32) * 0.5, prefix + '_conv_b': jnp.zeros((DI,), jnp.float32), prefix + '_xproj_w': jax.random.normal(ks[2], (DTR + 2 * DS, DI), jnp.float32) * s_di, prefix + '_dt_w': jax.random.normal(ks[3], (DI, DTR), jnp.float32) * s_dt, prefix + '_dt_b': jax.random.normal(ks[4], (DI,), jnp.float32) * 0.1 - 4.0, prefix + '_A_log': A_log, prefix + '_D': jnp.ones((DI,), jnp.float32), prefix + '_out_w': jax.random.normal(ks[5], (DIM, DI), jnp.float32) * s_di}

        def _dw_conv(x, w, b):
            xt = jnp.transpose(x, (0, 2, 1))
            xp = jnp.pad(xt, ((0, 0), (0, 0), (DCONV - 1, 0)))
            Ln = xt.shape[-1]
            y = b[None, :, None]
            for kk in range(DCONV):
                y = y + w[:, kk][None, :, None] * xp[:, :, kk:kk + Ln]
            return jnp.transpose(y, (0, 2, 1))

        def _selective_scan(xi, dt, Bm, Cm, A, D):

            def step(h, inp):
                dt_t, B_t, C_t, x_t = inp
                dA = jnp.exp(dt_t[..., None] * A)
                h = dA * h + (dt_t * x_t)[..., None] * B_t[:, None, :]
                y = jnp.einsum('bds,bs->bd', h, C_t)
                return (h, y)
            h0 = jnp.zeros((xi.shape[0], DI, DS), xi.dtype)
            inps = (jnp.swapaxes(dt, 0, 1), jnp.swapaxes(Bm, 0, 1), jnp.swapaxes(Cm, 0, 1), jnp.swapaxes(xi, 0, 1))
            _, ys = jax.lax.scan(step, h0, inps)
            return jnp.swapaxes(ys, 0, 1) + xi * D

        def _mamba(x, in_w, conv_w, conv_b, xproj_w, dt_w, dt_b, A_log, D, out_w):
            xz = jnp.einsum('bld,ed->ble', x, in_w)
            xi, z = jnp.split(xz, 2, axis=-1)
            xi = jax.nn.silu(_dw_conv(xi, conv_w, conv_b))
            xdb = jnp.einsum('bld,ed->ble', xi, xproj_w)
            dtr, Bm, Cm = (xdb[..., :DTR], xdb[..., DTR:DTR + DS], xdb[..., DTR + DS:])
            dt = jax.nn.softplus(jnp.einsum('blr,dr->bld', dtr, dt_w) + dt_b)
            y = _selective_scan(xi, dt, Bm, Cm, -jnp.exp(A_log), D)
            y = y * jax.nn.silu(z)
            return jnp.einsum('bld,ed->ble', y, out_w)

        def _layernorm(x, g, b, eps=1e-05):
            mu = jnp.mean(x, -1, keepdims=True)
            var = jnp.mean(jnp.square(x - mu), -1, keepdims=True)
            return (x - mu) * jax.lax.rsqrt(var + eps) * g + b
        key = jax.random.key(seed)
        k = jax.random.split(key, 8)
        inp = {'img_patches': jax.random.normal(k[0], (B, L, FUSED), jnp.float32), 'w_in': jax.random.normal(k[1], (DIM, FUSED), jnp.float32) / np.sqrt(FUSED), 'b_in': jnp.zeros((DIM,), jnp.float32), 'ln_g': jnp.ones((DIM,), jnp.float32), 'ln_b': jnp.zeros((DIM,), jnp.float32), 'w_out': jax.random.normal(k[2], (DIM, DIM), jnp.float32) / np.sqrt(DIM), 'b_out': jnp.zeros((DIM,), jnp.float32)}
        inp.update(_mamba_params(k[3], 'fm'))
        inp.update(_mamba_params(k[4], 'bm'))
        return inp
    _L1_attn_all = _L1_attn_setup()
    _L1_attn_in = {k: v for k, v in _L1_attn_all.items() if k in ('w_in', 'b_in', 'fm_in_w', 'fm_conv_w', 'fm_conv_b', 'fm_xproj_w', 'fm_dt_w', 'fm_dt_b', 'fm_A_log', 'fm_D', 'fm_out_w', 'bm_in_w', 'bm_conv_w', 'bm_conv_b', 'bm_xproj_w', 'bm_dt_w', 'bm_dt_b', 'bm_A_log', 'bm_D', 'bm_out_w', 'ln_g', 'ln_b', 'w_out', 'b_out')}
    del _L1_attn_all

    def _L1_xattn_setup():
        import jax, jax.numpy as jnp
        import numpy as np
        B, S, L = (2, 128, 128)
        DIM_Q, H, K, D_C, D_CQ, R = (256, 16, 128, 64, 192, 64)

        def _rope_tables(length, dim):
            inv = 1.0 / 10000.0 ** (jnp.arange(0, dim, 2, dtype=jnp.float32) / dim)
            f = jnp.arange(length, dtype=jnp.float32)[:, None] * inv[None, :]
            sin = jnp.repeat(jnp.sin(f), 2, axis=-1)
            cos = jnp.repeat(jnp.cos(f), 2, axis=-1)
            return (sin, cos)

        def _rotate_half(x):
            half = x.shape[-1] // 2
            return jnp.concatenate([-x[..., half:], x[..., :half]], axis=-1)

        def _apply_rope(x, sin, cos):
            return x * cos + _rotate_half(x) * sin
        key = jax.random.key(seed)
        ks = jax.random.split(key, 8)
        return {'hidden_q': jax.random.normal(ks[0], (B, S, DIM_Q), jnp.float32), 'kv_c': jax.random.normal(ks[1], (B, L, D_C), jnp.float32), 'Wq': jax.random.normal(ks[2], (H * K, DIM_Q), jnp.float32) / np.sqrt(DIM_Q).astype(np.float32), 'w_kc_q': jax.random.normal(ks[3], (H, K, D_CQ), jnp.float32) / np.sqrt(K).astype(np.float32), 'w_kc_kv': jax.random.normal(ks[4], (H, K, D_C), jnp.float32) / np.sqrt(K).astype(np.float32), 'W_qr': jax.random.normal(ks[5], (H, D_CQ, R), jnp.float32) / np.float32(np.sqrt(D_CQ) * np.sqrt(R)), 'W_kr': jax.random.normal(ks[6], (H, D_C, R), jnp.float32) / np.sqrt(D_C).astype(np.float32), 'Wo': jax.random.normal(ks[7], (DIM_Q, H * K), jnp.float32) / np.sqrt(H * K).astype(np.float32)}
    _L1_xattn_all = _L1_xattn_setup()
    _L1_xattn_in = {k: v for k, v in _L1_xattn_all.items() if k in ('Wq', 'w_kc_q', 'w_kc_kv', 'W_qr', 'W_kr', 'Wo')}
    del _L1_xattn_all

    def _L1_ffn_setup():
        import jax, jax.numpy as jnp
        import numpy as np
        B, T, D = (4, 128, 256)
        N, S, H = (8, 8, 8)
        ETA = 1.0
        key = jax.random.key(seed)
        ks = jax.random.split(key, 9)
        return {'x': jax.random.normal(ks[0], (B, T, D), jnp.float32), 'select_weight': jax.random.normal(ks[1], (N, D, S), jnp.float32) / D, 'select_mean_diff': jax.random.normal(ks[2], (N, D), jnp.float32) / D, 'imp_center': jax.random.normal(ks[3], (N,), jnp.float32), 'imp_slope': jax.random.normal(ks[4], (N,), jnp.float32) * 5.0, 'lora_update': jax.random.normal(ks[5], (N, D, H), jnp.float32) * 0.02, 'lora_degen': jax.random.normal(ks[6], (N, D, H), jnp.float32) * 0.02, 'bias_w': jax.random.normal(ks[7], (N, D), jnp.float32) * 0.02, 'debias_w': jax.random.normal(ks[8], (N, D), jnp.float32) * 0.02}
    _L1_ffn_all = _L1_ffn_setup()
    _L1_ffn_in = {k: v for k, v in _L1_ffn_all.items() if k in ('select_weight', 'select_mean_diff', 'imp_center', 'imp_slope', 'lora_update', 'lora_degen', 'bias_w', 'debias_w')}
    del _L1_ffn_all
    return {'x': x, 'ctx_512': ctx_512, 'L0_attn_in_proj_w': _L0_attn_in['in_proj_w'], 'L0_attn_conv_w': _L0_attn_in['conv_w'], 'L0_attn_conv_b': _L0_attn_in['conv_b'], 'L0_attn_dt_bias': _L0_attn_in['dt_bias'], 'L0_attn_A_log': _L0_attn_in['A_log'], 'L0_attn_D_param': _L0_attn_in['D_param'], 'L0_attn_norm_w': _L0_attn_in['norm_w'], 'L0_attn_out_proj_w': _L0_attn_in['out_proj_w'], 'L0_xattn_W_k': _L0_xattn_in['W_k'], 'L0_xattn_b_k': _L0_xattn_in['b_k'], 'L0_xattn_ln_gamma': _L0_xattn_in['ln_gamma'], 'L0_xattn_ln_beta': _L0_xattn_in['ln_beta'], 'L0_ffn_factors': _L0_ffn_in['factors'], 'L0_ffn_bias': _L0_ffn_in['bias'], 'L1_attn_w_in': _L1_attn_in['w_in'], 'L1_attn_b_in': _L1_attn_in['b_in'], 'L1_attn_fm_in_w': _L1_attn_in['fm_in_w'], 'L1_attn_fm_conv_w': _L1_attn_in['fm_conv_w'], 'L1_attn_fm_conv_b': _L1_attn_in['fm_conv_b'], 'L1_attn_fm_xproj_w': _L1_attn_in['fm_xproj_w'], 'L1_attn_fm_dt_w': _L1_attn_in['fm_dt_w'], 'L1_attn_fm_dt_b': _L1_attn_in['fm_dt_b'], 'L1_attn_fm_A_log': _L1_attn_in['fm_A_log'], 'L1_attn_fm_D': _L1_attn_in['fm_D'], 'L1_attn_fm_out_w': _L1_attn_in['fm_out_w'], 'L1_attn_bm_in_w': _L1_attn_in['bm_in_w'], 'L1_attn_bm_conv_w': _L1_attn_in['bm_conv_w'], 'L1_attn_bm_conv_b': _L1_attn_in['bm_conv_b'], 'L1_attn_bm_xproj_w': _L1_attn_in['bm_xproj_w'], 'L1_attn_bm_dt_w': _L1_attn_in['bm_dt_w'], 'L1_attn_bm_dt_b': _L1_attn_in['bm_dt_b'], 'L1_attn_bm_A_log': _L1_attn_in['bm_A_log'], 'L1_attn_bm_D': _L1_attn_in['bm_D'], 'L1_attn_bm_out_w': _L1_attn_in['bm_out_w'], 'L1_attn_ln_g': _L1_attn_in['ln_g'], 'L1_attn_ln_b': _L1_attn_in['ln_b'], 'L1_attn_w_out': _L1_attn_in['w_out'], 'L1_attn_b_out': _L1_attn_in['b_out'], 'L1_xattn_Wq': _L1_xattn_in['Wq'], 'L1_xattn_w_kc_q': _L1_xattn_in['w_kc_q'], 'L1_xattn_w_kc_kv': _L1_xattn_in['w_kc_kv'], 'L1_xattn_W_qr': _L1_xattn_in['W_qr'], 'L1_xattn_W_kr': _L1_xattn_in['W_kr'], 'L1_xattn_Wo': _L1_xattn_in['Wo'], 'L1_ffn_select_weight': _L1_ffn_in['select_weight'], 'L1_ffn_select_mean_diff': _L1_ffn_in['select_mean_diff'], 'L1_ffn_imp_center': _L1_ffn_in['imp_center'], 'L1_ffn_imp_slope': _L1_ffn_in['imp_slope'], 'L1_ffn_lora_update': _L1_ffn_in['lora_update'], 'L1_ffn_lora_degen': _L1_ffn_in['lora_degen'], 'L1_ffn_bias_w': _L1_ffn_in['bias_w'], 'L1_ffn_debias_w': _L1_ffn_in['debias_w']}

def reference(x, ctx_512, L0_attn_in_proj_w, L0_attn_conv_w, L0_attn_conv_b, L0_attn_dt_bias, L0_attn_A_log, L0_attn_D_param, L0_attn_norm_w, L0_attn_out_proj_w, L0_xattn_W_k, L0_xattn_b_k, L0_xattn_ln_gamma, L0_xattn_ln_beta, L0_ffn_factors, L0_ffn_bias, L1_attn_w_in, L1_attn_b_in, L1_attn_fm_in_w, L1_attn_fm_conv_w, L1_attn_fm_conv_b, L1_attn_fm_xproj_w, L1_attn_fm_dt_w, L1_attn_fm_dt_b, L1_attn_fm_A_log, L1_attn_fm_D, L1_attn_fm_out_w, L1_attn_bm_in_w, L1_attn_bm_conv_w, L1_attn_bm_conv_b, L1_attn_bm_xproj_w, L1_attn_bm_dt_w, L1_attn_bm_dt_b, L1_attn_bm_A_log, L1_attn_bm_D, L1_attn_bm_out_w, L1_attn_ln_g, L1_attn_ln_b, L1_attn_w_out, L1_attn_b_out, L1_xattn_Wq, L1_xattn_w_kc_q, L1_xattn_w_kc_kv, L1_xattn_W_qr, L1_xattn_W_kr, L1_xattn_Wo, L1_ffn_select_weight, L1_ffn_select_mean_diff, L1_ffn_imp_center, L1_ffn_imp_slope, L1_ffn_lora_update, L1_ffn_lora_degen, L1_ffn_bias_w, L1_ffn_debias_w):
    import jax
    import jax.numpy as jnp

    def _L0_attn_ref(hidden_states, in_proj_w, conv_w, conv_b, dt_bias, A_log, D_param, norm_w, out_proj_w):
        import jax, jax.numpy as jnp
        import numpy as np
        from jax import lax
        H, P, N, G, K, CHUNK = (64, 64, 128, 1, 4, 32)
        D_MODEL = 256
        D_INNER = H * P
        CONV_DIM = D_INNER + 2 * G * N
        EPS = 1e-05

        def _mamba2_forward(hidden_states, in_proj_w, conv_w, conv_b, dt_bias, A_log, D_param, norm_w, out_proj_w):
            b, l, _ = hidden_states.shape
            c = l // CHUNK
            proj = hidden_states @ in_proj_w
            gate = proj[..., :D_INNER]
            hbc = proj[..., D_INNER:D_INNER + CONV_DIM]
            dt = proj[..., D_INNER + CONV_DIM:]
            xt = hbc.transpose(0, 2, 1)
            y = lax.conv_general_dilated(xt, conv_w[:, None, :], window_strides=(1,), padding=[(K - 1, 0)], feature_group_count=CONV_DIM, dimension_numbers=('NCH', 'OIH', 'NCH'))
            hbc = jax.nn.silu(y + conv_b[None, :, None]).transpose(0, 2, 1)
            per_g = D_INNER // G
            hg = hbc.reshape(b, l, G, per_g + 2 * N)
            x = hg[..., :per_g].reshape(b, l, H, P)
            Bm = hg[..., per_g:per_g + N]
            Cm = hg[..., per_g + N:]
            hpg = H // G
            Bh = jnp.repeat(Bm, hpg, axis=2)
            Ch = jnp.repeat(Cm, hpg, axis=2)
            dt = jax.nn.softplus(dt + dt_bias)
            A = -jnp.exp(A_log)
            x_c = x.reshape(b, c, CHUNK, H, P)
            B_c = Bh.reshape(b, c, CHUNK, H, N)
            C_c = Ch.reshape(b, c, CHUNK, H, N)
            dt_c = dt.reshape(b, c, CHUNK, H)
            dA = dt_c * A[None, None, None, :]
            cum = jnp.cumsum(dA, axis=2)
            diff = cum[:, :, :, None, :] - cum[:, :, None, :, :]
            i = jnp.arange(CHUNK)
            mask = i[:, None] >= i[None, :]
            decay = jnp.exp(jnp.where(mask[None, None, :, :, None], diff, -jnp.inf))
            scores = jnp.einsum('bcihn,bcjhn->bcijh', C_c, B_c) * decay * dt_c[:, :, None, :, :]
            Y_diag = jnp.einsum('bcijh,bcjhp->bcihp', scores, x_c)
            decay_states = jnp.exp(cum[:, :, -1:, :] - cum)
            states = jnp.einsum('bclh,bclhn,bclhp->bchpn', decay_states * dt_c, B_c, x_c)
            chunk_decay = jnp.exp(cum[:, :, -1, :])

            def step(prev, inp):
                st, cd = inp
                new = cd[:, :, None, None] * prev + st
                return (new, prev)
            init = jnp.zeros((b, H, P, N), hidden_states.dtype)
            _, prev_states = lax.scan(step, init, (jnp.moveaxis(states, 1, 0), jnp.moveaxis(chunk_decay, 1, 0)))
            prev_states = jnp.moveaxis(prev_states, 0, 1)
            state_decay_out = jnp.exp(cum)
            Y_off = jnp.einsum('bclhn,bchpn,bclh->bclhp', C_c, prev_states, state_decay_out)
            yh = (Y_diag + Y_off).reshape(b, l, H, P) + D_param[None, None, :, None] * x
            yr = yh.reshape(b, l, D_INNER)
            hidden = yr * jax.nn.silu(gate)
            var = jnp.mean(hidden * hidden, axis=-1, keepdims=True)
            hidden = hidden * lax.rsqrt(var + EPS) * norm_w
            return hidden @ out_proj_w
        return _mamba2_forward(hidden_states, in_proj_w, conv_w, conv_b, dt_bias, A_log, D_param, norm_w, out_proj_w)

    def _L0_xattn_ref(p, k_v, W_k, b_k, ln_gamma, ln_beta):
        import jax, jax.numpy as jnp
        import numpy as np
        EPS = 1e-06
        IMAGE_DIMS = 256
        kv = k_v @ W_k.T + b_k
        out = jnp.einsum('bij,bjd->bid', p, kv)
        scale = IMAGE_DIMS ** (-0.5)
        sim = jnp.einsum('bid,bjd->bij', out, kv) * scale
        mu = jnp.mean(sim, axis=-1, keepdims=True)
        var = jnp.var(sim, axis=-1, keepdims=True)
        sim = (sim - mu) * jax.lax.rsqrt(var + EPS) * ln_gamma + ln_beta
        attn = jax.nn.softmax(sim, axis=-1)
        return attn

    def _L0_ffn_ref(x, factors, bias):
        import math
        import jax, jax.numpy as jnp
        import numpy as np
        DIM = 256
        RANK = 8
        B, T = (4, 512)

        def _orthogonal(key, n):
            a = jax.random.normal(key, (n, n), dtype=jnp.float32)
            q, r = jnp.linalg.qr(a)
            q = q * jnp.sign(jnp.diagonal(r))[None, :]
            return q
        rank = factors.shape[0]
        mixed = jnp.einsum('btd,rde->bte', x, factors)
        mixed = mixed / math.sqrt(rank) + bias
        return mixed

    def _L1_attn_ref(img_patches, w_in, b_in, fm_in_w, fm_conv_w, fm_conv_b, fm_xproj_w, fm_dt_w, fm_dt_b, fm_A_log, fm_D, fm_out_w, bm_in_w, bm_conv_w, bm_conv_b, bm_xproj_w, bm_dt_w, bm_dt_b, bm_A_log, bm_D, bm_out_w, ln_g, ln_b, w_out, b_out):
        import jax, jax.numpy as jnp
        import numpy as np
        B, L, FUSED, DIM = (4, 72, 256, 256)
        DI, DS, DCONV, DTR = (2 * DIM, 16, 4, 128)

        def _mamba_params(key, prefix):
            ks = jax.random.split(key, 6)
            s_in = 1.0 / np.sqrt(DIM)
            s_di = 1.0 / np.sqrt(DI)
            s_dt = 1.0 / np.sqrt(DTR)
            A_log = jnp.log(jnp.broadcast_to(jnp.arange(1, DS + 1, dtype=jnp.float32), (DI, DS)))
            return {prefix + '_in_w': jax.random.normal(ks[0], (2 * DI, DIM), jnp.float32) * s_in, prefix + '_conv_w': jax.random.normal(ks[1], (DI, DCONV), jnp.float32) * 0.5, prefix + '_conv_b': jnp.zeros((DI,), jnp.float32), prefix + '_xproj_w': jax.random.normal(ks[2], (DTR + 2 * DS, DI), jnp.float32) * s_di, prefix + '_dt_w': jax.random.normal(ks[3], (DI, DTR), jnp.float32) * s_dt, prefix + '_dt_b': jax.random.normal(ks[4], (DI,), jnp.float32) * 0.1 - 4.0, prefix + '_A_log': A_log, prefix + '_D': jnp.ones((DI,), jnp.float32), prefix + '_out_w': jax.random.normal(ks[5], (DIM, DI), jnp.float32) * s_di}

        def _dw_conv(x, w, b):
            xt = jnp.transpose(x, (0, 2, 1))
            xp = jnp.pad(xt, ((0, 0), (0, 0), (DCONV - 1, 0)))
            Ln = xt.shape[-1]
            y = b[None, :, None]
            for kk in range(DCONV):
                y = y + w[:, kk][None, :, None] * xp[:, :, kk:kk + Ln]
            return jnp.transpose(y, (0, 2, 1))

        def _selective_scan(xi, dt, Bm, Cm, A, D):

            def step(h, inp):
                dt_t, B_t, C_t, x_t = inp
                dA = jnp.exp(dt_t[..., None] * A)
                h = dA * h + (dt_t * x_t)[..., None] * B_t[:, None, :]
                y = jnp.einsum('bds,bs->bd', h, C_t)
                return (h, y)
            h0 = jnp.zeros((xi.shape[0], DI, DS), xi.dtype)
            inps = (jnp.swapaxes(dt, 0, 1), jnp.swapaxes(Bm, 0, 1), jnp.swapaxes(Cm, 0, 1), jnp.swapaxes(xi, 0, 1))
            _, ys = jax.lax.scan(step, h0, inps)
            return jnp.swapaxes(ys, 0, 1) + xi * D

        def _mamba(x, in_w, conv_w, conv_b, xproj_w, dt_w, dt_b, A_log, D, out_w):
            xz = jnp.einsum('bld,ed->ble', x, in_w)
            xi, z = jnp.split(xz, 2, axis=-1)
            xi = jax.nn.silu(_dw_conv(xi, conv_w, conv_b))
            xdb = jnp.einsum('bld,ed->ble', xi, xproj_w)
            dtr, Bm, Cm = (xdb[..., :DTR], xdb[..., DTR:DTR + DS], xdb[..., DTR + DS:])
            dt = jax.nn.softplus(jnp.einsum('blr,dr->bld', dtr, dt_w) + dt_b)
            y = _selective_scan(xi, dt, Bm, Cm, -jnp.exp(A_log), D)
            y = y * jax.nn.silu(z)
            return jnp.einsum('bld,ed->ble', y, out_w)

        def _layernorm(x, g, b, eps=1e-05):
            mu = jnp.mean(x, -1, keepdims=True)
            var = jnp.mean(jnp.square(x - mu), -1, keepdims=True)
            return (x - mu) * jax.lax.rsqrt(var + eps) * g + b
        h = jax.nn.gelu(jnp.einsum('blf,df->bld', img_patches, w_in) + b_in, approximate=False)
        fwd = _mamba(h, fm_in_w, fm_conv_w, fm_conv_b, fm_xproj_w, fm_dt_w, fm_dt_b, fm_A_log, fm_D, fm_out_w)
        bwd = _mamba(jnp.flip(h, 1), bm_in_w, bm_conv_w, bm_conv_b, bm_xproj_w, bm_dt_w, bm_dt_b, bm_A_log, bm_D, bm_out_w)
        r = fwd + jnp.flip(bwd, 1) + h
        r = _layernorm(r, ln_g, ln_b)
        return jnp.einsum('bld,ed->ble', r, w_out) + b_out

    def _L1_xattn_ref(hidden_q, kv_c, Wq, w_kc_q, w_kc_kv, W_qr, W_kr, Wo):
        import jax, jax.numpy as jnp
        import numpy as np
        B, S, L = (2, 128, 128)
        DIM_Q, H, K, D_C, D_CQ, R = (256, 16, 128, 64, 192, 64)

        def _rope_tables(length, dim):
            inv = 1.0 / 10000.0 ** (jnp.arange(0, dim, 2, dtype=jnp.float32) / dim)
            f = jnp.arange(length, dtype=jnp.float32)[:, None] * inv[None, :]
            sin = jnp.repeat(jnp.sin(f), 2, axis=-1)
            cos = jnp.repeat(jnp.cos(f), 2, axis=-1)
            return (sin, cos)

        def _rotate_half(x):
            half = x.shape[-1] // 2
            return jnp.concatenate([-x[..., half:], x[..., :half]], axis=-1)

        def _apply_rope(x, sin, cos):
            return x * cos + _rotate_half(x) * sin
        Bv, Sv, _ = hidden_q.shape
        _, Lv, _ = kv_c.shape
        q_hk = (hidden_q @ Wq.T).reshape(Bv, Sv, H, K)
        q_big = jnp.einsum('bshk,hkq->bshq', q_hk, w_kc_q)
        sin_q, cos_q = _rope_tables(Sv, D_CQ)
        q_big = _apply_rope(q_big, sin_q[None, :, None, :], cos_q[None, :, None, :])
        sin_k, cos_k = _rope_tables(Lv, D_C)
        kv_r = _apply_rope(kv_c, sin_k[None], cos_k[None])
        q_r = jnp.einsum('bshq,hqr->bhsr', q_big, W_qr)
        k_r = jnp.einsum('bld,hdr->bhlr', kv_r, W_kr)
        scores = jnp.einsum('bhsr,bhlr->bhsl', q_r, k_r)
        attn = jax.nn.softmax(scores, axis=-1)
        ctx_c = jnp.einsum('bhsl,bld->bhsd', attn, kv_r)
        ctx_lat = jnp.einsum('bhsd,hkd->bhsk', ctx_c, w_kc_kv)
        ctx = ctx_lat.transpose(0, 2, 1, 3).reshape(Bv, Sv, H * K)
        return ctx @ Wo.T

    def _L1_ffn_ref(x, select_weight, select_mean_diff, imp_center, imp_slope, lora_update, lora_degen, bias_w, debias_w):
        import jax, jax.numpy as jnp
        import numpy as np
        B, T, D = (4, 128, 256)
        N, S, H = (8, 8, 8)
        ETA = 1.0
        x_diff = x[:, None, :, :] - select_mean_diff[None, :, None, :]
        x_diff = x_diff / jnp.linalg.norm(x_diff, axis=3, keepdims=True)
        cont = jnp.einsum('nds,bntd->bnts', select_weight, x_diff) ** 2
        score = cont.sum(axis=-1)
        gate = jax.nn.sigmoid(imp_slope[None, :, None] * (score - imp_center[None, :, None]))
        sel_scale = gate.max(axis=1)[..., None]
        sel_idx = gate.argmax(axis=1)
        debias = jnp.take(debias_w, sel_idx, axis=0)
        bias = jnp.take(bias_w, sel_idx, axis=0)
        upd = jnp.take(lora_update, sel_idx, axis=0)
        dgn = jnp.take(lora_degen, sel_idx, axis=0)
        x_debias = x - debias
        mod_x = jnp.einsum('btdh,btd->bth', upd, x_debias)
        degen_up = jnp.einsum('btdh,bth->btd', dgn, mod_x)
        mod_x_bias = ETA * (bias + degen_up)
        return (1.0 - sel_scale) * x + sel_scale * mod_x_bias
    x = _layernorm(x + _L0_attn_ref(x, L0_attn_in_proj_w, L0_attn_conv_w, L0_attn_conv_b, L0_attn_dt_bias, L0_attn_A_log, L0_attn_D_param, L0_attn_norm_w, L0_attn_out_proj_w), axis=-1)
    x = _layernorm(x + _L0_xattn_ref(x, ctx_512, L0_xattn_W_k, L0_xattn_b_k, L0_xattn_ln_gamma, L0_xattn_ln_beta), axis=-1)
    x = _layernorm(x + _L0_ffn_ref(x, L0_ffn_factors, L0_ffn_bias), axis=-1)
    x = _layernorm(x + _L1_attn_ref(x, L1_attn_w_in, L1_attn_b_in, L1_attn_fm_in_w, L1_attn_fm_conv_w, L1_attn_fm_conv_b, L1_attn_fm_xproj_w, L1_attn_fm_dt_w, L1_attn_fm_dt_b, L1_attn_fm_A_log, L1_attn_fm_D, L1_attn_fm_out_w, L1_attn_bm_in_w, L1_attn_bm_conv_w, L1_attn_bm_conv_b, L1_attn_bm_xproj_w, L1_attn_bm_dt_w, L1_attn_bm_dt_b, L1_attn_bm_A_log, L1_attn_bm_D, L1_attn_bm_out_w, L1_attn_ln_g, L1_attn_ln_b, L1_attn_w_out, L1_attn_b_out), axis=-1)
    x = _layernorm(x + _L1_xattn_ref(x, ctx_512, L1_xattn_Wq, L1_xattn_w_kc_q, L1_xattn_w_kc_kv, L1_xattn_W_qr, L1_xattn_W_kr, L1_xattn_Wo), axis=-1)
    x = _layernorm(x + _L1_ffn_ref(x, L1_ffn_select_weight, L1_ffn_select_mean_diff, L1_ffn_imp_center, L1_ffn_imp_slope, L1_ffn_lora_update, L1_ffn_lora_degen, L1_ffn_bias_w, L1_ffn_debias_w), axis=-1)
    return x

_drawn_inputs = setup_inputs


def setup_inputs(seed=0):
    import zlib

    import numpy as np

    out = dict(_drawn_inputs(seed))
    spreads = {'L0_attn_conv_b': (0.0, 0.1),
     'L0_attn_dt_bias': (1.0, 0.2),
     'L0_attn_D_param': (1.0, 0.2),
     'L0_attn_norm_w': (1.0, 0.2),
     'L0_xattn_b_k': (0.0, 2.0),
     'L0_xattn_ln_gamma': (1.0, 0.6),
     'L0_xattn_ln_beta': (0.0, 0.8),
     'L0_ffn_bias': (0.0, 0.1),
     'L1_attn_b_in': (0.0, 0.1),
     'L1_attn_fm_conv_b': (0.0, 0.358),
     'L1_attn_fm_D': (1.0, 0.6),
     'L1_attn_bm_conv_b': (0.0, 0.316),
     'L1_attn_bm_D': (1.0, 0.6),
     'L1_attn_ln_g': (1.0, 0.2),
     'L1_attn_ln_b': (0.0, 0.1),
     'L1_attn_b_out': (0.0, 0.1)}
    factors = {'L0_xattn_W_k': 8.0,
     'L1_attn_fm_xproj_w': 4.921,
     'L1_attn_fm_dt_w': 8.0,
     'L1_attn_fm_dt_b': 8.0,
     'L1_attn_fm_A_log': 6.578,
     'L1_attn_bm_xproj_w': 4.781,
     'L1_attn_bm_dt_w': 8.0,
     'L1_attn_bm_dt_b': 8.0,
     'L1_attn_bm_A_log': 8.0,
     'L1_ffn_select_weight': 64.0,
     'L1_ffn_select_mean_diff': 64.0,
     'L1_ffn_lora_update': 3.159,
     'L1_ffn_lora_degen': 3.126,
     'L1_ffn_bias_w': 2.95,
     'L1_ffn_debias_w': 8.0}
    for name, (base, spread) in spreads.items():
        noise = np.random.default_rng([zlib.crc32(name.encode()), seed]).standard_normal(out[name].shape)
        drawn = base * np.exp(spread * noise) if base else spread * noise
        out[name] = jnp.asarray(drawn.astype(out[name].dtype))
    for name, factor in factors.items():
        out[name] = (out[name] * factor).astype(out[name].dtype)
    return out
```

```python
from contextlib import ExitStack

import concourse.bass as bass
from concourse import mybir

F32 = mybir.dt.float32
BF16 = mybir.dt.bfloat16
ALU = mybir.AluOpType
ACT = mybir.ActivationFunctionType
AX = mybir.AxisListType

P = 128
BATCH, SEQ, D = 4, 256, 256
TOK = BATCH * SEQ
TILES = TOK // P
KD = D // P
HALVES = SEQ // P
CTX = 64
LN_EPS = 1e-5


class Chip:

    def __init__(self, nc, dram):
        self.nc, self.dram = nc, dram
        self.kept = ExitStack()
        self.part_sems = []

    def sem(self, name):
        return self.nc.alloc_semaphore(name)

    def part_sem(self, name):
        self.part_sems.append(self.nc.alloc_semaphore(name))
        return self.part_sems[-1]

    def end_part(self):
        self.nc.clear_and_free_semaphores(self.part_sems)
        self.nc.all_engine_barrier()
        self.part_sems = []

    def keep(self, name, shape, dtype=F32):
        return self.kept.enter_context(self.nc.sbuf_tensor(name, shape, dtype))


class Part:

    def __init__(self, chip, name, held):
        self.chip, self.name, self.held = chip, name, held

    def sb(self, name, shape, dtype=F32):
        return self.held.enter_context(self.chip.nc.sbuf_tensor(f"{self.name}_{name}", shape, dtype))

    def ps(self, name, shape, dtype=F32):
        return self.held.enter_context(self.chip.nc.psum_tensor(f"{self.name}_{name}", shape, dtype))

    def sem(self, name):
        return self.chip.part_sem(f"{self.name}_{name}")


def in_turn(eng, sem):
    count = [0]

    def then_wait(instruction):
        instruction.then_inc(sem, 1)
        count[0] += 1
        eng.wait_ge(sem, count[0])

    return then_wait


class PostNorm:

    def __init__(self, part, last=False):
        chip = part.chip
        self.chip, self.last = chip, last
        self.raw = part.sb("ln_raw", [P, TILES, 6])
        self.mean_var = part.sb("ln_mean_var", [P, TILES, 2])
        self.var_eps = part.sb("ln_var_eps", [P, TILES])
        self.rstd = part.sb("ln_rstd", [P, TILES])
        self.turned = part.ps("ln_turned", [P, 512])
        self.stats_ready = part.sem("ln_stats_ready")
        self.eps_added = part.sem("ln_eps_added")
        self.rstd_ready = part.sem("ln_rstd_ready")
        self.normed = part.sem("ln_normed")
        self.turned_ready = part.sem("ln_turned_ready")
        self.feat_ready = part.sem("ln_feat_ready")

    def stats(self, dve, then_wait, b):
        x = self.chip.x_tok
        for t in (2 * b, 2 * b + 1):
            then_wait(dve.bn_stats(self.raw[:, t, :], x[:, t, :]))
            dve.bn_aggr(self.mean_var[:, t, :], self.raw[:, t, :]).then_inc(self.stats_ready, 1)

    def rstds(self, pool):
        for b in range(BATCH):
            two = slice(2 * b, 2 * b + 2)
            pool.wait_ge(self.stats_ready, 2 * (b + 1))
            pool.tensor_scalar(self.var_eps[:, two], self.mean_var[:, two, 1], LN_EPS, None,
                               ALU.add).then_inc(self.eps_added, 1)
            pool.wait_ge(self.eps_added, b + 1)
            pool.tensor_tensor(self.rstd[:, two], self.var_eps[:, two], self.chip.minus_half[:, 0:2],
                               ALU.pow).then_inc(self.rstd_ready, 1)

    def scale(self, dve, b):
        x = self.chip.x_tok
        dve.wait_ge(self.rstd_ready, b + 1)
        for t in (2 * b, 2 * b + 1):
            dve.tensor_scalar(x[:, t, :], x[:, t, :], self.mean_var[:, t, 0:1], self.rstd[:, t:t + 1],
                              ALU.subtract, ALU.mult).then_inc(self.normed, 1)

    def turn(self, pe):
        if self.last:
            return
        for b in range(BATCH):
            pe.wait_ge(self.normed, 2 * (b + 1))
            if b:
                pe.wait_ge(self.feat_ready, b)
            for k in range(KD):
                for h in range(HALVES):
                    at = (k * HALVES + h) * P
                    turned = pe.transpose(self.turned[:, at:at + P],
                                          self.chip.x_tok[:, 2 * b + h, k * P:(k + 1) * P],
                                          self.chip.ident[:, :])
            turned.then_inc(self.turned_ready, 1)

    def write_feat(self, act):
        if self.last:
            return
        for b in range(BATCH):
            act.wait_ge(self.turned_ready, b + 1)
            act.activation(self.chip.x_feat[:, :, b * SEQ:(b + 1) * SEQ],
                           self.turned[:, :].rearrange("p (k t) -> p k t", k=KD),
                           ACT.Copy).then_inc(self.feat_ready, 1)


def ctx_attention(chip, name="xa"):
    nc, dram = chip.nc, chip.dram
    with ExitStack() as held:
        part = Part(chip, name, held)
        sb, ps, sem = part.sb, part.ps, part.sem
        norm = PostNorm(part)
        ctx_feat = sb("ctx_feat", [CTX, TOK])
        wk = sb("wk", [CTX, CTX])
        bk = sb("bk", [CTX, 1])
        gamma = sb("gamma", [P, SEQ])
        beta = sb("beta", [P, SEQ])
        kv_feat = sb("kv_feat", [CTX, TOK])
        kv_tok = sb("kv_tok", [P, TILES, CTX])
        mixed = sb("mixed", [CTX, BATCH, SEQ])
        raw = sb("raw", [P, TILES, 6])
        mean_var = sb("mean_var", [P, TILES, 2])
        var_eps = sb("var_eps", [P, TILES])
        rstd = sb("rstd", [P, TILES])
        sim = sb("sim", [P, BATCH, 2, SEQ])
        minus_max = sb("minus_max", [P, TILES])
        total = sb("total", [P, TILES])
        share = sb("share", [P, TILES])
        ps_kv = ps("ps_kv", [CTX, 2, 512])
        ps_kvt = ps("ps_kvt", [P, TILES, CTX])
        ps_mix = ps("ps_mix", [CTX, 512])
        ps_sim = ps("ps_sim", [P, 2, 2, SEQ])

        loaded, tables = sem("loaded"), sem("tables")
        kv_made, kv_kept, kv_turned, kv_tok_kept = sem("kv_made"), sem("kv_kept"), sem("kv_turned"), sem("kv_tok_kept")
        mix_made, mix_kept, sim_made = sem("mix_made"), sem("mix_kept"), sem("sim_made")
        stats_ready, eps_added, rstd_ready = sem("stats_ready"), sem("eps_added"), sem("rstd_ready")
        sim_read, max_ready, exp_ready, turn = sem("sim_read"), sem("max_ready"), sem("exp_ready"), sem("turn")

        with nc.Block() as block:

            @block.sync
            def _(sp):
                sp.dma_start(ctx_feat[:, :], dram["ctx_feat"]).then_inc(loaded, 16)
                sp.dma_start(wk[:, :], dram["L0_xattn_W_k_t"]).then_inc(loaded, 16)
                sp.dma_start(bk[:, :], dram["L0_xattn_b_k"]).then_inc(loaded, 16)
                sp.dma_start(gamma[:, :], dram["L0_xattn_ln_gamma"].partition_broadcast(P)).then_inc(tables, 16)
                sp.dma_start(beta[:, :], dram["L0_xattn_ln_beta"].partition_broadcast(P)).then_inc(tables, 16)

            @block.tensor
            def _(pe):
                pe.wait_ge(loaded, 48)
                for c in range(2):
                    kv = pe.matmul(ps_kv[:, c, :], wk[:, :], ctx_feat[:, c * 512:(c + 1) * 512],
                                   start=True, stop=True)
                kv.then_inc(kv_made, 1)
                pe.wait_ge(kv_kept, 1)
                for t in range(TILES):
                    turned = pe.transpose(ps_kvt[:, t, :], kv_feat[:, t * P:(t + 1) * P], chip.ident[0:CTX, 0:CTX])
                turned.then_inc(kv_turned, 1)
                pe.wait_ge(kv_tok_kept, 1)
                for b in range(BATCH):
                    if b:
                        pe.wait_ge(mix_kept, b)
                    for k in range(KD):
                        mix = pe.matmul(ps_mix[:, 0:SEQ], kv_tok[:, 2 * b + k, :],
                                        chip.x_feat[:, k, b * SEQ:(b + 1) * SEQ], start=(k == 0), stop=(k == KD - 1))
                    mix.then_inc(mix_made, 1)
                    pe.wait_ge(mix_kept, b + 1)
                    if b >= 2:
                        pe.wait_ge(sim_read, 2 * (b - 1))
                    for h in range(HALVES):
                        s = pe.matmul(ps_sim[:, b % 2, h, :], mixed[:, b, h * P:(h + 1) * P],
                                      kv_feat[:, b * SEQ:(b + 1) * SEQ], start=True, stop=True)
                    s.then_inc(sim_made, 1)
                norm.turn(pe)

            @block.scalar
            def _(act):
                act.wait_ge(kv_made, 1)
                act.activation(kv_feat[:, :], ps_kv[:, :, :].rearrange("p a t -> p (a t)"), ACT.Identity,
                               bias=bk[:, 0:1]).then_inc(kv_kept, 1)
                act.wait_ge(kv_turned, 1)
                act.activation(kv_tok[:, :, :], ps_kvt[:, :, :], ACT.Copy).then_inc(kv_tok_kept, 1)
                for b in range(BATCH):
                    act.wait_ge(mix_made, b + 1)
                    act.activation(mixed[:, b, :], ps_mix[:, 0:SEQ], ACT.Copy, scale=D ** -0.5).then_inc(mix_kept, 1)
                for b in range(BATCH):
                    act.wait_ge(max_ready, b + 1)
                    for h in range(HALVES):
                        t = 2 * b + h
                        act.activation(sim[:, b, h, :], sim[:, b, h, :], ACT.Exp, bias=minus_max[:, t:t + 1],
                                       accum_out=total[:, t:t + 1]).then_inc(exp_ready, 1)
                norm.write_feat(act)

            @block.gpsimd
            def _(pool):
                for b in range(BATCH):
                    two = slice(2 * b, 2 * b + 2)
                    pool.wait_ge(stats_ready, 2 * (b + 1))
                    pool.tensor_scalar(var_eps[:, two], mean_var[:, two, 1], 1e-6, None, ALU.add).then_inc(eps_added, 1)
                    pool.wait_ge(eps_added, b + 1)
                    pool.tensor_tensor(rstd[:, two], var_eps[:, two], chip.minus_half[:, 0:2],
                                       ALU.pow).then_inc(rstd_ready, 1)
                norm.rstds(pool)

            @block.vector
            def _(dve):
                then_wait = in_turn(dve, turn)

                def sim_stats(b):
                    dve.wait_ge(sim_made, b + 1)
                    for h in range(HALVES):
                        t = 2 * b + h
                        then_wait(dve.bn_stats(raw[:, t, :], ps_sim[:, b % 2, h, :]))
                        dve.bn_aggr(mean_var[:, t, :], raw[:, t, :]).then_inc(stats_ready, 1)

                def sim_norm(b):
                    dve.wait_ge(rstd_ready, b + 1)
                    for h in range(HALVES):
                        t = 2 * b + h
                        dve.tensor_scalar(sim[:, b, h, :], ps_sim[:, b % 2, h, :], mean_var[:, t, 0:1],
                                          rstd[:, t:t + 1], ALU.subtract, ALU.mult).then_inc(sim_read, 1)
                    dve.wait_ge(sim_read, 2 * (b + 1))
                    both = sim[:, b, :, :]
                    then_wait(dve.tensor_tensor(both, both, gamma[:, :].unsqueeze(1).to_broadcast([P, 2, SEQ]), ALU.mult))
                    then_wait(dve.tensor_tensor(both, both, beta[:, :].unsqueeze(1).to_broadcast([P, 2, SEQ]), ALU.add))
                    dve.tensor_reduce(minus_max[:, 2 * b:2 * b + 2], both, AX.X, ALU.max,
                                      negate=True).then_inc(max_ready, 1)

                def add_share(b):
                    dve.wait_ge(exp_ready, 2 * (b + 1))
                    then_wait(dve.reciprocal(share[:, 2 * b:2 * b + 2], total[:, 2 * b:2 * b + 2]))
                    for h in range(HALVES):
                        t = 2 * b + h
                        then_wait(dve.scalar_tensor_tensor(out=chip.x_tok[:, t, :], in0=sim[:, b, h, :],
                                                           scalar=share[:, t:t + 1], in1=chip.x_tok[:, t, :],
                                                           op0=ALU.mult, op1=ALU.add))
                    norm.stats(dve, then_wait, b)

                dve.wait_ge(tables, 32)
                sim_stats(0)
                for b in range(BATCH):
                    if b + 1 < BATCH:
                        sim_stats(b + 1)
                    sim_norm(b)
                    if b:
                        add_share(b - 1)
                    if b >= 2:
                        norm.scale(dve, b - 2)
                add_share(BATCH - 1)
                norm.scale(dve, BATCH - 2)
                norm.scale(dve, BATCH - 1)


def factor_ffn(chip, name="ff"):
    nc, dram = chip.nc, chip.dram
    rank = 8
    with ExitStack() as held:
        part = Part(chip, name, held)
        sb, ps, sem = part.sb, part.ps, part.sem
        norm = PostNorm(part)
        factors = sb("factors", [P, rank, KD, D])
        bias = sb("bias", [P, D])
        ps_out = ps("ps_out", [P, BATCH, 2, D])
        loaded, bias_loaded, summed, made, turn = sem("loaded"), sem("bias_loaded"), sem("summed"), sem("made"), sem("turn")
        with nc.Block() as block:

            @block.sync
            def _(sp):
                sp.dma_start(factors[:, :, :, :], dram["L0_ffn_factors"]).then_inc(loaded, 16)
                sp.dma_start(bias[:, :], dram["L0_ffn_bias"].partition_broadcast(P)).then_inc(bias_loaded, 16)

            @block.tensor
            def _(pe):
                pe.wait_ge(summed, 3)
                for t in range(TILES):
                    for k in range(KD):
                        out = pe.matmul(ps_out[:, t // 2, t % 2, :], chip.x_feat[:, k, t * P:(t + 1) * P],
                                        factors[:, 0, k, :], start=(k == 0), stop=(k == KD - 1))
                    out.then_inc(made, 1)
                norm.turn(pe)

            @block.scalar
            def _(act):
                norm.write_feat(act)

            @block.gpsimd
            def _(pool):
                norm.rstds(pool)

            @block.vector
            def _(dve):
                then_wait = in_turn(dve, turn)
                dve.wait_ge(loaded, 16)
                for n, left in enumerate((4, 2, 1)):
                    dve.tensor_tensor(factors[:, 0:left, :, :].rearrange("p r k d -> p (r k d)"),
                                      factors[:, 0:left, :, :].rearrange("p r k d -> p (r k d)"),
                                      factors[:, left:2 * left, :, :].rearrange("p r k d -> p (r k d)"),
                                      ALU.add).then_inc(summed, 1)
                    dve.wait_ge(summed, n + 1)
                dve.wait_ge(bias_loaded, 16)
                for b in range(BATCH):
                    x = chip.x_tok[:, 2 * b:2 * b + 2, :]
                    then_wait(dve.tensor_tensor(x, x, bias[:, :].unsqueeze(1).to_broadcast([P, 2, D]), ALU.add))
                    dve.wait_ge(made, 2 * (b + 1))
                    then_wait(dve.scalar_tensor_tensor(out=x, in0=ps_out[:, b, :, :], scalar=rank ** -0.5, in1=x,
                                                       op0=ALU.mult, op1=ALU.add))
                    norm.stats(dve, then_wait, b)
                    if b:
                        norm.scale(dve, b - 1)
                norm.scale(dve, BATCH - 1)


def expert_ffn(chip, name="ex"):
    nc, dram = chip.nc, chip.dram
    E, S, H = 8, 8, 8
    ES = E * S
    WIDE = 2 * ES + E
    with ExitStack() as held:
        part = Part(chip, name, held)
        sb, ps, sem = part.sb, part.ps, part.sem
        norm = PostNorm(part, last=True)
        weights = sb("weights", [P, KD, WIDE])
        away = sb("away", [P, KD, 2, E])
        dots = sb("dots", [P, KD, WIDE])
        down = sb("down", [ES + E, D])
        center = sb("center", [P, E])
        slope = sb("slope", [P, E])
        const = sb("const", [P, WIDE])
        proj = sb("proj", [P, TILES, WIDE])
        square = sb("square", [P, TILES, ES])
        x_square = sb("x_square", [P, D])
        x_norm = sb("x_norm", [P, TILES])
        score = sb("score", [P, TILES, E])
        dist = sb("dist", [P, TILES, E])
        gate = sb("gate", [P, TILES, E])
        key = sb("key", [P, TILES, E])
        best = sb("best", [P, TILES])
        rest = sb("rest", [P, TILES])
        best_key = sb("best_key", [P, TILES])
        rank_key = sb("rank_key", [P, E])
        picked = sb("picked", [P, TILES, ES + E])
        picked_t = sb("picked_t", [ES + E, TILES, P])
        ps_const = ps("ps_const", [P, 512])
        ps_proj = ps("ps_proj", [P, 2, 512])
        ps_turn = ps("ps_turn", [ES + E, 512])
        ps_out = ps("ps_out", [P, 2, 512])
        loaded, tables, dotted, const_made, const_kept = sem("loaded"), sem("tables"), sem("dotted"), sem("const_made"), sem("const_kept")
        proj_made, proj_kept, squared, scored, exped = sem("proj_made"), sem("proj_kept"), sem("squared"), sem("scored"), sem("exped")
        ranked, pick_ready, turned, turned_kept, made, mixed, turn, stored, x_scaled = (
            sem("ranked"), sem("pick_ready"), sem("turned"), sem("turned_kept"), sem("made"), sem("mixed"), sem("turn"),
            sem("stored"), sem("x_scaled"))
        with nc.Block() as block:

            @block.sync
            def _(sp):
                sp.dma_start(weights[:, :, :], dram["expert_in"]).then_inc(loaded, 16)
                sp.dma_start(away[:, :, :, :], dram["expert_away"]).then_inc(loaded, 16)
                sp.dma_start(down[:, :], dram["expert_down"]).then_inc(tables, 16)
                sp.dma_start(center[:, :], dram["L1_ffn_imp_center"].partition_broadcast(P)).then_inc(tables, 16)
                sp.dma_start(slope[:, :], dram["L1_ffn_imp_slope"].partition_broadcast(P)).then_inc(tables, 16)
                for b in range(BATCH):
                    sp.wait_ge(norm.normed, 2 * (b + 1))
                    sp.dma_start(dram["out"][:, 2 * b:2 * b + 2, :], chip.x_tok[:, 2 * b:2 * b + 2, :]).then_inc(stored, 16)
                sp.wait_ge(stored, 16 * BATCH)

            @block.tensor
            def _(pe):
                pe.wait_ge(loaded, 32)
                for t in range(TILES):
                    if t >= 2:
                        pe.wait_ge(proj_kept, t - 1)
                    for k in range(KD):
                        p = pe.matmul(ps_proj[:, t % 2, 0:WIDE], chip.x_feat[:, k, t * P:(t + 1) * P],
                                      weights[:, k, :], start=(k == 0), stop=(k == KD - 1))
                    p.then_inc(proj_made, 1)
                    if t == 1:
                        pe.wait_ge(dotted, 2 * KD + 1)
                        for k in range(KD):
                            c = pe.matmul(ps_const[:, 0:WIDE], chip.ones[:, :], dots[:, k, :],
                                          start=(k == 0), stop=(k == KD - 1))
                        c.then_inc(const_made, 1)
                for g in range(2):
                    pe.wait_ge(pick_ready, 1)
                    if g:
                        pe.wait_ge(turned_kept, g)
                    for t in range(4):
                        r = pe.transpose(ps_turn[:, t * P:(t + 1) * P], picked[:, 4 * g + t, :], chip.ident[:, :])
                    r.then_inc(turned, 1)
                pe.wait_ge(tables, 48)
                for b in range(BATCH):
                    pe.wait_ge(turned_kept, b // 2 + 1)
                    if b >= 2:
                        pe.wait_ge(mixed, b - 1)
                    for h in range(HALVES):
                        o = pe.matmul(ps_out[:, b % 2, h * D:(h + 1) * D], picked_t[:, 2 * b + h, :], down[:, :],
                                      start=True, stop=True)
                    o.then_inc(made, 1)

            @block.scalar
            def _(act):
                for t in range(TILES):
                    if t:
                        act.wait_ge(squared, t)
                    act.activation(x_square[:, :], chip.x_tok[:, t, :], ACT.Square,
                                   accum_out=x_norm[:, t:t + 1]).then_inc(squared, 1)
                act.wait_ge(scored, 1)
                act.activation(gate[:, :, :], score[:, :, :], ACT.Exp).then_inc(exped, 1)
                for g in range(2):
                    act.wait_ge(turned, g + 1)
                    act.activation(picked_t[:, 4 * g:4 * g + 4, :], ps_turn[:, :].rearrange("p (t c) -> p t c", t=4),
                                   ACT.Copy).then_inc(turned_kept, 1)

            @block.gpsimd
            def _(pool):
                for e in range(E):
                    pool.memset(rank_key[:, e:e + 1], float(E - e)).then_inc(ranked, 1)
                norm.rstds(pool)

            @block.vector
            def _(dve):
                then_wait = in_turn(dve, turn)
                dve.wait_ge(loaded, 32)
                for k in range(KD):
                    dve.tensor_tensor(dots[:, k, 0:2 * ES].rearrange("p (w e s) -> p w e s", w=2, e=E),
                                      weights[:, k, 0:2 * ES].rearrange("p (w e s) -> p w e s", w=2, e=E),
                                      away[:, k, :, :].unsqueeze(3).to_broadcast([P, 2, E, S]),
                                      ALU.mult).then_inc(dotted, 1)
                    dve.tensor_tensor(dots[:, k, 2 * ES:WIDE], away[:, k, 0, :], away[:, k, 0, :],
                                      ALU.mult).then_inc(dotted, 1)
                dve.wait_ge(chip.constants_ready, chip.CONSTANTS)
                dve.memset(best[:, :], 0.0).then_inc(dotted, 1)
                dve.wait_ge(const_made, 1)
                then_wait(dve.tensor_copy(const[:, :], ps_const[:, 0:WIDE]))
                for t in range(TILES):
                    dve.wait_ge(proj_made, t + 1)
                    dve.tensor_tensor(proj[:, t, 0:2 * ES], ps_proj[:, t % 2, 0:2 * ES], const[:, 0:2 * ES],
                                      ALU.subtract)
                    dve.scalar_tensor_tensor(out=proj[:, t, 2 * ES:WIDE], in0=ps_proj[:, t % 2, 2 * ES:WIDE],
                                             scalar=-2.0, in1=const[:, 2 * ES:WIDE], op0=ALU.mult,
                                             op1=ALU.add).then_inc(proj_kept, 1)
                dve.wait_ge(proj_kept, TILES)
                then_wait(dve.tensor_tensor(square[:, :, :], proj[:, :, 0:ES], proj[:, :, 0:ES], ALU.mult))
                then_wait(dve.tensor_reduce(score[:, :, :], square[:, :, :].rearrange("p t (e s) -> p t e s", e=E),
                                            AX.X, ALU.add))
                dve.wait_ge(squared, TILES)
                then_wait(dve.tensor_tensor(dist[:, :, :], proj[:, :, 2 * ES:WIDE],
                                            x_norm[:, :].unsqueeze(2).to_broadcast([P, TILES, E]), ALU.add))
                then_wait(dve.reciprocal(dist[:, :, :], dist[:, :, :]))
                then_wait(dve.tensor_tensor(score[:, :, :], score[:, :, :], dist[:, :, :], ALU.mult))
                dve.wait_ge(tables, 48)
                then_wait(dve.tensor_tensor(score[:, :, :], center[:, :].unsqueeze(1).to_broadcast([P, TILES, E]),
                                            score[:, :, :], ALU.subtract))
                then_wait(dve.tensor_tensor(score[:, :, :], score[:, :, :],
                                            slope[:, :].unsqueeze(1).to_broadcast([P, TILES, E]), ALU.mult))
                dve.tensor_scalar(score[:, :, :], score[:, :, :], 80.0, None, ALU.min).then_inc(scored, 1)
                dve.wait_ge(exped, 1)
                then_wait(dve.tensor_scalar(gate[:, :, :], gate[:, :, :], 1.0, None, ALU.add))
                then_wait(dve.reciprocal(gate[:, :, :], gate[:, :, :]))
                then_wait(dve.tensor_reduce(best[:, :], gate[:, :, :], AX.X, ALU.max))
                then_wait(dve.tensor_tensor(key[:, :, :], gate[:, :, :],
                                            best[:, :].unsqueeze(2).to_broadcast([P, TILES, E]), ALU.is_ge))
                dve.wait_ge(ranked, E)
                then_wait(dve.tensor_tensor(key[:, :, :], key[:, :, :],
                                            rank_key[:, :].unsqueeze(1).to_broadcast([P, TILES, E]), ALU.mult))
                then_wait(dve.tensor_reduce(best_key[:, :], key[:, :, :], AX.X, ALU.max))
                then_wait(dve.tensor_tensor(picked[:, :, ES:ES + E], key[:, :, :],
                                            best_key[:, :].unsqueeze(2).to_broadcast([P, TILES, E]), ALU.is_equal))
                then_wait(dve.tensor_scalar(rest[:, :], best[:, :], -1.0, 2.0, ALU.mult, ALU.add))
                for g in range(2):
                    four = slice(4 * g, 4 * g + 4)
                    then_wait(dve.tensor_tensor(picked[:, four, 0:ES].rearrange("p t (e s) -> p t e s", e=E),
                                                proj[:, four, ES:2 * ES].rearrange("p t (e s) -> p t e s", e=E),
                                                picked[:, four, ES:ES + E].unsqueeze(3).to_broadcast([P, 4, E, H]),
                                                ALU.mult))
                dve.memset(rank_key[:, 0:1], float(E)).then_inc(pick_ready, 1)
                for t in range(TILES):
                    then_wait(dve.tensor_scalar(chip.x_tok[:, t, :], chip.x_tok[:, t, :], rest[:, t:t + 1], None,
                                                ALU.mult))
                for b in range(BATCH):
                    dve.wait_ge(made, b + 1)
                    for h in range(HALVES):
                        t = 2 * b + h
                        mix = dve.scalar_tensor_tensor(out=chip.x_tok[:, t, :], in0=ps_out[:, b % 2, h * D:(h + 1) * D],
                                                       scalar=best[:, t:t + 1], in1=chip.x_tok[:, t, :],
                                                       op0=ALU.mult, op1=ALU.add)
                    mix.then_inc(mixed, 1)
                    dve.wait_ge(mixed, b + 1)
                    norm.stats(dve, then_wait, b)
                    if b:
                        norm.scale(dve, b - 1)
                norm.scale(dve, BATCH - 1)



def wait_if_positive(eng, sem, count):
    if isinstance(count, int) and count <= 0:
        return
    eng.wait_ge(sem, count)


M2_HEADS, M2_P, M2_N, M2_K = 64, 64, 128, 4
M2_INNER = M2_HEADS * M2_P
M2_CT = M2_INNER // P
M2_PAD = M2_K - 1
M2_VEC = M2_K + 1
M2_BLOCKS = 3 * P
HALF_TOK = TOK // 2
M2_W = 2 * KD * P
M2_ROW = M2_W + D


def mamba2_setup(chip, outer):
    nc, dram = chip.nc, chip.dram
    kept = Part(chip, "m2", outer)
    chip.m2_sel = kept.sb("sel", [3 * 32, 32, P], BF16)
    chip.m2_mask = kept.sb("mask", [P, P], BF16)
    chip.m2_ident = kept.sb("ident", [P, P], BF16)
    chip.m2_cum_parts = kept.sb("cum_parts", [3 * 32, 2, TOK], BF16)
    chip.m2_dt_tok = kept.sb("dt_tok", [P, TILES, 2, 32])
    chip.m2_minus_cum_tok = kept.sb("minus_cum_tok", [P, TILES, 2, 32])
    chip.m2_cb = kept.sb("cb", [P, BATCH, M2_BLOCKS])
    chip.m2_vec = kept.sb("vec", [P, M2_CT + 2, M2_VEC])
    chip.m2_d = kept.sb("d", [P, M2_CT])
    chip.m2_nw = kept.sb("nw", [P, M2_CT])
    with ExitStack() as held:
        part = Part(chip, "m2s", held)
        sb, ps, sem = part.sb, part.ps, part.sem
        w_dt = sb("w_dt", [P, KD, 2, 3 * 32])
        w_bc = sb("w_bc", [P, KD, 2, P])
        dt_bias = sb("dt_bias", [3 * 32, 2])
        a = sb("a", [3 * 32, 2])
        z = sb("z", [3 * 32, 2, TOK])
        soft = sb("soft", [3 * 32, 2, TOK])
        cum = sb("cum", [3 * 32, 2, TOK])
        mid = sb("mid", [3 * 32, 2, TOK], BF16)
        run_ones = sb("run_ones", [3 * 32, SEQ])
        mask_f = sb("mask_f", [P, P])
        pad = sb("pad", [P, 2, BATCH, M2_PAD + SEQ])
        conv = sb("conv", [P, 2, BATCH, SEQ])
        tanh = sb("tanh", [P, 2, TOK])
        ps_dt = ps("ps_dt", [P, 2, 2, 512])
        ps_bc = ps("ps_bc", [P, 2, 2, 512])

        loaded, vec_loaded, dt_made, bc_made = sem("loaded"), sem("vec_loaded"), sem("dt_made"), sem("bc_made")
        vec_ready, tables = sem("vec_ready"), sem("tables")
        padded, evacuated, z_ready, abs_ready, e_ready, ln_ready, a_ready = (
            sem("padded"), sem("evacuated"), sem("z_ready"), sem("abs_ready"), sem("e_ready"), sem("ln_ready"), sem("a_ready"))
        turn, dt_ready, cum_ready, tok_made, conv_ready, tanh_ready, bc_ready, cb_made, cb_kept = (
            sem("turn"), sem("dt_ready"), sem("cum_ready"), sem("tok_made"), sem("conv_ready"), sem("tanh_ready"),
            sem("bc_ready"), sem("cb_made"), sem("cb_kept"))

        with nc.Block() as block:

            @block.sync
            def _(sp):
                sp.dma_start(w_dt[:, :, :, :], dram["m2_w_dt"]).then_inc(loaded, 16)
                sp.dma_start(w_bc[:, :, :, :], dram["m2_w_bc"]).then_inc(loaded, 16)
                sp.dma_start(dt_bias[:, :], dram["m2_dt_bias"]).then_inc(loaded, 16)
                sp.dma_start(a[:, :], dram["m2_a_log"]).then_inc(loaded, 16)
                sp.dma_start(chip.m2_vec[:, :, :], dram["m2_vec"]).then_inc(vec_loaded, 16)
                sp.dma_start(chip.m2_d[:, :], dram["m2_d"]).then_inc(vec_loaded, 16)
                sp.dma_start(chip.m2_nw[:, :], dram["m2_nw"]).then_inc(vec_loaded, 16)

            @block.gpsimd
            def _(pool):
                pool.memset(pad[:, :, :, 0:M2_PAD], 0.0).then_inc(padded, 1)
                pool.memset(run_ones[:, :], 1.0).then_inc(padded, 1)
                pool.memset(mask_f[:, :], 0.0).then_inc(tables, 1)
                pool.memset(chip.m2_sel[:, :, :], 0.0).then_inc(tables, 1)
                pool.wait_ge(tables, 2)
                pool.affine_select(out=mask_f[:, :], in_=mask_f[:, :], compare_op=ALU.is_ge, fill=-1e30, base=0,
                                   pattern=[[1, P]], channel_multiplier=-1).then_inc(tables, 1)
                for r in range(3):
                    pool.affine_select(out=chip.m2_sel[:, :, :], in_=chip.m2_sel[:, :, :], compare_op=ALU.not_equal,
                                       fill=1.0, base=-32 * r, pattern=[[-1, 32], [0, P]],
                                       channel_multiplier=1).then_inc(tables, 1)
                    pool.wait_ge(tables, 4 + r)
                pool.tensor_copy(chip.m2_mask[:, :], mask_f[:, :]).then_inc(tables, 1)
                pool.tensor_copy(chip.m2_ident[:, :], chip.ident[:, :]).then_inc(tables, 1)
                pool.wait_ge(vec_loaded, 48)
                pool.tensor_scalar(chip.m2_vec[:, :, :], chip.m2_vec[:, :, :], 0.5, None, ALU.mult).then_inc(vec_ready, 1)
                pool.tensor_scalar(chip.m2_nw[:, :], chip.m2_nw[:, :], 0.5, None, ALU.mult).then_inc(vec_ready, 1)

            @block.tensor
            def _(pe):
                pe.wait_ge(loaded, 64)
                for group in range(2):
                    for half in range(2):
                        for k in range(KD):
                            m = pe.matmul(ps_dt[0:96, group, half, :], w_dt[:, k, group, :],
                                          chip.x_feat[:, k, half * 512:(half + 1) * 512], start=(k == 0), stop=(k == KD - 1))
                m.then_inc(dt_made, 1)
                for which in range(2):
                    for half in range(2):
                        for k in range(KD):
                            m = pe.matmul(ps_bc[:, which, half, :], w_bc[:, k, which, :],
                                          chip.x_feat[:, k, half * 512:(half + 1) * 512], start=(k == 0), stop=(k == KD - 1))
                    m.then_inc(bc_made, 1)
                pe.wait_ge(z_ready, 2)
                for n, (source, ready) in enumerate(((soft, dt_ready), (cum, cum_ready))):
                    pe.wait_ge(ready, 1 if n == 0 else BATCH * 2)
                    for t in range(TILES):
                        for group in range(2):
                            at = (t * 2 + group) * 32
                            m = pe.transpose(ps_dt[:, 0, n, at:at + 32], source[0:32, group, t * P:(t + 1) * P],
                                             chip.ident[0:32, 0:32])
                    m.then_inc(tok_made, 1)
                pe.wait_ge(bc_ready, 2)
                for b in range(BATCH):
                    for j in range(HALVES):
                        m = pe.matmul(ps_bc[:, b // 2, b % 2, j * SEQ:j * P + SEQ],
                                      tanh[:, 0, b * SEQ + j * P:b * SEQ + (j + 1) * P],
                                      tanh[:, 1, b * SEQ + j * P:(b + 1) * SEQ], start=True, stop=True)
                m.then_inc(cb_made, 1)

            @block.scalar
            def _(act):
                act.wait_ge(loaded, 64)
                act.activation(a[:, :], a[:, :], ACT.Exp).then_inc(a_ready, 1)
                act.wait_ge(dt_made, 1)
                for group in range(2):
                    act.activation(z[:, group, :], ps_dt[0:96, group, :, :].rearrange("p a t -> p (a t)"),
                                   ACT.Identity, bias=dt_bias[:, group:group + 1]).then_inc(z_ready, 1)
                act.wait_ge(z_ready, 2)
                act.wait_ge(bc_made, 2)
                act.wait_ge(padded, 2)
                for which in range(2):
                    for half in range(2):
                        act.activation(pad[:, which, 2 * half:2 * half + 2, M2_PAD:],
                                       ps_bc[:, which, half, :].rearrange("p (b t) -> p b t", b=2),
                                       ACT.Copy).then_inc(evacuated, 1)
                act.activation(soft[:, :, :], z[:, :, :], ACT.Abs).then_inc(abs_ready, 1)
                act.wait_ge(abs_ready, 1)
                act.activation(soft[:, :, :], soft[:, :, :], ACT.Exp, scale=-1.0).then_inc(e_ready, 1)
                act.wait_ge(e_ready, 1)
                act.activation(soft[:, :, :], soft[:, :, :], ACT.Ln, bias=1.0).then_inc(ln_ready, 1)
                act.wait_ge(conv_ready, 2)
                act.activation(tanh[:, :, :], conv[:, :, :, :].rearrange("p w b t -> p w (b t)"), ACT.Tanh).then_inc(tanh_ready, 1)
                act.wait_ge(tok_made, 2)
                act.activation(chip.m2_minus_cum_tok[:, :, :, :],
                               ps_dt[:, 0, 1, :].rearrange("p (t g n) -> p t g n", t=TILES, g=2), ACT.Copy,
                               scale=-1.0)
                act.activation(chip.m2_dt_tok[:, :, :, :],
                               ps_dt[:, 0, 0, :].rearrange("p (t g n) -> p t g n", t=TILES, g=2), ACT.Copy)
                act.wait_ge(cb_made, 1)
                act.activation(chip.m2_cb[:, :, :],
                               ps_bc[:, :, :, 0:M2_BLOCKS].rearrange("p a b t -> p (a b) t"), ACT.Copy).then_inc(cb_kept, 1)
                act.wait_ge(cb_kept, 1)

            @block.vector
            def _(dve):
                then_wait = in_turn(dve, turn)
                dve.wait_ge(vec_ready, 2)
                dve.wait_ge(evacuated, 4)
                for which in range(2):
                    vec = chip.m2_vec[:, M2_CT + which, :]
                    out = conv[:, which, :, :]
                    then_wait(dve.tensor_scalar(out, pad[:, which, :, M2_PAD:], vec[:, 3:4], vec[:, 4:5],
                                                ALU.mult, ALU.add))
                    for tap in range(M2_PAD):
                        m = dve.scalar_tensor_tensor(out=out, in0=pad[:, which, :, tap:tap + SEQ],
                                                     scalar=vec[:, tap:tap + 1], in1=out, op0=ALU.mult, op1=ALU.add)
                        if tap < M2_PAD - 1:
                            then_wait(m)
                    m.then_inc(conv_ready, 1)
                dve.wait_ge(ln_ready, 1)
                dve.scalar_tensor_tensor(out=soft[:, :, :], in0=z[:, :, :], scalar=0.0, in1=soft[:, :, :],
                                         op0=ALU.max, op1=ALU.add).then_inc(dt_ready, 1)
                dve.wait_ge(dt_ready, 1)
                dve.wait_ge(a_ready, 1)
                for group in range(2):
                    then_wait(dve.tensor_scalar(z[:, group, :], soft[:, group, :], a[:, group:group + 1], -1.0,
                                                ALU.mult, ALU.mult))
                for group in range(2):
                    for b in range(BATCH):
                        span = slice(b * SEQ, (b + 1) * SEQ)
                        dve.tensor_tensor_scan(cum[:, group, span], run_ones[:, :], z[:, group, span], 0.0,
                                               ALU.mult, ALU.add).then_inc(cum_ready, 1)
                dve.wait_ge(tanh_ready, 1)
                for which in range(2):
                    dve.scalar_tensor_tensor(out=tanh[:, which, :], in0=tanh[:, which, :], scalar=1.0,
                                             in1=conv[:, which, :, :].rearrange("p b t -> p (b t)"),
                                             op0=ALU.add, op1=ALU.mult).then_inc(bc_ready, 1)
                dve.wait_ge(cum_ready, 2 * BATCH)
                parts = chip.m2_cum_parts
                then_wait(dve.tensor_copy(parts[:, :, :], cum[:, :, :]))
                then_wait(dve.tensor_tensor(z[:, :, :], cum[:, :, :], parts[:, :, :], ALU.subtract))
                then_wait(dve.tensor_copy(mid[:, :, :], z[:, :, :]))
                then_wait(dve.tensor_tensor(z[:, :, :], z[:, :, :], mid[:, :, :], ALU.subtract))
                then_wait(dve.tensor_copy(parts[32:64, :, :], mid[32:64, :, :]))
                then_wait(dve.tensor_copy(parts[64:96, :, :], z[64:96, :, :]))


def mamba2_heads(chip):
    nc, dram = chip.nc, chip.dram
    STEPS = 2 * M2_CT
    with ExitStack() as held:
        part = Part(chip, "m2h", held)
        sb, ps, sem = part.sb, part.ps, part.sem
        w = sb("w", [P, 2, M2_ROW])
        wo = sb("wo", [P, 2, D])
        pad = sb("pad", [P, 2, 2, M2_PAD + SEQ])
        conv = sb("conv", [P, 2, 2, SEQ])
        tanh_x = sb("tanh_x", [P, HALF_TOK])
        xs = sb("xs", [P, 2, HALF_TOK])
        xdt = sb("xdt", [P, 4, 2, M2_P])
        G = sb("G", [P, 2, 2, 2, M2_BLOCKS])
        tanh_g = sb("tanh_g", [P, HALF_TOK])
        gate = sb("gate", [P, 2, HALF_TOK])
        y = sb("y", [P, HALF_TOK])
        hidden = sb("hidden", [P, 2, HALF_TOK])
        square = sb("square", [P, HALF_TOK])
        squares = sb("squares", [P, HALF_TOK])
        zeros = sb("zeros", [P, 512], BF16)
        rms = sb("rms", [P, 4])
        rms_inv = sb("rms_inv", [P, 4])
        ps_x = ps("ps_x", [P, 512])
        ps_g = ps("ps_g", [P, 512])
        ps_turn = ps("ps_turn", [P, 512])
        ps_y = ps("ps_y", [P, 512])
        ps_diff = ps("ps_diff", [P, 2, 512])
        ps_out = ps("ps_out", [P, 2, 2, D])

        w_loaded = [sem("w_loaded0"), sem("w_loaded1")]
        x_made, x_evac, conv_ready, tanh_x_ready, xs_ready, x_turned, xdt_ready = (
            sem("x_made"), sem("x_evac"), sem("conv_ready"), sem("tanh_x_ready"), sem("xs_ready"), sem("x_turned"),
            sem("xdt_ready"))
        g_made, tanh_g_ready, gate_ready = sem("g_made"), sem("tanh_g_ready"), sem("gate_ready")
        diff_made, exp_ready, G_ready, y_made, y_read, hidden_ready = (
            sem("diff_made"), sem("exp_ready"), sem("G_ready"), sem("y_made"), sem("y_read"), sem("hidden_ready"))
        square_ready, square_added, wo_ready, out_made = (
            sem("square_ready"), sem("square_added"), sem("wo_ready"), sem("out_made"))
        zeroed, sums_made, rms_ready, rms_inv_ready, out_read, turn = (
            sem("zeroed"), sem("sums_made"), sem("rms_ready"), sem("rms_inv_ready"), sem("out_read"), sem("turn"))

        def steps(eng, step):
            for g in (0, 1, 2):
                step(g, g % 2, g // 2, 0, 0)
            with eng.Fori(0, M2_CT // 2 - 2) as i:
                step(i * 2 + 3, 1, i + 1, 0, 0)
                step(i * 2 + 4, 0, i + 2, 0, 0)
            step(M2_CT - 1, 1, M2_CT // 2 - 1, 0, 0)
            step(M2_CT, 0, M2_CT // 2, 1, 0)
            step(M2_CT + 1, 1, M2_CT // 2, 1, 1)
            step(M2_CT + 2, 0, M2_CT // 2 + 1, 1, 1)
            with eng.Fori(0, M2_CT // 2 - 2) as i:
                step(i * 2 + M2_CT + 3, 1, i + M2_CT // 2 + 1, 1, 1)
                step(i * 2 + M2_CT + 4, 0, i + M2_CT // 2 + 2, 1, 1)
            step(STEPS - 1, 1, STEPS // 2 - 1, 1, 1)
            step(STEPS, 0, STEPS // 2, None, 1)

        with nc.Block() as block:

            @block.sync
            def _(sp):
                def step(g, q, u, half, _):
                    if half is None:
                        return
                    wait_if_positive(sp, g_made, g - 1)
                    wait_if_positive(sp, wo_ready, g - 1)
                    ct = g - M2_CT * half
                    src = dram["m2_w"][ct] if isinstance(ct, int) else dram["m2_w"][bass.ds(ct, 1), :, :].rearrange("a p n -> p (a n)")
                    sp.dma_start(w[:, q, :], src).then_inc(w_loaded[q], 16)

                steps(sp, step)

            @block.gpsimd
            def _(pool):
                pool.memset(zeros[:, :], 0.0).then_inc(zeroed, 1)
                pool.memset(pad[:, :, :, 0:M2_PAD], 0.0).then_inc(zeroed, 1)

                def step(g, q, u, half, prev):
                    if half is not None:
                        ct = g - M2_CT * half
                        pool.wait_ge(w_loaded[q], (u + 1) * 16)
                        wait_if_positive(pool, out_made, g - 1)
                        pool.tensor_tensor(wo[:, q, :], w[:, q, M2_W:M2_ROW],
                                           chip.m2_nw[:, bass.ds(ct, 1)].to_broadcast([P, D]), ALU.mult).then_inc(wo_ready, 1)
                        for b in range(2):
                            pool.wait_ge(exp_ready, g * 4 + 2 * b + 2)
                            pool.tensor_tensor(G[:, q, b, :, :], G[:, q, b, :, :],
                                               chip.m2_cb[:, 2 * half + b, :].unsqueeze(1).to_broadcast([P, 2, M2_BLOCKS]),
                                               ALU.mult).then_inc(G_ready, 1)
                    if isinstance(g, int) and g == 0:
                        return
                    pool.wait_ge(square_ready, g)
                    if isinstance(g, int) and g in (1, M2_CT + 1):
                        if g > 1:
                            pool.wait_ge(sums_made, 1)
                        pool.tensor_copy(squares[:, :], square[:, :]).then_inc(square_added, 1)
                    else:
                        pool.wait_ge(square_added, g - 1)
                        pool.tensor_tensor(squares[:, :], squares[:, :], square[:, :], ALU.add).then_inc(square_added, 1)
                    if isinstance(g, int) and g in (M2_CT, STEPS):
                        pool.wait_ge(rms_ready, g // M2_CT)
                        pool.tensor_tensor(rms_inv[:, :], rms[:, :], chip.minus_half[:, 0:1].to_broadcast([P, 4]),
                                           ALU.pow).then_inc(rms_inv_ready, 1)

                steps(pool, step)

            @block.scalar
            def _(act):
                act.wait_ge(zeroed, 2)

                def step(g, q, u, half, prev):
                    if half is not None:
                        ct = g - M2_CT * half

                        def exps(b):
                            for h in range(2):
                                n = 2 * b + h
                                act.wait_ge(diff_made, g * 4 + n + 1)
                                for j, (lo, hi) in enumerate(((0, SEQ), (SEQ, M2_BLOCKS))):
                                    e = act.activation(G[:, q, b, h, lo:hi], ps_diff[:, n % 2, lo:hi], ACT.Exp,
                                                       bias=chip.m2_minus_cum_tok[:, 4 * half + 2 * b + j, h, bass.ds(ct, 1)])
                                e.then_inc(exp_ready, 1)

                        wait_if_positive(act, y_made, g - 1)
                        exps(0)
                        act.wait_ge(x_made, g + 1)
                        wait_if_positive(act, conv_ready, g - 1)
                        act.activation(pad[:, q, :, M2_PAD:], ps_x[:, :].rearrange("p (b t) -> p b t", b=2),
                                       ACT.Copy).then_inc(x_evac, 1)
                        vec = chip.m2_vec[:, bass.ds(ct, 1), :].rearrange("p a v -> p (a v)")
                        act.activation(conv[:, q, :, :].rearrange("p b t -> p (b t)"), ps_x[:, :], ACT.Identity,
                                       scale=vec[:, 3:4], bias=vec[:, 4:5]).then_inc(x_evac, 1)
                        exps(1)
                        act.wait_ge(g_made, g + 1)
                        wait_if_positive(act, gate_ready, g)
                        act.activation(tanh_g[:, :], ps_g[:, :], ACT.Tanh, scale=0.5).then_inc(tanh_g_ready, 1)
                        act.wait_ge(conv_ready, g + 1)
                        wait_if_positive(act, xs_ready, g)
                        act.activation(tanh_x[:, :], conv[:, q, :, :].rearrange("p b t -> p (b t)"),
                                       ACT.Tanh).then_inc(tanh_x_ready, 1)
                    if isinstance(g, int) and g == 0:
                        return
                    act.wait_ge(hidden_ready, g)
                    wait_if_positive(act, square_added, g - 1)
                    act.activation(square[:, :], hidden[:, 1 - q, :], ACT.Square, scale=0.5).then_inc(square_ready, 1)

                steps(act, step)

            @block.tensor
            def _(pe):
                pe.wait_ge(zeroed, 2)

                def open_out():
                    for t in range(2):
                        pe.matmul(ps_out[:, t, :, :].rearrange("p a d -> p (a d)"), zeros[:, 0:P], zeros[:, :],
                                  start=True, stop=False)

                def step(g, q, u, half, prev):
                    is_first = isinstance(g, int) and g == 0
                    if half is not None:
                        ct = g - M2_CT * half
                        tokens = slice(half * HALF_TOK, (half + 1) * HALF_TOK)
                        sel = chip.m2_sel[:, bass.ds(ct, 1), :].rearrange("p a m -> p (a m)")

                        def diffs(b):
                            at = half * HALF_TOK + b * SEQ
                            for h in range(2):
                                n = 2 * b + h
                                wait_if_positive(pe, exp_ready, g * 4 + n - 1)
                                pe.matmul(ps_diff[:, n % 2, P:SEQ], sel, chip.m2_cum_parts[:, h, at + P:at + SEQ],
                                          start=True, stop=True)
                                diagonal = ps_diff[:, n % 2, :].rearrange("p (a i) -> p a i", a=2)[:, :, 0:P]
                                pe.matmul(diagonal, chip.m2_ident[:, :],
                                          chip.m2_mask[:, :].unsqueeze(1).to_broadcast([P, 2, P]), start=True, stop=False)
                                m = pe.matmul(diagonal, sel, chip.m2_cum_parts[:, h, at:at + SEQ].rearrange(
                                    "p (a i) -> p a i", a=2), start=False, stop=True)
                                m.then_inc(diff_made, 1)

                        diffs(0)
                        pe.wait_ge(w_loaded[q], (u + 1) * 16)
                        wait_if_positive(pe, x_evac, g * 2)
                        for k in range(KD):
                            m = pe.matmul(ps_x[:, :], w[:, q, k * P:(k + 1) * P], chip.x_feat[:, k, tokens],
                                          start=(k == 0), stop=(k == KD - 1))
                        m.then_inc(x_made, 1)
                    if not is_first:
                        pe.wait_ge(G_ready, g * 2)
                        pe.wait_ge(xdt_ready, g)
                        wait_if_positive(pe, y_read, g - 1)
                        for b in range(2):
                            for h in range(2):
                                for j, (lo, hi) in enumerate(((0, SEQ), (SEQ, M2_BLOCKS))):
                                    m = pe.matmul(ps_y[h * M2_P:(h + 1) * M2_P, b * SEQ + j * P:(b + 1) * SEQ],
                                                  xdt[:, 2 * b + j, h, :], G[:, 1 - q, b, h, lo:hi],
                                                  start=(j == 0), stop=(j == 1))
                        m.then_inc(y_made, 1)
                    if half is not None:
                        diffs(1)
                        wait_if_positive(pe, gate_ready, g)
                        for k in range(KD):
                            m = pe.matmul(ps_g[:, :], w[:, q, (KD + k) * P:(KD + k + 1) * P], chip.x_feat[:, k, tokens],
                                          start=(k == 0), stop=(k == KD - 1))
                        m.then_inc(g_made, 1)
                    if not is_first:
                        pe.wait_ge(hidden_ready, g)
                        pe.wait_ge(wo_ready, g)
                        for t in range(4):
                            m = pe.matmul(ps_out[:, t // 2, t % 2, :], hidden[:, 1 - q, t * P:(t + 1) * P], wo[:, 1 - q, :],
                                          start=False, stop=False)
                        m.then_inc(out_made, 1)
                    if isinstance(g, int) and g in (M2_CT, STEPS):
                        n = g // M2_CT
                        for t in range(2):
                            pe.matmul(ps_out[:, t, :, :].rearrange("p a d -> p (a d)"), zeros[:, 0:P], zeros[:, :],
                                      start=False, stop=True)
                        pe.wait_ge(square_added, g)
                        pe.wait_ge(xdt_ready, g)
                        for t in range(4):
                            m = pe.matmul(ps_turn[:, t:t + 1], squares[:, t * P:(t + 1) * P], chip.ones[:, 0:1],
                                          start=True, stop=True)
                        m.then_inc(sums_made, 1)
                        if n == 1:
                            pe.wait_ge(out_read, 4)
                            open_out()
                    if half is not None:
                        pe.wait_ge(xs_ready, g + 1)
                        wait_if_positive(pe, xdt_ready, g)
                        for t in range(4):
                            m = pe.transpose(ps_turn[:, t * P:(t + 1) * P], xs[:, q, t * P:(t + 1) * P], chip.ident[:, :])
                        m.then_inc(x_turned, 1)

                open_out()
                steps(pe, step)

            @block.vector
            def _(dve):
                def step(g, q, u, half, prev):
                    has_prev = not (isinstance(g, int) and g == 0)
                    ct = None if half is None else g - M2_CT * half

                    def add_tap(tap):
                        if half is None:
                            return
                        if tap:
                            dve.wait_ge(turn, g * 2 + tap)
                        out = conv[:, q, :, :]
                        m = dve.scalar_tensor_tensor(out=out, in0=pad[:, q, :, tap:tap + SEQ],
                                                     scalar=chip.m2_vec[:, bass.ds(ct, 1), tap], in1=out,
                                                     op0=ALU.mult, op1=ALU.add)
                        m.then_inc(turn if tap < M2_PAD - 1 else conv_ready, 1)

                    if half is not None:
                        dve.wait_ge(x_evac, g * 2 + 2)
                    add_tap(0)
                    if has_prev:
                        before = g - 1 - M2_CT * prev
                        dve.wait_ge(y_made, g)
                        dve.scalar_tensor_tensor(out=y[:, :], in0=xs[:, 1 - q, :], scalar=chip.m2_d[:, bass.ds(before, 1)],
                                                 in1=ps_y[:, :], op0=ALU.mult, op1=ALU.add).then_inc(y_read, 1)
                    add_tap(1)
                    if has_prev:
                        dve.wait_ge(y_read, g)
                        wait_if_positive(dve, out_made, g - 2)
                        wait_if_positive(dve, square_ready, g - 2)
                        dve.tensor_tensor(hidden[:, 1 - q, :], y[:, :], gate[:, 1 - q, :], ALU.mult).then_inc(hidden_ready, 1)
                    add_tap(2)
                    if half is not None:
                        dve.wait_ge(tanh_x_ready, g + 1)
                        dve.scalar_tensor_tensor(out=xs[:, q, :], in0=tanh_x[:, :], scalar=1.0,
                                                 in1=conv[:, q, :, :].rearrange("p b t -> p (b t)"),
                                                 op0=ALU.add, op1=ALU.mult).then_inc(xs_ready, 1)
                        dve.wait_ge(tanh_g_ready, g + 1)
                        dve.scalar_tensor_tensor(out=gate[:, q, :], in0=tanh_g[:, :], scalar=1.0, in1=ps_g[:, :],
                                                 op0=ALU.add, op1=ALU.mult).then_inc(gate_ready, 1)
                    if isinstance(g, int) and g in (M2_CT, STEPS):
                        n = g // M2_CT
                        dve.wait_ge(sums_made, n)
                        dve.tensor_scalar(rms[:, :], ps_turn[:, 0:4], 1.0 / M2_INNER, 1e-5, ALU.mult,
                                          ALU.add).then_inc(rms_ready, 1)
                        dve.wait_ge(rms_inv_ready, n)
                        for t in range(4):
                            x = chip.x_tok[:, 4 * (n - 1) + t, :]
                            dve.scalar_tensor_tensor(out=x, in0=ps_out[:, t // 2, t % 2, :], scalar=rms_inv[:, t:t + 1],
                                                     in1=x, op0=ALU.mult, op1=ALU.add).then_inc(out_read, 1)
                    if half is not None:
                        dve.wait_ge(x_turned, g + 1)
                        dve.tensor_tensor(xdt[:, :, :, :], ps_turn[:, :].rearrange("p (t h c) -> p t h c", t=4, h=2),
                                          chip.m2_dt_tok[:, 4 * half:4 * half + 4, :, bass.ds(ct, 1)].to_broadcast([P, 4, 2, M2_P]),
                                          ALU.mult).then_inc(xdt_ready, 1)

                steps(dve, step)


def post_norm(chip, name):
    with ExitStack() as held:
        part = Part(chip, name, held)
        norm = PostNorm(part)
        turn = part.sem("turn")
        with chip.nc.Block() as block:

            @block.vector
            def _(dve):
                then_wait = in_turn(dve, turn)
                for b in range(BATCH):
                    norm.stats(dve, then_wait, b)
                    if b:
                        norm.scale(dve, b - 1)
                norm.scale(dve, BATCH - 1)

            @block.gpsimd
            def _(pool):
                norm.rstds(pool)

            @block.tensor
            def _(pe):
                norm.turn(pe)

            @block.scalar
            def _(act):
                norm.write_feat(act)


def mamba2(chip):
    with ExitStack() as outer:
        mamba2_setup(chip, outer)
        mamba2_heads(chip)
    post_norm(chip, "m2n")


def mamba2_inputs(given):
    import numpy as np

    w = given["L0_attn_in_proj_w"]
    conv_end = M2_INNER + M2_INNER + 2 * M2_N

    def tiles(m):
        return m.reshape(KD, P, -1, P).transpose(2, 1, 0, 3)

    gate, x, bc, dt = (w[:, :M2_INNER], w[:, M2_INNER:2 * M2_INNER], w[:, 2 * M2_INNER:conv_end], w[:, conv_end:])
    by_group = lambda v: np.stack([np.concatenate([v[..., g::2]] * 3, axis=-1) for g in range(2)], axis=-2)
    vec = np.concatenate([given["L0_attn_conv_w"], given["L0_attn_conv_b"][:, None]], axis=1)
    return {
        "m2_w": np.concatenate([tiles(x).reshape(M2_CT, P, -1), tiles(gate).reshape(M2_CT, P, -1),
                                given["L0_attn_out_proj_w"].reshape(M2_CT, P, D)], axis=2),
        "m2_w_bc": tiles(bc).transpose(1, 2, 0, 3),
        "m2_w_dt": by_group(dt.reshape(KD, P, M2_HEADS)).transpose(1, 0, 2, 3),
        "m2_dt_bias": by_group(given["L0_attn_dt_bias"]).T,
        "m2_a_log": by_group(given["L0_attn_A_log"]).T,
        "m2_vec": vec.reshape(M2_CT + 2, P, M2_VEC).transpose(1, 0, 2),
        "m2_d": np.repeat(given["L0_attn_D_param"], M2_P).reshape(M2_CT, P).T,
        "m2_nw": given["L0_attn_norm_w"].reshape(M2_CT, P).T,
    }


MORE = [mamba2_inputs]



BM_DI, BM_DS, BM_K, BM_R = 512, 16, 4, 128
BM_CT = BM_DI // P
BM_PAD = BM_K - 1


def bi_head(chip, part, h_feat):
    nc, dram = chip.nc, chip.dram
    w_in = part.sb("w_in", [P, KD, D])
    b_in = part.sb("b_in", [P, KD])
    loaded, made, h_ready = part.sem("head_loaded"), part.sem("head_made"), part.sem("h_ready")
    with ExitStack() as held:
        ps_h = Part(chip, "bmh", held).ps("ps_h", [P, KD, 2, 512])
        with nc.Block() as block:

            @block.sync
            def _(sp):
                sp.dma_start(w_in[:, :, :], dram["bm_w_in"]).then_inc(loaded, 16)
                sp.dma_start(b_in[:, :], dram["bm_b_in"]).then_inc(loaded, 16)

            @block.tensor
            def _(pe):
                pe.wait_ge(loaded, 32)
                for m in range(KD):
                    for half in range(2):
                        for k in range(KD):
                            o = pe.matmul(ps_h[:, m, half, :], w_in[:, k, m * P:(m + 1) * P],
                                          chip.x_feat[:, k, half * 512:(half + 1) * 512], start=(k == 0), stop=(k == KD - 1))
                    o.then_inc(made, 1)

            @block.scalar
            def _(act):
                for m in range(KD):
                    act.wait_ge(made, m + 1)
                    act.activation(h_feat[:, m, :], ps_h[:, m, :, :].rearrange("p a t -> p (a t)"), ACT.Gelu,
                                   bias=b_in[:, m:m + 1]).then_inc(h_ready, 1)


def bi_setup(chip, way, name, back, bufs):
    nc, dram = chip.nc, chip.dram
    xi, z, dt, u, A, skip, h_feat = bufs
    with ExitStack() as held:
        part = Part(chip, name, held)
        sb, ps, sem = part.sb, part.ps, part.sem
        w_xz = sb("w_xz", [P, KD, 2 * BM_DI])
        w_proj = sb("w_proj", [P, BM_CT, BM_R + 2 * BM_DS])
        w_dt = sb("w_dt", [P, BM_DI])
        vec = sb("vec", [P, BM_CT, BM_K + 1])
        dt_b = sb("dt_b", [P, BM_CT])
        pad = sb("pad", [P, 2, BATCH, SEQ + BM_PAD])
        tanh = sb("tanh", [P, TOK])
        rank = sb("rank", [P, TOK])
        bc = sb("bc", [2 * BM_DS, TOK])
        ln = sb("ln", [P, 2, TOK])
        series = sb("series", [P, TOK])
        is_small = sb("is_small", [P, TOK], mybir.dt.int32)
        ps_a = ps("ps_a", [P, 2, 2, 512])
        ps_rank = ps("ps_rank", [P, 2, 512])
        ps_bc = ps("ps_bc", [2 * BM_DS, 2, 512])
        loaded, vec_loaded, vec_ready, padded, a_ready = (
            sem("loaded"), sem("vec_loaded"), sem("vec_ready"), sem("padded"), sem("a_ready"))
        made, evac, conv_ready, tanh_ready, silu_ready = (
            sem("made"), sem("evac"), sem("conv_ready"), sem("tanh_ready"), sem("silu_ready"))
        proj_made, rank_ready, bc_ready, bc_stored, dt_made, dt_evac = (
            sem("proj_made"), sem("rank_ready"), sem("bc_ready"), sem("bc_stored"), sem("dt_made"), sem("dt_evac"))
        soft_ready, dt_ready, u_ready, turn, exp_ready = (
            sem("soft_ready"), sem("dt_ready"), sem("u_ready"), sem("turn"), sem("exp_ready"))
        own = 0 if back else BM_PAD
        tap_at = lambda tap: BM_PAD - tap if back else tap

        with nc.Block() as block:

            @block.sync
            def _(sp):
                sp.dma_start(w_xz[:, :, :], dram[f"{way}_w_xz"]).then_inc(loaded, 16)
                sp.dma_start(w_proj[:, :, :], dram[f"{way}_w_proj"]).then_inc(loaded, 16)
                sp.dma_start(w_dt[:, :], dram[f"{way}_w_dt"]).then_inc(loaded, 16)
                sp.dma_start(vec[:, :, :], dram[f"{way}_vec"]).then_inc(vec_loaded, 16)
                sp.dma_start(dt_b[:, :], dram[f"{way}_dt_b"]).then_inc(vec_loaded, 16)
                sp.dma_start(A[:, :, :], dram[f"{way}_a_log"]).then_inc(vec_loaded, 16)
                sp.dma_start(skip[:, :], dram[f"{way}_d"]).then_inc(vec_loaded, 16)
                sp.wait_ge(bc_ready, 1)
                sp.dma_start(dram["bm_bc"][back], bc[:, :]).then_inc(bc_stored, 16)
                sp.wait_ge(bc_stored, 16)

            @block.gpsimd
            def _(pool):
                zeros = slice(SEQ, SEQ + BM_PAD) if back else slice(0, BM_PAD)
                pool.memset(pad[:, :, :, zeros], 0.0).then_inc(padded, 1)
                pool.wait_ge(vec_loaded, 64)
                pool.tensor_scalar(vec[:, :, :], vec[:, :, :], 0.5, None, ALU.mult).then_inc(vec_ready, 1)
                pool.wait_ge(a_ready, 1)
                pool.tensor_scalar(A[:, :, :], A[:, :, :], -1.0, None, ALU.mult).then_inc(vec_ready, 1)

            @block.tensor
            def _(pe):
                pe.wait_ge(loaded, 48)
                for m in range(2 * BM_CT):
                    if m >= 2:
                        if m - 2 < BM_CT:
                            pe.wait_ge(evac, 2 * (m - 1))
                        else:
                            pe.wait_ge(silu_ready, m - 1)
                    for half in range(2):
                        for k in range(KD):
                            o = pe.matmul(ps_a[:, m % 2, half, :], w_xz[:, k, m * P:(m + 1) * P],
                                          h_feat[:, k, half * 512:(half + 1) * 512], start=(k == 0), stop=(k == KD - 1))
                    o.then_inc(made, 1)
                pe.wait_ge(silu_ready, BM_CT)
                for half in range(2):
                    span = slice(half * 512, (half + 1) * 512)
                    for k in range(BM_CT):
                        pe.matmul(ps_rank[:, half, :], w_proj[:, k, 0:BM_R], xi[:, k, span], start=(k == 0), stop=(k == BM_CT - 1))
                    for k in range(BM_CT):
                        o = pe.matmul(ps_bc[:, half, :], w_proj[:, k, BM_R:], xi[:, k, span], start=(k == 0), stop=(k == BM_CT - 1))
                o.then_inc(proj_made, 1)
                pe.wait_ge(rank_ready, 1)
                pe.wait_ge(silu_ready, 2 * BM_CT)
                for m in range(BM_CT):
                    if m >= 2:
                        pe.wait_ge(dt_evac, m - 1)
                    for half in range(2):
                        o = pe.matmul(ps_a[:, m % 2, half, :], w_dt[:, m * P:(m + 1) * P], rank[:, half * 512:(half + 1) * 512],
                                      start=True, stop=True)
                    o.then_inc(dt_made, 1)

            @block.scalar
            def _(act):
                act.wait_ge(padded, 1)
                act.wait_ge(vec_loaded, 64)
                act.activation(A[:, :, :], A[:, :, :], ACT.Exp).then_inc(a_ready, 1)
                act.wait_ge(vec_ready, 1)

                def tile(m):
                    flat = ps_a[:, m % 2, :, :].rearrange("p a t -> p (a t)")
                    act.wait_ge(made, m + 1)
                    if m < BM_CT:
                        if m >= 2:
                            act.wait_ge(conv_ready, m - 1)
                        act.activation(pad[:, m % 2, :, own:own + SEQ], flat.rearrange("p (b t) -> p b t", b=BATCH),
                                       ACT.Copy).then_inc(evac, 1)
                        act.activation(xi[:, m, :], flat, ACT.Identity, scale=vec[:, m, BM_K - 1:BM_K],
                                       bias=vec[:, m, BM_K:BM_K + 1]).then_inc(evac, 1)
                    else:
                        act.wait_ge(silu_ready, m)
                        act.activation(tanh[:, :], flat, ACT.Tanh, scale=0.5).then_inc(tanh_ready, 1)

                def tanh_x(m):
                    act.wait_ge(conv_ready, m + 1)
                    if m:
                        act.wait_ge(silu_ready, m)
                    act.activation(tanh[:, :], xi[:, m, :], ACT.Tanh).then_inc(tanh_ready, 1)

                tile(0)
                for m in range(1, BM_CT):
                    tile(m)
                    tanh_x(m - 1)
                tanh_x(BM_CT - 1)
                for m in range(BM_CT, 2 * BM_CT):
                    tile(m)
                act.wait_ge(proj_made, 1)
                act.activation(rank[:, :], ps_rank[:, :, :].rearrange("p a t -> p (a t)"), ACT.Copy).then_inc(rank_ready, 1)
                act.activation(bc[:, :], ps_bc[:, :, :].rearrange("p a t -> p (a t)"), ACT.Copy).then_inc(bc_ready, 1)
                for m in range(BM_CT):
                    act.wait_ge(dt_made, m + 1)
                    act.activation(dt[:, m, :], ps_a[:, m % 2, :, :].rearrange("p a t -> p (a t)"), ACT.Identity,
                                   bias=dt_b[:, m:m + 1]).then_inc(dt_evac, 1)
                act.wait_ge(dt_evac, BM_CT)
                act.activation(u[:, :, :], dt[:, :, :], ACT.Abs).then_inc(exp_ready, 1)
                act.wait_ge(exp_ready, 1)
                act.activation(u[:, :, :], u[:, :, :], ACT.Exp, scale=-1.0).then_inc(exp_ready, 1)
                act.wait_ge(exp_ready, 2)
                for m in range(BM_CT):
                    if m >= 2:
                        act.wait_ge(dt_ready, m - 1)
                    act.activation(ln[:, m % 2, :], u[:, m, :], ACT.Ln, bias=1.0).then_inc(soft_ready, 1)

            @block.vector
            def _(dve):
                then_wait = in_turn(dve, turn)
                dve.wait_ge(vec_ready, 1)
                for m in range(BM_CT):
                    dve.wait_ge(evac, 2 * (m + 1))
                    out = xi[:, m, :].rearrange("p (b t) -> p b t", b=BATCH)
                    for tap in range(BM_PAD):
                        at = tap_at(tap)
                        c = dve.scalar_tensor_tensor(out=out, in0=pad[:, m % 2, :, at:at + SEQ], scalar=vec[:, m, tap:tap + 1],
                                                     in1=out, op0=ALU.mult, op1=ALU.add)
                        if tap < BM_PAD - 1:
                            then_wait(c)
                    c.then_inc(conv_ready, 1)
                    dve.wait_ge(tanh_ready, m + 1)
                    dve.scalar_tensor_tensor(out=xi[:, m, :], in0=tanh[:, :], scalar=1.0, in1=xi[:, m, :],
                                             op0=ALU.add, op1=ALU.mult).then_inc(silu_ready, 1)
                for m in range(BM_CT, 2 * BM_CT):
                    dve.wait_ge(tanh_ready, m + 1)
                    dve.scalar_tensor_tensor(out=z[:, m - BM_CT, :], in0=tanh[:, :], scalar=1.0,
                                             in1=ps_a[:, m % 2, :, :].rearrange("p a t -> p (a t)"),
                                             op0=ALU.add, op1=ALU.mult).then_inc(silu_ready, 1)
                dve.wait_ge(exp_ready, 2)
                for m in range(BM_CT):
                    e, t = u[:, m, :], series[:, :]
                    then_wait(dve.tensor_scalar(t, e, 1.0 / 3.0, -0.5, ALU.mult, ALU.add))
                    then_wait(dve.tensor_tensor(t, t, e, ALU.mult))
                    then_wait(dve.tensor_scalar(is_small[:, :], e, 1.0 / 128.0, None, ALU.is_lt))
                    then_wait(dve.scalar_tensor_tensor(out=t, in0=t, scalar=1.0, in1=e, op0=ALU.add, op1=ALU.mult))
                    dve.wait_ge(soft_ready, m + 1)
                    then_wait(dve.copy_predicated(ln[:, m % 2, :], is_small[:, :], t))
                    dve.scalar_tensor_tensor(out=dt[:, m, :], in0=dt[:, m, :], scalar=0.0, in1=ln[:, m % 2, :],
                                             op0=ALU.max, op1=ALU.add).then_inc(dt_ready, 1)
                    dve.wait_ge(dt_ready, m + 1)
                    dve.tensor_tensor(u[:, m, :], dt[:, m, :], xi[:, m, :], ALU.mult).then_inc(u_ready, 1)
                dve.wait_ge(u_ready, BM_CT)


def bi_scan(chip, name, back, bufs):
    nc, dram = chip.nc, chip.dram
    xi, z, dt, u, A, skip, _ = bufs
    with ExitStack() as held:
        part = Part(chip, name, held)
        sb, ps, sem = part.sb, part.ps, part.sem
        bc = sb("bc", [P, 2, 2, TOK])
        decay = sb("decay", [P, 2, TOK])
        inp = sb("inp", [P, 2, TOK])
        state = sb("state", [P, 2, TOK])
        read = sb("read", [P, 2, TOK])
        ps_y = ps("ps_y", [P, BM_CT, 2, 512])
        zeros = sb("zeros", [P, 512], BF16)
        bc_loaded = [sem("bc_loaded0"), sem("bc_loaded1")]
        cleared, decay_ready, inp_ready, pool_inp_ready, state_ready, read_ready, added = (
            sem("cleared"), sem("decay_ready"), sem("inp_ready"), sem("pool_inp_ready"), sem("state_ready"),
            sem("read_ready"), sem("added"))
        closed, y_ready, gated = sem("closed"), sem("y_ready"), sem("gated")
        first = SEQ - 1 if back else 0
        rest = slice(0, SEQ - 1) if back else slice(1, SEQ)
        by_batch = lambda ap: ap.rearrange("p (b t) -> p b t", b=BATCH)
        order = (lambda ap: ap[:, ::-1]) if back else (lambda ap: ap)
        POOL_CT = BM_CT - 1

        def over_states(eng, body):
            body(0, 0, 0)
            body(1, 1, 0)
            with eng.Fori(0, BM_DS // 2 - 1) as i:
                body(i * 2 + 2, 0, i + 1)
                body(i * 2 + 3, 1, i + 1)

        with nc.Block() as block:

            @block.sync
            def _(sp):
                def body(s, q, v):
                    wait_if_positive(sp, read_ready, (s - 1) * BM_CT)
                    src = dram["bm_bc_rows"][back, s:s + 1, :] if isinstance(s, int) else \
                        dram["bm_bc_rows"][back, bass.ds(s, 1), :]
                    sp.dma_start(bc[:, q, :, :].rearrange("p a t -> p (a t)"), src.partition_broadcast(P)).then_inc(bc_loaded[q], 16)

                over_states(sp, body)

            @block.gpsimd
            def _(pool):
                pool.memset(decay[:, :, :].rearrange("p a (b t) -> p a b t", b=BATCH)[:, :, :, first:first + 1], 0.0).then_inc(cleared, 1)
                pool.memset(zeros[:, :], 0.0).then_inc(cleared, 1)

                def body(s, q, v):
                    pool.wait_ge(bc_loaded[q], (v + 1) * 16)
                    for ct in range(BM_CT):
                        n = s * BM_CT + ct
                        if ct == 2:
                            pool.wait_ge(state_ready, n)
                            pool.tensor_tensor(inp[:, POOL_CT % 2, :], u[:, POOL_CT, :], bc[:, q, 0, :],
                                               ALU.mult).then_inc(pool_inp_ready, 1)
                        pool.wait_ge(state_ready, n + 1)
                        wait_if_positive(pool, added, n - 1)
                        pool.tensor_tensor(read[:, ct % 2, :], state[:, ct % 2, :], bc[:, q, 1, :],
                                           ALU.mult).then_inc(read_ready, 1)

                over_states(pool, body)

            @block.scalar
            def _(act):
                act.wait_ge(cleared, 2)

                def body(s, q, v):
                    for ct in range(BM_CT):
                        n = s * BM_CT + ct
                        wait_if_positive(act, state_ready, n - 1)
                        act.activation(by_batch(decay[:, ct % 2, :])[:, :, rest], by_batch(dt[:, ct, :])[:, :, rest], ACT.Exp,
                                       scale=A[:, bass.ds(s, 1), ct]).then_inc(decay_ready, 1)

                over_states(act, body)

            @block.vector
            def _(dve):
                def body(s, q, v):
                    dve.wait_ge(bc_loaded[q], (v + 1) * 16)
                    for ct in range(BM_CT):
                        n = s * BM_CT + ct
                        if ct != POOL_CT:
                            wait_if_positive(dve, state_ready, n - 1)
                            dve.tensor_tensor(inp[:, ct % 2, :], u[:, ct, :], bc[:, q, 0, :], ALU.mult).then_inc(inp_ready, 1)
                            dve.wait_ge(inp_ready, s * POOL_CT + ct + 1)
                        else:
                            dve.wait_ge(pool_inp_ready, s + 1)
                        dve.wait_ge(decay_ready, n + 1)
                        wait_if_positive(dve, read_ready, n - 1)
                        dve.tensor_tensor_scan(order(state[:, ct % 2, :]), order(decay[:, ct % 2, :]), order(inp[:, ct % 2, :]),
                                               0.0, ALU.mult, ALU.add).then_inc(state_ready, 1)

                over_states(dve, body)
                dve.wait_ge(closed, 1)
                for ct in range(BM_CT):
                    y = inp[:, ct % 2, :]
                    if ct == 0:
                        dve.wait_ge(state_ready, BM_DS * BM_CT)
                    if ct >= 2:
                        dve.wait_ge(gated, ct - 1)
                    dve.scalar_tensor_tensor(out=y, in0=xi[:, ct, :], scalar=skip[:, ct:ct + 1],
                                             in1=ps_y[:, ct, :, :].rearrange("p a t -> p (a t)"), op0=ALU.mult,
                                             op1=ALU.add).then_inc(y_ready, 1)
                    dve.wait_ge(y_ready, ct + 1)
                    dve.tensor_tensor(z[:, ct, :], z[:, ct, :], y, ALU.mult).then_inc(gated, 1)

            @block.tensor
            def _(pe):
                pe.wait_ge(cleared, 2)
                for ct in range(BM_CT):
                    for half in range(2):
                        pe.matmul(ps_y[:, ct, half, :], zeros[:, 0:P], zeros[:, :], start=True, stop=False)

                def body(s, q, v):
                    for ct in range(BM_CT):
                        n = s * BM_CT + ct
                        pe.wait_ge(read_ready, n + 1)
                        for half in range(2):
                            m = pe.matmul(ps_y[:, ct, half, :], chip.ident[:, :], read[:, ct % 2, half * 512:(half + 1) * 512],
                                          start=False, stop=False)
                        m.then_inc(added, 1)

                over_states(pe, body)
                for ct in range(BM_CT):
                    for half in range(2):
                        m = pe.matmul(ps_y[:, ct, half, :], zeros[:, 0:P], zeros[:, :], start=False, stop=True)
                m.then_inc(closed, 1)


def bi_out(chip, way, name, back, bufs, total):
    nc, dram = chip.nc, chip.dram
    z, h_feat = bufs[1], bufs[6]
    with ExitStack() as held:
        part = Part(chip, name, held)
        w_out = part.sb("w_out", [P, BM_CT, D])
        twice = part.sb("twice", [P, KD, D])
        ps_out = part.ps("ps_out", [P, BATCH, 2, D])
        loaded, twice_ready, made, summed = (part.sem("loaded"), part.sem("twice_ready"), part.sem("made"),
                                             part.sem("summed"))
        with nc.Block() as block:

            @block.sync
            def _(sp):
                sp.dma_start(w_out[:, :, :], dram[f"{way}_w_out"]).then_inc(loaded, 16)

            @block.gpsimd
            def _(pool):
                pool.memset(twice[:, :, :], 0.0).then_inc(twice_ready, 1)
                pool.wait_ge(twice_ready, 1)
                for k in range(KD):
                    pool.tensor_scalar(twice[:, k, k * P:(k + 1) * P], chip.ident[:, :], 2.0, None,
                                       ALU.mult).then_inc(twice_ready, 1)

            @block.tensor
            def _(pe):
                pe.wait_ge(loaded, 16)
                pe.wait_ge(twice_ready, 1 + KD)
                for t in range(TILES):
                    for k in range(BM_CT):
                        o = pe.matmul(ps_out[:, t // 2, t % 2, :], z[:, k, t * P:(t + 1) * P], w_out[:, k, :],
                                      start=(k == 0), stop=(k == BM_CT - 1 and bool(back)))
                    if not back:
                        for k in range(KD):
                            o = pe.matmul(ps_out[:, t // 2, t % 2, :], h_feat[:, k, t * P:(t + 1) * P], twice[:, k, :],
                                          start=False, stop=(k == KD - 1))
                    o.then_inc(made, 1)

            @block.vector
            def _(dve):
                for b in range(BATCH):
                    dve.wait_ge(made, 2 * (b + 1))
                    out = total[:, 2 * b:2 * b + 2, :]
                    if back:
                        dve.scalar_tensor_tensor(out=out, in0=ps_out[:, b, :, :], scalar=0.5, in1=out,
                                                 op0=ALU.mult, op1=ALU.add).then_inc(summed, 1)
                    else:
                        dve.tensor_scalar(out, ps_out[:, b, :, :], 0.5, None, ALU.mult).then_inc(summed, 1)


def bi_tail(chip, name, total):
    nc, dram = chip.nc, chip.dram
    with ExitStack() as held:
        part = Part(chip, name, held)
        sb, ps, sem = part.sb, part.ps, part.sem
        norm = PostNorm(part)
        w_out = sb("w_out", [P, KD, D])
        gain = sb("gain", [P, KD])
        shift = sb("shift", [P, KD])
        b_out = sb("b_out", [P, D])
        raw = sb("raw", [P, TILES, 6])
        mean_var = sb("mean_var", [P, TILES, 2])
        var_eps = sb("var_eps", [P, TILES])
        rstd = sb("rstd", [P, TILES])
        feat = sb("feat", [P, KD, TOK])
        ps_turn = ps("ps_turn", [P, 2, 512])
        ps_out = ps("ps_out", [P, BATCH, 2, D])
        loaded, tables, turn, stats_ready, eps_added, rstd_ready, normed, turned, feat_ready, made = (
            sem("loaded"), sem("tables"), sem("turn"), sem("stats_ready"), sem("eps_added"), sem("rstd_ready"),
            sem("normed"), sem("turned"), sem("feat_ready"), sem("made"))
        with nc.Block() as block:

            @block.sync
            def _(sp):
                sp.dma_start(w_out[:, :, :], dram["bm_w_last"]).then_inc(loaded, 16)
                sp.dma_start(gain[:, :], dram["bm_ln_g"]).then_inc(tables, 16)
                sp.dma_start(shift[:, :], dram["bm_ln_b"]).then_inc(tables, 16)
                sp.dma_start(b_out[:, :], dram["bm_b_out"].partition_broadcast(P)).then_inc(tables, 16)

            @block.gpsimd
            def _(pool):
                for b in range(BATCH):
                    two = slice(2 * b, 2 * b + 2)
                    pool.wait_ge(stats_ready, 2 * (b + 1))
                    pool.tensor_scalar(var_eps[:, two], mean_var[:, two, 1], LN_EPS, None, ALU.add).then_inc(eps_added, 1)
                    pool.wait_ge(eps_added, b + 1)
                    pool.tensor_tensor(rstd[:, two], var_eps[:, two], chip.minus_half[:, 0:2],
                                       ALU.pow).then_inc(rstd_ready, 1)
                norm.rstds(pool)

            @block.tensor
            def _(pe):
                for b in range(BATCH):
                    pe.wait_ge(normed, 2 * (b + 1))
                    if b >= 2:
                        pe.wait_ge(feat_ready, KD * (b - 1))
                    for k in range(KD):
                        for h in range(HALVES):
                            at = (k * HALVES + h) * P
                            m = pe.transpose(ps_turn[:, b % 2, at:at + P], total[:, 2 * b + h, k * P:(k + 1) * P],
                                             chip.ident[:, :])
                    m.then_inc(turned, 1)
                pe.wait_ge(loaded, 16)
                for t in range(TILES):
                    pe.wait_ge(feat_ready, KD * (t // 2 + 1))
                    for k in range(KD):
                        m = pe.matmul(ps_out[:, t // 2, t % 2, :], feat[:, k, t * P:(t + 1) * P], w_out[:, k, :],
                                      start=(k == 0), stop=(k == KD - 1))
                    m.then_inc(made, 1)
                norm.turn(pe)

            @block.scalar
            def _(act):
                act.wait_ge(tables, 48)
                for b in range(BATCH):
                    act.wait_ge(turned, b + 1)
                    for k in range(KD):
                        act.activation(feat[:, k, b * SEQ:(b + 1) * SEQ], ps_turn[:, b % 2, k * SEQ:(k + 1) * SEQ],
                                       ACT.Identity, scale=gain[:, k:k + 1], bias=shift[:, k:k + 1]).then_inc(feat_ready, 1)
                norm.write_feat(act)

            @block.vector
            def _(dve):
                then_wait = in_turn(dve, turn)
                for b in range(BATCH):
                    for t in (2 * b, 2 * b + 1):
                        then_wait(dve.bn_stats(raw[:, t, :], total[:, t, :]))
                        dve.bn_aggr(mean_var[:, t, :], raw[:, t, :]).then_inc(stats_ready, 1)
                for b in range(BATCH):
                    dve.wait_ge(rstd_ready, b + 1)
                    for t in (2 * b, 2 * b + 1):
                        dve.tensor_scalar(total[:, t, :], total[:, t, :], mean_var[:, t, 0:1], rstd[:, t:t + 1],
                                          ALU.subtract, ALU.mult).then_inc(normed, 1)
                dve.wait_ge(tables, 48)
                for b in range(BATCH):
                    x = chip.x_tok[:, 2 * b:2 * b + 2, :]
                    then_wait(dve.tensor_tensor(x, x, b_out[:, :].unsqueeze(1).to_broadcast([P, 2, D]), ALU.add))
                    dve.wait_ge(made, 2 * (b + 1))
                    then_wait(dve.tensor_tensor(x, x, ps_out[:, b, :, :], ALU.add))
                    norm.stats(dve, then_wait, b)
                    if b:
                        norm.scale(dve, b - 1)
                norm.scale(dve, BATCH - 1)


def bi_mamba(chip):
    with ExitStack() as outer:
        part = Part(chip, "bm", outer)
        h_feat = part.sb("h_feat", [P, KD, TOK])
        total = part.sb("total", [P, TILES, D])
        bufs = tuple(part.sb(n, [P, BM_CT, TOK]) for n in ("xi", "z", "dt", "u")) + (
            part.sb("A", [P, BM_DS, BM_CT]), part.sb("skip", [P, BM_CT]), h_feat)
        bi_head(chip, part, h_feat)
        for back, way in enumerate(("fm", "bm")):
            bi_setup(chip, way, f"{way}s", back, bufs)
            bi_scan(chip, f"{way}r", back, bufs)
            bi_out(chip, way, f"{way}o", back, bufs, total)
        bi_tail(chip, "bmt", total)


def bi_mamba_inputs(given):
    import numpy as np

    def halves(w):
        return w.reshape(w.shape[0] // P, P, -1).transpose(1, 0, 2)

    columns = lambda v: v.reshape(-1, P).T
    g = lambda n: given[f"L1_attn_{n}"]
    out = {"bm_w_in": halves(g("w_in").T), "bm_b_in": columns(g("b_in")), "bm_w_last": halves(g("w_out").T),
           "bm_ln_g": columns(g("ln_g")), "bm_ln_b": columns(g("ln_b")), "bm_b_out": g("b_out").reshape(1, D)}
    turn = list(range(BM_R)) + [BM_R + which * BM_DS + s for s in range(BM_DS) for which in range(2)]
    for way in ("fm", "bm"):
        h = lambda n: g(f"{way}_{n}")
        out[f"{way}_w_xz"] = halves(h("in_w").T)
        out[f"{way}_w_proj"] = halves(h("xproj_w")[turn].T)
        out[f"{way}_w_dt"] = h("dt_w").T
        out[f"{way}_vec"] = np.concatenate([h("conv_w"), h("conv_b")[:, None]], axis=1).reshape(BM_CT, P, -1).transpose(1, 0, 2)
        out[f"{way}_dt_b"] = columns(h("dt_b"))
        out[f"{way}_a_log"] = h("A_log").reshape(BM_CT, P, BM_DS).transpose(1, 2, 0)
        out[f"{way}_d"] = columns(h("D"))
        out[f"{way}_w_out"] = halves(h("out_w").T)
    return out


MORE.append(bi_mamba_inputs)
SCRATCH = {"bm_bc": (2, 2 * BM_DS, TOK)}



RA_HEADS, RA_K, RA_CQ, RA_R = 16, 128, 192, 64
RA_HQ = RA_CQ // 2
RA_WIDE = D + RA_CQ + CTX + D


def rope_attention(chip, name="ra"):
    nc, dram = chip.nc, chip.dram
    STEPS = 2 * RA_HEADS
    with ExitStack() as outer:
        kept = Part(chip, name, outer)
        kv_tok = kept.sb("kv_tok", [P, TILES, CTX])
        kv_feat = kept.sb("kv_feat", [CTX, TOK])
        cos_q = kept.sb("cos_q", [RA_HQ, 2, SEQ])
        sin_q = kept.sb("sin_q", [RA_HQ, 2, SEQ])
        q_tables = kept.sem("q_tables")

        with ExitStack() as held:
            part = Part(chip, f"{name}s", held)
            ctx_tok = part.sb("ctx_tok", [P, TILES, CTX])
            cos_k = part.sb("cos_k", [P, HALVES, CTX])
            sin_k = part.sb("sin_k", [P, HALVES, CTX])
            crossed = part.sb("crossed", [P, TILES, CTX])
            ps_kv = part.ps("ps_kv", [CTX, 2, 512])
            loaded, turn, kv_ready, turned, kept_feat = (part.sem("loaded"), part.sem("turn"), part.sem("kv_ready"),
                                                         part.sem("turned"), part.sem("kept_feat"))
            with nc.Block() as block:

                @block.sync
                def _(sp):
                    sp.dma_start(ctx_tok[:, :, :], dram["ctx_tok"]).then_inc(loaded, 16)
                    sp.dma_start(cos_k[:, :, :], dram["rope_cos_k"]).then_inc(loaded, 16)
                    sp.dma_start(sin_k[:, :, :], dram["rope_sin_k"]).then_inc(loaded, 16)
                    sp.dma_start(cos_q[:, :, :], dram["rope_cos_q"]).then_inc(q_tables, 16)
                    sp.dma_start(sin_q[:, :, :], dram["rope_sin_q"]).then_inc(q_tables, 16)

                @block.vector
                def _(dve):
                    then_wait = in_turn(dve, turn)
                    dve.wait_ge(loaded, 48)
                    by_seq = lambda ap: ap.rearrange("p (b h) c -> p b h c", h=HALVES)
                    for to, of in ((slice(0, 32), slice(32, 64)), (slice(32, 64), slice(0, 32))):
                        for h in range(HALVES):
                            then_wait(dve.tensor_tensor(by_seq(crossed[:, :, :])[:, :, h, to], by_seq(ctx_tok[:, :, :])[:, :, h, of],
                                                        sin_k[:, h, to].unsqueeze(1).to_broadcast([P, BATCH, 32]), ALU.mult))
                    for h in range(HALVES):
                        then_wait(dve.tensor_tensor(by_seq(kv_tok[:, :, :])[:, :, h, :], by_seq(ctx_tok[:, :, :])[:, :, h, :],
                                                    cos_k[:, h, :].unsqueeze(1).to_broadcast([P, BATCH, CTX]), ALU.mult))
                    dve.tensor_tensor(kv_tok[:, :, :], kv_tok[:, :, :], crossed[:, :, :], ALU.add).then_inc(kv_ready, 1)

                @block.tensor
                def _(pe):
                    pe.wait_ge(kv_ready, 1)
                    for t in range(TILES):
                        m = pe.transpose(ps_kv[:, t // 4, (t % 4) * P:(t % 4 + 1) * P], kv_tok[:, t, :], chip.ident[:, :])
                    m.then_inc(turned, 1)

                @block.scalar
                def _(act):
                    act.wait_ge(turned, 1)
                    act.activation(kv_feat[:, :], ps_kv[:, :, :].rearrange("p a t -> p (a t)"), ACT.Copy).then_inc(kept_feat, 1)
                    act.wait_ge(kept_feat, 1)

        with ExitStack() as held:
            part = Part(chip, f"{name}h", held)
            sb, ps, sem = part.sb, part.ps, part.sem
            w = sb("w", [P, 2, RA_WIDE])
            w_r = sb("w_r", [RA_R, 2, RA_CQ + CTX])
            M = sb("M", [P, KD, RA_CQ])
            Z = sb("Z", [RA_HQ, 2, CTX])
            N = sb("N", [P, 2, D])
            straight = sb("straight", [RA_HQ, 2, HALF_TOK])
            crossed = sb("crossed", [RA_HQ, 2, HALF_TOK])
            zq = sb("zq", [CTX, HALF_TOK])
            attn = sb("attn", [P, 2, 2, SEQ])
            attn_t = sb("attn_t", [P, 2, SEQ])
            minus_max = sb("minus_max", [P, 2, 2])
            total = sb("total", [P, 2, 2])
            share = sb("share", [P, 2, 2])
            mixed = sb("mixed", [P, HALF_TOK])
            zeros = sb("zeros", [P, 512], BF16)
            ps_lo = ps("ps_lo", [P, 512])
            ps_hi = ps("ps_hi", [P, 512])
            ps_z = ps("ps_z", [P, 512])
            ps_s = ps("ps_s", [P, 512])
            ps_t = ps("ps_t", [P, 512])
            ps_c = ps("ps_c", [P, 512])
            ps_out = ps("ps_out", [P, 2, 2, D])
            w_loaded = [sem("w_loaded0"), sem("w_loaded1")]
            q_lo_made = sem("q_lo_made")
            m_made, m_kept, zn_made, zn_kept, q_made, rope_read, hi_parts, hi_roped, lo_roped = (
                sem("m_made"), sem("m_kept"), sem("zn_made"), sem("zn_kept"), sem("q_made"), sem("rope_read"),
                sem("hi_parts"), sem("hi_roped"), sem("lo_roped"))
            zq_made, zq_kept, scored, max_ready, exp_ready, share_ready, normed = (
                sem("zq_made"), sem("zq_kept"), sem("scored"), sem("max_ready"), sem("exp_ready"), sem("share_ready"),
                sem("normed"))
            t_made, t_kept, ctx_made, c_kept, out_made, zeroed, closed, out_read = (
                sem("t_made"), sem("t_kept"), sem("ctx_made"), sem("c_kept"), sem("out_made"), sem("zeroed"),
                sem("closed"), sem("out_read"))

            def steps(eng, step):
                for half in range(2):
                    base = half * RA_HEADS
                    for r in range(4):
                        step(base + r, r, (base + r) // 2, half)
                    with eng.Fori(0, RA_HEADS // 4 - 1) as i:
                        for r in range(4):
                            step(i * 4 + (base + 4 + r), r, i * 2 + (base + 4 + r) // 2, half)
                step(STEPS, 0, STEPS // 2, None)

            with nc.Block() as block:

                @block.sync
                def _(sp):
                    def step(g, r, pair, half):
                        if half is None:
                            return
                        q = r % 2
                        wait_if_positive(sp, zn_made, g - 1)
                        head = g - half * RA_HEADS
                        sp.dma_start(w[:, q, :], dram["ra_w"][bass.ds(head, 1), :, :].rearrange("a p n -> p (a n)")).then_inc(w_loaded[q], 16)
                        sp.dma_start(w_r[:, q, :], dram["ra_w_r"][bass.ds(head, 1), :, :].rearrange("a p n -> p (a n)")).then_inc(w_loaded[q], 16)

                    steps(sp, step)

                @block.gpsimd
                def _(pool):
                    pool.memset(zeros[:, :], 0.0).then_inc(zeroed, 1)

                    def step(g, r, pair, half):
                        if half is None:
                            return
                        pool.wait_ge(hi_parts, g + 1)
                        pool.tensor_tensor(straight[:, 1, :], straight[:, 1, :], crossed[:, 1, :], ALU.add).then_inc(hi_roped, 1)

                    steps(pool, step)

                @block.tensor
                def _(pe):
                    pe.wait_ge(zeroed, 1)

                    def zero_products(start, stop):
                        for t in range(2):
                            m = pe.matmul(ps_out[:, t, :, :].rearrange("p a d -> p (a d)"), zeros[:, 0:P], zeros[:, :],
                                          start=start, stop=stop)
                        return m

                    def scores(p, b, half_p):
                        pe.wait_ge(zq_kept, p + 1)
                        wait_if_positive(pe, exp_ready, p * 4 + 2 * b)
                        tokens = slice(half_p * HALF_TOK + b * SEQ, half_p * HALF_TOK + (b + 1) * SEQ)
                        for t in range(2):
                            m = pe.matmul(ps_s[:, t * SEQ:(t + 1) * SEQ], zq[:, b * SEQ + t * P:b * SEQ + (t + 1) * P],
                                          kv_feat[:, tokens], start=True, stop=True)
                        m.then_inc(scored, 1)

                    def turn_attn(p, b):
                        pe.wait_ge(normed, p * 2 + b + 1)
                        wait_if_positive(pe, t_kept, p * 2 + b)
                        for l in range(2):
                            for t in range(2):
                                m = pe.transpose(ps_t[:, l * SEQ + t * P:l * SEQ + (t + 1) * P], attn[:, b, t, l * P:(l + 1) * P],
                                                 chip.ident[:, :])
                        m.then_inc(t_made, 1)

                    def context(p, b, rows, half_p):
                        pe.wait_ge(t_kept, p * 2 + b + 1)
                        wait_if_positive(pe, c_kept, p)
                        for l in range(2):
                            m = pe.matmul(ps_c[rows, b * SEQ:(b + 1) * SEQ], kv_tok[:, 4 * half_p + 2 * b + l, :],
                                          attn_t[:, l, :], start=(l == 0), stop=(l == 1))
                        m.then_inc(ctx_made, 1)

                    def output(slot, heads_kept):
                        pe.wait_ge(c_kept, heads_kept)
                        for t in range(4):
                            m = pe.matmul(ps_out[:, t // 2, t % 2, :], mixed[:, t * P:(t + 1) * P], N[:, slot, :],
                                          start=False, stop=False)
                        m.then_inc(out_made, 1)

                    def step(g, r, pair, half):
                        q = r % 2
                        has_back = not (isinstance(g, int) and g == 0)
                        p = g - 1
                        new_half = isinstance(g, int) and g in (RA_HEADS, STEPS)
                        half_p = (g // RA_HEADS - 1) if new_half else half
                        back_rows = slice((1 - q) * CTX, (2 - q) * CTX)

                        def q_part(n, bank):
                            tokens = slice(half * HALF_TOK, (half + 1) * HALF_TOK)
                            for k in range(KD):
                                m = pe.matmul(bank[0:RA_HQ, :], M[:, k, n * RA_HQ:(n + 1) * RA_HQ], chip.x_feat[:, k, tokens],
                                              start=(k == 0), stop=(k == KD - 1))
                            return m

                        if half is not None:
                            pe.wait_ge(w_loaded[q], (pair + 1) * 32)
                            wait_if_positive(pe, rope_read, g)
                            for k in range(KD):
                                m = pe.matmul(ps_lo[:, k * RA_CQ:(k + 1) * RA_CQ], w[:, q, k * P:(k + 1) * P],
                                              w[:, q, D:D + RA_CQ], start=True, stop=True)
                            m.then_inc(m_made, 1)
                        if has_back:
                            scores(p, 0, half_p)
                        if half is not None:
                            wait_if_positive(pe, zq_kept, g)
                            for k in range(2):
                                pe.matmul(ps_z[0:RA_HQ, k * CTX:(k + 1) * CTX], w_r[:, q, k * RA_HQ:(k + 1) * RA_HQ],
                                          w_r[:, q, RA_CQ:], start=True, stop=True)
                            m = pe.matmul(ps_z[q * CTX:(q + 1) * CTX, SEQ:2 * SEQ], w[:, q, D + RA_CQ:D + RA_CQ + CTX],
                                          w[:, q, D + RA_CQ + CTX:], start=True, stop=True)
                            m.then_inc(zn_made, 1)
                            pe.wait_ge(m_kept, g + 1)
                            q_part(0, ps_lo).then_inc(q_lo_made, 1)
                        if has_back:
                            scores(p, 1, half_p)
                            turn_attn(p, 0)
                        if half is not None:
                            q_part(1, ps_hi).then_inc(q_made, 1)
                        if has_back:
                            context(p, 0, back_rows, half_p)
                            turn_attn(p, 1)
                            if q == 1 and not (isinstance(g, int) and g % RA_HEADS == 1):
                                output(1 if r == 1 else 0, g - 1)
                            context(p, 1, back_rows, half_p)
                        if half is not None:
                            pe.wait_ge(zn_kept, g + 1)
                            pe.wait_ge(hi_roped, g + 1)
                            pe.wait_ge(lo_roped, g + 1)
                            for k in range(2):
                                m = pe.matmul(ps_z[0:CTX, :], Z[:, k, :], straight[:, k, :], start=(k == 0), stop=(k == 1))
                            m.then_inc(zq_made, 1)
                        if new_half:
                            output(1, g)
                        if new_half:
                            zero_products(False, True).then_inc(closed, 1)
                            if g < STEPS:
                                pe.wait_ge(out_read, 2)
                                zero_products(True, False)

                    zero_products(True, False)
                    steps(pe, step)

                @block.scalar
                def _(act):
                    def exps(p, b):
                        act.wait_ge(max_ready, p * 2 + b + 1)
                        wait_if_positive(act, t_made, p * 2 + b - 1)
                        for t in range(2):
                            act.activation(attn[:, b, t, :], ps_s[:, t * SEQ:(t + 1) * SEQ], ACT.Exp,
                                           bias=minus_max[:, b, t:t + 1], accum_out=total[:, b, t:t + 1]).then_inc(exp_ready, 1)

                    def keep_turned(p, b):
                        act.wait_ge(t_made, p * 2 + b + 1)
                        wait_if_positive(act, ctx_made, p * 2 + b)
                        act.activation(attn_t[:, :, :], ps_t[:, :].rearrange("p (l s) -> p l s", l=2), ACT.Copy).then_inc(t_kept, 1)

                    def step(g, r, pair, half):
                        q = r % 2
                        has_back = not (isinstance(g, int) and g == 0)
                        p = g - 1
                        if half is not None:
                            act.wait_ge(m_made, g + 1)
                            wait_if_positive(act, q_made, g)
                            act.activation(M[:, :, :], ps_lo[:, 0:KD * RA_CQ].rearrange("p (k n) -> p k n", k=KD),
                                           ACT.Copy).then_inc(m_kept, 1)
                        if has_back:
                            exps(p, 0)
                        if half is not None:
                            act.wait_ge(zn_made, g + 1)
                            wait_if_positive(act, zq_made, g)
                            act.activation(Z[:, :, :], ps_z[0:RA_HQ, 0:2 * CTX].rearrange("p (k n) -> p k n", k=2), ACT.Copy)
                            wait_if_positive(act, out_made, pair - 1)
                            act.activation(N[q * CTX:(q + 1) * CTX, r // 2, :], ps_z[q * CTX:(q + 1) * CTX, SEQ:2 * SEQ],
                                           ACT.Copy).then_inc(zn_kept, 1)
                        if has_back:
                            keep_turned(p, 0)
                            exps(p, 1)
                            keep_turned(p, 1)
                            rows = slice((1 - q) * CTX, (2 - q) * CTX)
                            act.wait_ge(ctx_made, p * 2 + 2)
                            wait_if_positive(act, out_made, pair - 1 if q == 0 else pair)
                            act.activation(mixed[rows, :], ps_c[rows, :], ACT.Copy).then_inc(c_kept, 1)
                        if half is not None:
                            act.wait_ge(zq_made, g + 1)
                            wait_if_positive(act, scored, g * 2)
                            act.activation(zq[:, :], ps_z[0:CTX, :], ACT.Copy).then_inc(zq_kept, 1)

                    steps(act, step)

                @block.vector
                def _(dve):
                    dve.wait_ge(q_tables, 32)

                    def maxima(p, b):
                        dve.wait_ge(scored, p * 2 + b + 1)
                        wait_if_positive(dve, exp_ready, p * 4 + 2 * b - 2)
                        dve.tensor_reduce(minus_max[:, b, :], ps_s[:, :].rearrange("p (t l) -> p t l", t=2), AX.X, ALU.max,
                                          negate=True).then_inc(max_ready, 1)

                    def normalise(p, b):
                        dve.wait_ge(exp_ready, p * 4 + 2 * b + 2)
                        dve.reciprocal(share[:, b, :], total[:, b, :]).then_inc(share_ready, 1)
                        dve.wait_ge(share_ready, p * 2 + b + 1)
                        for t in range(2):
                            m = dve.tensor_scalar(attn[:, b, t, :], attn[:, b, t, :], share[:, b, t:t + 1], None, ALU.mult)
                        m.then_inc(normed, 1)

                    def step(g, r, pair, half):
                        has_back = not (isinstance(g, int) and g == 0)
                        p = g - 1
                        if has_back:
                            maxima(p, 0)
                            normalise(p, 0)
                            maxima(p, 1)
                        if half is not None:
                            by_batch = lambda ap: ap.rearrange("p (b t) -> p b t", b=2)
                            spread = lambda table: table.unsqueeze(1).to_broadcast([RA_HQ, 2, SEQ])
                            lo, hi = by_batch(ps_lo[0:RA_HQ, :]), by_batch(ps_hi[0:RA_HQ, :])
                            dve.wait_ge(q_lo_made, g + 1)
                            wait_if_positive(dve, zq_made, g)
                            wait_if_positive(dve, hi_roped, g)
                            wait_if_positive(dve, lo_roped, g)
                            dve.tensor_tensor(by_batch(crossed[:, 1, :]), lo, spread(sin_q[:, 1, :]), ALU.mult)
                            dve.tensor_tensor(by_batch(straight[:, 0, :]), lo, spread(cos_q[:, 0, :]), ALU.mult)
                        if has_back:
                            normalise(p, 1)
                        if half is not None:
                            dve.wait_ge(q_made, g + 1)
                            dve.tensor_tensor(by_batch(straight[:, 1, :]), hi, spread(cos_q[:, 1, :]), ALU.mult).then_inc(hi_parts, 1)
                            dve.tensor_tensor(by_batch(crossed[:, 0, :]), hi, spread(sin_q[:, 0, :]), ALU.mult).then_inc(rope_read, 1)
                            dve.wait_ge(rope_read, g + 1)
                            dve.tensor_tensor(straight[:, 0, :], straight[:, 0, :], crossed[:, 0, :], ALU.add).then_inc(lo_roped, 1)
                        if isinstance(g, int) and g in (RA_HEADS, STEPS):
                            n = g // RA_HEADS
                            dve.wait_ge(closed, n)
                            for b in range(2):
                                x = chip.x_tok[:, 4 * (n - 1) + 2 * b:4 * (n - 1) + 2 * b + 2, :]
                                dve.tensor_tensor(x, ps_out[:, b, :, :], x, ALU.add).then_inc(out_read, 1)

                    steps(dve, step)
    post_norm(chip, "ran")


def rope_inputs(given):
    import numpy as np

    def tables(width):
        inv = (np.float32(1.0) / np.float32(10000.0) ** (np.arange(0, width, 2, dtype=np.float32) / np.float32(width))).astype(np.float32)
        f = np.arange(SEQ, dtype=np.float32)[:, None] * inv[None, :]
        sin, cos = np.repeat(np.sin(f), 2, axis=-1), np.repeat(np.cos(f), 2, axis=-1)
        signed = np.concatenate([-sin[:, :width // 2], sin[:, width // 2:]], axis=-1)
        return signed.astype(np.float32), cos.astype(np.float32)

    g = lambda n: given[f"L1_xattn_{n}"]
    sin_q, cos_q = tables(RA_CQ)
    sin_k, cos_k = tables(CTX)
    by_half = lambda t: t.T.reshape(2, RA_HQ, SEQ).transpose(1, 0, 2)
    by_tile = lambda t: t.reshape(HALVES, P, CTX).transpose(1, 0, 2)
    return {
        "ctx_tok": given["ctx_512"].reshape(TILES, P, CTX).transpose(1, 0, 2),
        "rope_cos_q": by_half(cos_q), "rope_sin_q": by_half(sin_q),
        "rope_cos_k": by_tile(cos_k), "rope_sin_k": by_tile(sin_k),
        "ra_w": np.concatenate([g("Wq").reshape(RA_HEADS, RA_K, D), g("w_kc_q"), g("w_kc_kv"),
                                g("Wo").T.reshape(RA_HEADS, RA_K, D)], axis=2),
        "ra_w_r": np.concatenate([g("W_qr").transpose(0, 2, 1), g("W_kr").transpose(0, 2, 1)], axis=2),
    }


MORE.append(rope_inputs)



def load_and_constants(chip):
    nc, dram = chip.nc, chip.dram
    chip.x_tok = chip.keep("x_tok", [P, TILES, D])
    chip.x_feat = chip.keep("x_feat", [P, KD, TOK])
    chip.ident = chip.keep("ident", [P, P])
    chip.ones = chip.keep("ones", [P, P])
    chip.minus_half = chip.keep("minus_half", [P, 2])
    chip.constants_ready = chip.sem("constants_ready")
    chip.x_loaded = chip.sem("x_loaded")
    chip.CONSTANTS = 4
    with nc.Block() as block:

        @block.sync
        def _(sp):
            sp.dma_start(chip.x_feat[:, :, :], dram["x_feat"]).then_inc(chip.x_loaded, 16)
            sp.dma_start(chip.x_tok[:, :, :], dram["x_tok"]).then_inc(chip.x_loaded, 16)
            sp.wait_ge(chip.x_loaded, 32)

        @block.gpsimd
        def _(pool):
            pool.memset(chip.ident[:, :], 0.0).then_inc(chip.constants_ready, 1)
            pool.memset(chip.ones[:, :], 1.0).then_inc(chip.constants_ready, 1)
            pool.memset(chip.minus_half[:, :], -0.5).then_inc(chip.constants_ready, 1)
            pool.wait_ge(chip.constants_ready, 3)
            pool.affine_select(out=chip.ident[:, :], in_=chip.ident[:, :], compare_op=ALU.not_equal, fill=1.0,
                               base=0, pattern=[[-1, P]], channel_multiplier=1).then_inc(chip.constants_ready, 1)
            pool.wait_ge(chip.constants_ready, 4)


PARTS = [mamba2, ctx_attention, factor_ffn, bi_mamba, rope_attention, expert_ffn]


def decoder(nc, dram, parts):
    chip = Chip(nc, dram)
    with chip.kept:
        load_and_constants(chip)
        for part in parts:
            part(chip)
            chip.end_part()


def laid_out(inputs):
    import numpy as np

    def halves(w):
        k = w.shape[0] // P
        return w.reshape(k, P, -1).transpose(1, 0, 2)

    given = {n: np.asarray(a) for n, a in inputs.items()}
    x = given["x"].reshape(TOK, D)
    out = {
        "x_tok": x.reshape(TILES, P, D).transpose(1, 0, 2),
        "x_feat": halves(x.T),
        "ctx_feat": given["ctx_512"].reshape(TOK, CTX).T,
        "L0_xattn_W_k_t": given["L0_xattn_W_k"].T,
        "L0_xattn_b_k": given["L0_xattn_b_k"].reshape(CTX, 1),
        "L0_xattn_ln_gamma": given["L0_xattn_ln_gamma"].reshape(1, SEQ),
        "L0_xattn_ln_beta": given["L0_xattn_ln_beta"].reshape(1, SEQ),
        "L0_ffn_factors": given["L0_ffn_factors"].reshape(8, KD, P, D).transpose(2, 0, 1, 3),
        "L0_ffn_bias": given["L0_ffn_bias"].reshape(1, D),
        "L1_ffn_imp_center": given["L1_ffn_imp_center"].reshape(1, 8),
        "L1_ffn_imp_slope": given["L1_ffn_imp_slope"].reshape(1, 8),
        "expert_in": halves(np.concatenate([
            given["L1_ffn_select_weight"].transpose(1, 0, 2).reshape(D, 64),
            given["L1_ffn_lora_update"].transpose(1, 0, 2).reshape(D, 64),
            given["L1_ffn_select_mean_diff"].T], axis=1)),
        "expert_away": np.stack([given["L1_ffn_select_mean_diff"].T.reshape(KD, P, 8),
                                 given["L1_ffn_debias_w"].T.reshape(KD, P, 8)], axis=2).transpose(1, 0, 2, 3),
        "expert_down": np.concatenate([given["L1_ffn_lora_degen"].transpose(0, 2, 1).reshape(64, D),
                                       given["L1_ffn_bias_w"]], axis=0),
    }
    for more in MORE:
        out.update(more(given))
    return {n: np.ascontiguousarray(a) for n, a in out.items()}


def kernel(**inputs):
    import numpy as np
    import concourse.bacc as bacc
    from concourse.bass_utils import run_bass_kernel_spmd

    nc = bacc.Bacc("TRN2", target_bir_lowering=False, num_devices=1)
    arrays = laid_out(inputs)
    dram = {n: nc.dram_tensor(f"in_{n}", a.shape, mybir.dt.from_np(a.dtype), kind="ExternalInput").ap()
            for n, a in arrays.items()}
    for name, shape in SCRATCH.items():
        dram[name] = nc.dram_tensor(f"scratch_{name}", shape, F32, kind="Internal").ap()
    dram["bm_bc_rows"] = dram["bm_bc"].rearrange("w (s c) t -> w s (c t)", c=2) if "bm_bc" in dram else None
    out = nc.dram_tensor("out", (TILES, P, D), F32, kind="ExternalOutput").ap()
    dram["out"] = out.rearrange("t p d -> p t d")
    decoder(nc, dram, PARTS)
    result = run_bass_kernel_spmd(nc, [{f"in_{n}": a for n, a in arrays.items()}], core_ids=[0])
    return result.results[0]["out"].reshape(BATCH, SEQ, D)
```

```python
from contextlib import ExitStack

import concourse.bass as bass
from concourse import mybir

F32 = mybir.dt.float32
F32R = mybir.dt.float32r
BF16 = mybir.dt.bfloat16
ALU = mybir.AluOpType
ACT = mybir.ActivationFunctionType
AX = mybir.AxisListType

P = 128
BATCH, SEQ, D = 4, 256, 256
TOK = BATCH * SEQ
TILES = TOK // P
KD = D // P
HALVES = SEQ // P
CTX = 64
LN_EPS = 1e-5


class Chip:

    def __init__(self, nc, dram):
        self.nc, self.dram = nc, dram
        self.kept = ExitStack()
        self.part_sems = []

    def sem(self, name):
        return self.nc.alloc_semaphore(name)

    def part_sem(self, name):
        self.part_sems.append(self.nc.alloc_semaphore(name))
        return self.part_sems[-1]

    def end_part(self):
        self.nc.clear_and_free_semaphores(self.part_sems)
        self.nc.all_engine_barrier()
        self.part_sems = []

    def keep(self, name, shape, dtype=F32):
        return self.kept.enter_context(self.nc.sbuf_tensor(name, shape, dtype))


class Part:

    def __init__(self, chip, name, held):
        self.chip, self.name, self.held = chip, name, held

    def sb(self, name, shape, dtype=F32):
        return self.held.enter_context(self.chip.nc.sbuf_tensor(f"{self.name}_{name}", shape, dtype))

    def ps(self, name, shape, dtype=F32):
        return self.held.enter_context(self.chip.nc.psum_tensor(f"{self.name}_{name}", shape, dtype))

    def sem(self, name):
        return self.chip.part_sem(f"{self.name}_{name}")


def in_turn(eng, sem):
    count = [0]

    def then_wait(instruction):
        instruction.then_inc(sem, 1)
        count[0] += 1
        eng.wait_ge(sem, count[0])

    return then_wait


class PostNorm:

    def __init__(self, part, last=False):
        chip = part.chip
        self.chip, self.last = chip, last
        self.raw = part.sb("ln_raw", [P, TILES, 6])
        self.mean_var = part.sb("ln_mean_var", [P, TILES, 2])
        self.var_eps = part.sb("ln_var_eps", [P, TILES])
        self.rstd = part.sb("ln_rstd", [P, TILES])
        self.turned = part.ps("ln_turned", [P, 512])
        self.stats_ready = part.sem("ln_stats_ready")
        self.eps_added = part.sem("ln_eps_added")
        self.rstd_ready = part.sem("ln_rstd_ready")
        self.normed = part.sem("ln_normed")
        self.turned_ready = part.sem("ln_turned_ready")
        self.feat_ready = part.sem("ln_feat_ready")

    def stats(self, dve, then_wait, b):
        x = self.chip.x_tok
        for t in (2 * b, 2 * b + 1):
            then_wait(dve.bn_stats(self.raw[:, t, :], x[:, t, :]))
            dve.bn_aggr(self.mean_var[:, t, :], self.raw[:, t, :]).then_inc(self.stats_ready, 1)

    def rstds(self, pool):
        for b in range(BATCH):
            two = slice(2 * b, 2 * b + 2)
            pool.wait_ge(self.stats_ready, 2 * (b + 1))
            pool.tensor_scalar(self.var_eps[:, two], self.mean_var[:, two, 1], LN_EPS, None,
                               ALU.add).then_inc(self.eps_added, 1)
            pool.wait_ge(self.eps_added, b + 1)
            pool.tensor_tensor(self.rstd[:, two], self.var_eps[:, two], self.chip.minus_half[:, 0:2],
                               ALU.pow).then_inc(self.rstd_ready, 1)

    def scale(self, dve, b):
        x = self.chip.x_tok
        dve.wait_ge(self.rstd_ready, b + 1)
        for t in (2 * b, 2 * b + 1):
            dve.tensor_scalar(x[:, t, :], x[:, t, :], self.mean_var[:, t, 0:1], self.rstd[:, t:t + 1],
                              ALU.subtract, ALU.mult).then_inc(self.normed, 1)

    def turn(self, pe):
        if self.last:
            return
        for b in range(BATCH):
            pe.wait_ge(self.normed, 2 * (b + 1))
            if b:
                pe.wait_ge(self.feat_ready, b)
            for k in range(KD):
                for h in range(HALVES):
                    at = (k * HALVES + h) * P
                    turned = pe.transpose(self.turned[:, at:at + P],
                                          self.chip.x_tok[:, 2 * b + h, k * P:(k + 1) * P],
                                          self.chip.ident[:, :])
            turned.then_inc(self.turned_ready, 1)

    def write_feat(self, act):
        if self.last:
            return
        for b in range(BATCH):
            act.wait_ge(self.turned_ready, b + 1)
            act.activation(self.chip.x_feat[:, :, b * SEQ:(b + 1) * SEQ],
                           self.turned[:, :].rearrange("p (k t) -> p k t", k=KD),
                           ACT.Copy).then_inc(self.feat_ready, 1)


def ctx_attention(chip, name="xa"):
    nc, dram = chip.nc, chip.dram
    with ExitStack() as held:
        part = Part(chip, name, held)
        sb, ps, sem = part.sb, part.ps, part.sem
        norm = PostNorm(part)
        ctx_feat = sb("ctx_feat", [CTX, TOK])
        wk = sb("wk", [CTX, CTX])
        bk = sb("bk", [CTX, 1])
        gamma = sb("gamma", [P, SEQ])
        beta = sb("beta", [P, SEQ])
        kv_feat = sb("kv_feat", [CTX, TOK])
        kv_tok = sb("kv_tok", [P, TILES, CTX])
        mixed = sb("mixed", [CTX, BATCH, SEQ])
        raw = sb("raw", [P, TILES, 6])
        mean_var = sb("mean_var", [P, TILES, 2])
        var_eps = sb("var_eps", [P, TILES])
        rstd = sb("rstd", [P, TILES])
        sim = sb("sim", [P, BATCH, 2, SEQ])
        minus_max = sb("minus_max", [P, TILES])
        total = sb("total", [P, TILES])
        share = sb("share", [P, TILES])
        ps_kv = ps("ps_kv", [CTX, 2, 512])
        ps_kvt = ps("ps_kvt", [P, TILES, CTX])
        ps_mix = ps("ps_mix", [CTX, 512])
        ps_sim = ps("ps_sim", [P, 2, 2, SEQ])

        loaded, tables = sem("loaded"), sem("tables")
        kv_made, kv_kept, kv_turned, kv_tok_kept = sem("kv_made"), sem("kv_kept"), sem("kv_turned"), sem("kv_tok_kept")
        mix_made, mix_kept, sim_made = sem("mix_made"), sem("mix_kept"), sem("sim_made")
        stats_ready, eps_added, rstd_ready = sem("stats_ready"), sem("eps_added"), sem("rstd_ready")
        sim_read, max_ready, exp_ready, turn = sem("sim_read"), sem("max_ready"), sem("exp_ready"), sem("turn")

        with nc.Block() as block:

            @block.sync
            def _(sp):
                sp.dma_start(ctx_feat[:, :], dram["ctx_feat"]).then_inc(loaded, 16)
                sp.dma_start(wk[:, :], dram["L0_xattn_W_k_t"]).then_inc(loaded, 16)
                sp.dma_start(bk[:, :], dram["L0_xattn_b_k"]).then_inc(loaded, 16)
                sp.dma_start(gamma[:, :], dram["L0_xattn_ln_gamma"].partition_broadcast(P)).then_inc(tables, 16)
                sp.dma_start(beta[:, :], dram["L0_xattn_ln_beta"].partition_broadcast(P)).then_inc(tables, 16)

            @block.tensor
            def _(pe):
                pe.wait_ge(loaded, 48)
                for c in range(2):
                    kv = pe.matmul(ps_kv[:, c, :], wk[:, :], ctx_feat[:, c * 512:(c + 1) * 512],
                                   start=True, stop=True)
                kv.then_inc(kv_made, 1)
                pe.wait_ge(kv_kept, 1)
                for t in range(TILES):
                    turned = pe.transpose(ps_kvt[:, t, :], kv_feat[:, t * P:(t + 1) * P], chip.ident[0:CTX, 0:CTX])
                turned.then_inc(kv_turned, 1)
                pe.wait_ge(kv_tok_kept, 1)
                for b in range(BATCH):
                    if b:
                        pe.wait_ge(mix_kept, b)
                    for k in range(KD):
                        mix = pe.matmul(ps_mix[:, 0:SEQ], kv_tok[:, 2 * b + k, :],
                                        chip.x_feat[:, k, b * SEQ:(b + 1) * SEQ], start=(k == 0), stop=(k == KD - 1))
                    mix.then_inc(mix_made, 1)
                    pe.wait_ge(mix_kept, b + 1)
                    if b >= 2:
                        pe.wait_ge(sim_read, 2 * (b - 1))
                    for h in range(HALVES):
                        s = pe.matmul(ps_sim[:, b % 2, h, :], mixed[:, b, h * P:(h + 1) * P],
                                      kv_feat[:, b * SEQ:(b + 1) * SEQ], start=True, stop=True)
                    s.then_inc(sim_made, 1)
                norm.turn(pe)

            @block.scalar
            def _(act):
                act.wait_ge(kv_made, 1)
                act.activation(kv_feat[:, :], ps_kv[:, :, :].rearrange("p a t -> p (a t)"), ACT.Identity,
                               bias=bk[:, 0:1]).then_inc(kv_kept, 1)
                act.wait_ge(kv_turned, 1)
                act.activation(kv_tok[:, :, :], ps_kvt[:, :, :], ACT.Copy).then_inc(kv_tok_kept, 1)
                for b in range(BATCH):
                    act.wait_ge(mix_made, b + 1)
                    act.activation(mixed[:, b, :], ps_mix[:, 0:SEQ], ACT.Copy, scale=D ** -0.5).then_inc(mix_kept, 1)
                for b in range(BATCH):
                    act.wait_ge(max_ready, b + 1)
                    for h in range(HALVES):
                        t = 2 * b + h
                        act.activation(sim[:, b, h, :], sim[:, b, h, :], ACT.Exp, bias=minus_max[:, t:t + 1],
                                       accum_out=total[:, t:t + 1]).then_inc(exp_ready, 1)
                norm.write_feat(act)

            @block.gpsimd
            def _(pool):
                for b in range(BATCH):
                    two = slice(2 * b, 2 * b + 2)
                    pool.wait_ge(stats_ready, 2 * (b + 1))
                    pool.tensor_scalar(var_eps[:, two], mean_var[:, two, 1], 1e-6, None, ALU.add).then_inc(eps_added, 1)
                    pool.wait_ge(eps_added, b + 1)
                    pool.tensor_tensor(rstd[:, two], var_eps[:, two], chip.minus_half[:, 0:2],
                                       ALU.pow).then_inc(rstd_ready, 1)
                norm.rstds(pool)

            @block.vector
            def _(dve):
                then_wait = in_turn(dve, turn)

                def sim_stats(b):
                    dve.wait_ge(sim_made, b + 1)
                    for h in range(HALVES):
                        t = 2 * b + h
                        then_wait(dve.bn_stats(raw[:, t, :], ps_sim[:, b % 2, h, :]))
                        dve.bn_aggr(mean_var[:, t, :], raw[:, t, :]).then_inc(stats_ready, 1)

                def sim_norm(b):
                    dve.wait_ge(rstd_ready, b + 1)
                    for h in range(HALVES):
                        t = 2 * b + h
                        dve.tensor_scalar(sim[:, b, h, :], ps_sim[:, b % 2, h, :], mean_var[:, t, 0:1],
                                          rstd[:, t:t + 1], ALU.subtract, ALU.mult).then_inc(sim_read, 1)
                    dve.wait_ge(sim_read, 2 * (b + 1))
                    both = sim[:, b, :, :]
                    then_wait(dve.tensor_tensor(both, both, gamma[:, :].unsqueeze(1).to_broadcast([P, 2, SEQ]), ALU.mult))
                    then_wait(dve.tensor_tensor(both, both, beta[:, :].unsqueeze(1).to_broadcast([P, 2, SEQ]), ALU.add))
                    dve.tensor_reduce(minus_max[:, 2 * b:2 * b + 2], both, AX.X, ALU.max,
                                      negate=True).then_inc(max_ready, 1)

                def add_share(b):
                    dve.wait_ge(exp_ready, 2 * (b + 1))
                    then_wait(dve.reciprocal(share[:, 2 * b:2 * b + 2], total[:, 2 * b:2 * b + 2]))
                    for h in range(HALVES):
                        t = 2 * b + h
                        then_wait(dve.scalar_tensor_tensor(out=chip.x_tok[:, t, :], in0=sim[:, b, h, :],
                                                           scalar=share[:, t:t + 1], in1=chip.x_tok[:, t, :],
                                                           op0=ALU.mult, op1=ALU.add))
                    norm.stats(dve, then_wait, b)

                dve.wait_ge(tables, 32)
                sim_stats(0)
                for b in range(BATCH):
                    if b + 1 < BATCH:
                        sim_stats(b + 1)
                    sim_norm(b)
                    if b:
                        add_share(b - 1)
                    if b >= 2:
                        norm.scale(dve, b - 2)
                add_share(BATCH - 1)
                norm.scale(dve, BATCH - 2)
                norm.scale(dve, BATCH - 1)


def factor_ffn(chip, name="ff"):
    nc, dram = chip.nc, chip.dram
    rank = 8
    with ExitStack() as held:
        part = Part(chip, name, held)
        sb, ps, sem = part.sb, part.ps, part.sem
        norm = PostNorm(part)
        factors = sb("factors", [P, rank, KD, D])
        bias = sb("bias", [P, D])
        ps_out = ps("ps_out", [P, BATCH, 2, D])
        loaded, bias_loaded, summed, made, turn = sem("loaded"), sem("bias_loaded"), sem("summed"), sem("made"), sem("turn")
        with nc.Block() as block:

            @block.sync
            def _(sp):
                sp.dma_start(factors[:, :, :, :], dram["L0_ffn_factors"]).then_inc(loaded, 16)
                sp.dma_start(bias[:, :], dram["L0_ffn_bias"].partition_broadcast(P)).then_inc(bias_loaded, 16)

            @block.tensor
            def _(pe):
                pe.wait_ge(summed, 3)
                for t in range(TILES):
                    for k in range(KD):
                        out = pe.matmul(ps_out[:, t // 2, t % 2, :], chip.x_feat[:, k, t * P:(t + 1) * P],
                                        factors[:, 0, k, :], start=(k == 0), stop=(k == KD - 1))
                    out.then_inc(made, 1)
                norm.turn(pe)

            @block.scalar
            def _(act):
                norm.write_feat(act)

            @block.gpsimd
            def _(pool):
                norm.rstds(pool)

            @block.vector
            def _(dve):
                then_wait = in_turn(dve, turn)
                dve.wait_ge(loaded, 16)
                for n, left in enumerate((4, 2, 1)):
                    dve.tensor_tensor(factors[:, 0:left, :, :].rearrange("p r k d -> p (r k d)"),
                                      factors[:, 0:left, :, :].rearrange("p r k d -> p (r k d)"),
                                      factors[:, left:2 * left, :, :].rearrange("p r k d -> p (r k d)"),
                                      ALU.add).then_inc(summed, 1)
                    dve.wait_ge(summed, n + 1)
                dve.wait_ge(bias_loaded, 16)
                for b in range(BATCH):
                    x = chip.x_tok[:, 2 * b:2 * b + 2, :]
                    then_wait(dve.tensor_tensor(x, x, bias[:, :].unsqueeze(1).to_broadcast([P, 2, D]), ALU.add))
                    dve.wait_ge(made, 2 * (b + 1))
                    then_wait(dve.scalar_tensor_tensor(out=x, in0=ps_out[:, b, :, :], scalar=rank ** -0.5, in1=x,
                                                       op0=ALU.mult, op1=ALU.add))
                    norm.stats(dve, then_wait, b)
                    if b:
                        norm.scale(dve, b - 1)
                norm.scale(dve, BATCH - 1)


def expert_ffn(chip, name="ex"):
    nc, dram = chip.nc, chip.dram
    E, S, H = 8, 8, 8
    ES = E * S
    WIDE = 2 * ES + E
    with ExitStack() as held:
        part = Part(chip, name, held)
        sb, ps, sem = part.sb, part.ps, part.sem
        norm = PostNorm(part, last=True)
        weights = sb("weights", [P, KD, WIDE])
        away = sb("away", [P, KD, 2, E])
        dots = sb("dots", [P, KD, WIDE])
        down = sb("down", [ES + E, D])
        center = sb("center", [P, E])
        slope = sb("slope", [P, E])
        const = sb("const", [P, WIDE])
        proj = sb("proj", [P, TILES, WIDE])
        square = sb("square", [P, TILES, ES])
        x_square = sb("x_square", [P, D])
        x_norm = sb("x_norm", [P, TILES])
        score = sb("score", [P, TILES, E])
        dist = sb("dist", [P, TILES, E])
        gate = sb("gate", [P, TILES, E])
        key = sb("key", [P, TILES, E])
        best = sb("best", [P, TILES])
        rest = sb("rest", [P, TILES])
        best_key = sb("best_key", [P, TILES])
        rank_key = sb("rank_key", [P, E])
        picked = sb("picked", [P, TILES, ES + E])
        picked_t = sb("picked_t", [ES + E, TILES, P])
        ps_const = ps("ps_const", [P, 512])
        ps_proj = ps("ps_proj", [P, 2, 512])
        ps_turn = ps("ps_turn", [ES + E, 512])
        ps_out = ps("ps_out", [P, 2, 512])
        loaded, tables, dotted, const_made, const_kept = sem("loaded"), sem("tables"), sem("dotted"), sem("const_made"), sem("const_kept")
        proj_made, proj_kept, squared, scored, exped = sem("proj_made"), sem("proj_kept"), sem("squared"), sem("scored"), sem("exped")
        ranked, pick_ready, turned, turned_kept, made, mixed, turn, stored, x_scaled = (
            sem("ranked"), sem("pick_ready"), sem("turned"), sem("turned_kept"), sem("made"), sem("mixed"), sem("turn"),
            sem("stored"), sem("x_scaled"))
        with nc.Block() as block:

            @block.sync
            def _(sp):
                sp.dma_start(weights[:, :, :], dram["expert_in"]).then_inc(loaded, 16)
                sp.dma_start(away[:, :, :, :], dram["expert_away"]).then_inc(loaded, 16)
                sp.dma_start(down[:, :], dram["expert_down"]).then_inc(tables, 16)
                sp.dma_start(center[:, :], dram["L1_ffn_imp_center"].partition_broadcast(P)).then_inc(tables, 16)
                sp.dma_start(slope[:, :], dram["L1_ffn_imp_slope"].partition_broadcast(P)).then_inc(tables, 16)
                for b in range(BATCH):
                    sp.wait_ge(norm.normed, 2 * (b + 1))
                    sp.dma_start(dram["out"][:, 2 * b:2 * b + 2, :], chip.x_tok[:, 2 * b:2 * b + 2, :]).then_inc(stored, 16)
                sp.wait_ge(stored, 16 * BATCH)

            @block.tensor
            def _(pe):
                pe.wait_ge(loaded, 32)
                for t in range(TILES):
                    if t >= 2:
                        pe.wait_ge(proj_kept, t - 1)
                    for k in range(KD):
                        p = pe.matmul(ps_proj[:, t % 2, 0:WIDE], chip.x_feat[:, k, t * P:(t + 1) * P],
                                      weights[:, k, :], start=(k == 0), stop=(k == KD - 1))
                    p.then_inc(proj_made, 1)
                    if t == 1:
                        pe.wait_ge(dotted, 2 * KD + 1)
                        for k in range(KD):
                            c = pe.matmul(ps_const[:, 0:WIDE], chip.ones[:, :], dots[:, k, :],
                                          start=(k == 0), stop=(k == KD - 1))
                        c.then_inc(const_made, 1)
                for g in range(2):
                    pe.wait_ge(pick_ready, 1)
                    if g:
                        pe.wait_ge(turned_kept, g)
                    for t in range(4):
                        r = pe.transpose(ps_turn[:, t * P:(t + 1) * P], picked[:, 4 * g + t, :], chip.ident[:, :])
                    r.then_inc(turned, 1)
                pe.wait_ge(tables, 48)
                for b in range(BATCH):
                    pe.wait_ge(turned_kept, b // 2 + 1)
                    if b >= 2:
                        pe.wait_ge(mixed, b - 1)
                    for h in range(HALVES):
                        o = pe.matmul(ps_out[:, b % 2, h * D:(h + 1) * D], picked_t[:, 2 * b + h, :], down[:, :],
                                      start=True, stop=True)
                    o.then_inc(made, 1)

            @block.scalar
            def _(act):
                for t in range(TILES):
                    if t:
                        act.wait_ge(squared, t)
                    act.activation(x_square[:, :], chip.x_tok[:, t, :], ACT.Square,
                                   accum_out=x_norm[:, t:t + 1]).then_inc(squared, 1)
                act.wait_ge(scored, 1)
                act.activation(gate[:, :, :], score[:, :, :], ACT.Exp).then_inc(exped, 1)
                for g in range(2):
                    act.wait_ge(turned, g + 1)
                    act.activation(picked_t[:, 4 * g:4 * g + 4, :], ps_turn[:, :].rearrange("p (t c) -> p t c", t=4),
                                   ACT.Copy).then_inc(turned_kept, 1)

            @block.gpsimd
            def _(pool):
                for e in range(E):
                    pool.memset(rank_key[:, e:e + 1], float(E - e)).then_inc(ranked, 1)
                norm.rstds(pool)

            @block.vector
            def _(dve):
                then_wait = in_turn(dve, turn)
                dve.wait_ge(loaded, 32)
                for k in range(KD):
                    dve.tensor_tensor(dots[:, k, 0:2 * ES].rearrange("p (w e s) -> p w e s", w=2, e=E),
                                      weights[:, k, 0:2 * ES].rearrange("p (w e s) -> p w e s", w=2, e=E),
                                      away[:, k, :, :].unsqueeze(3).to_broadcast([P, 2, E, S]),
                                      ALU.mult).then_inc(dotted, 1)
                    dve.tensor_tensor(dots[:, k, 2 * ES:WIDE], away[:, k, 0, :], away[:, k, 0, :],
                                      ALU.mult).then_inc(dotted, 1)
                dve.wait_ge(chip.constants_ready, chip.CONSTANTS)
                dve.memset(best[:, :], 0.0).then_inc(dotted, 1)
                dve.wait_ge(const_made, 1)
                then_wait(dve.tensor_copy(const[:, :], ps_const[:, 0:WIDE]))
                for t in range(TILES):
                    dve.wait_ge(proj_made, t + 1)
                    dve.tensor_tensor(proj[:, t, 0:2 * ES], ps_proj[:, t % 2, 0:2 * ES], const[:, 0:2 * ES],
                                      ALU.subtract)
                    dve.scalar_tensor_tensor(out=proj[:, t, 2 * ES:WIDE], in0=ps_proj[:, t % 2, 2 * ES:WIDE],
                                             scalar=-2.0, in1=const[:, 2 * ES:WIDE], op0=ALU.mult,
                                             op1=ALU.add).then_inc(proj_kept, 1)
                dve.wait_ge(proj_kept, TILES)
                then_wait(dve.tensor_tensor(square[:, :, :], proj[:, :, 0:ES], proj[:, :, 0:ES], ALU.mult))
                then_wait(dve.tensor_reduce(score[:, :, :], square[:, :, :].rearrange("p t (e s) -> p t e s", e=E),
                                            AX.X, ALU.add))
                dve.wait_ge(squared, TILES)
                then_wait(dve.tensor_tensor(dist[:, :, :], proj[:, :, 2 * ES:WIDE],
                                            x_norm[:, :].unsqueeze(2).to_broadcast([P, TILES, E]), ALU.add))
                then_wait(dve.reciprocal(dist[:, :, :], dist[:, :, :]))
                then_wait(dve.tensor_tensor(score[:, :, :], score[:, :, :], dist[:, :, :], ALU.mult))
                dve.wait_ge(tables, 48)
                then_wait(dve.tensor_tensor(score[:, :, :], center[:, :].unsqueeze(1).to_broadcast([P, TILES, E]),
                                            score[:, :, :], ALU.subtract))
                then_wait(dve.tensor_tensor(score[:, :, :], score[:, :, :],
                                            slope[:, :].unsqueeze(1).to_broadcast([P, TILES, E]), ALU.mult))
                dve.tensor_scalar(score[:, :, :], score[:, :, :], 80.0, None, ALU.min).then_inc(scored, 1)
                dve.wait_ge(exped, 1)
                then_wait(dve.tensor_scalar(gate[:, :, :], gate[:, :, :], 1.0, None, ALU.add))
                then_wait(dve.reciprocal(gate[:, :, :], gate[:, :, :]))
                then_wait(dve.tensor_reduce(best[:, :], gate[:, :, :], AX.X, ALU.max))
                then_wait(dve.tensor_tensor(key[:, :, :], gate[:, :, :],
                                            best[:, :].unsqueeze(2).to_broadcast([P, TILES, E]), ALU.is_ge))
                dve.wait_ge(ranked, E)
                then_wait(dve.tensor_tensor(key[:, :, :], key[:, :, :],
                                            rank_key[:, :].unsqueeze(1).to_broadcast([P, TILES, E]), ALU.mult))
                then_wait(dve.tensor_reduce(best_key[:, :], key[:, :, :], AX.X, ALU.max))
                then_wait(dve.tensor_tensor(picked[:, :, ES:ES + E], key[:, :, :],
                                            best_key[:, :].unsqueeze(2).to_broadcast([P, TILES, E]), ALU.is_equal))
                then_wait(dve.tensor_scalar(rest[:, :], best[:, :], -1.0, 2.0, ALU.mult, ALU.add))
                for g in range(2):
                    four = slice(4 * g, 4 * g + 4)
                    then_wait(dve.tensor_tensor(picked[:, four, 0:ES].rearrange("p t (e s) -> p t e s", e=E),
                                                proj[:, four, ES:2 * ES].rearrange("p t (e s) -> p t e s", e=E),
                                                picked[:, four, ES:ES + E].unsqueeze(3).to_broadcast([P, 4, E, H]),
                                                ALU.mult))
                dve.memset(rank_key[:, 0:1], float(E)).then_inc(pick_ready, 1)
                for t in range(TILES):
                    then_wait(dve.tensor_scalar(chip.x_tok[:, t, :], chip.x_tok[:, t, :], rest[:, t:t + 1], None,
                                                ALU.mult))
                for b in range(BATCH):
                    dve.wait_ge(made, b + 1)
                    for h in range(HALVES):
                        t = 2 * b + h
                        mix = dve.scalar_tensor_tensor(out=chip.x_tok[:, t, :], in0=ps_out[:, b % 2, h * D:(h + 1) * D],
                                                       scalar=best[:, t:t + 1], in1=chip.x_tok[:, t, :],
                                                       op0=ALU.mult, op1=ALU.add)
                    mix.then_inc(mixed, 1)
                    dve.wait_ge(mixed, b + 1)
                    norm.stats(dve, then_wait, b)
                    if b:
                        norm.scale(dve, b - 1)
                norm.scale(dve, BATCH - 1)



def wait_if_positive(eng, sem, count):
    if isinstance(count, int) and count <= 0:
        return
    eng.wait_ge(sem, count)


M2_HEADS, M2_P, M2_N, M2_K = 64, 64, 128, 4
M2_INNER = M2_HEADS * M2_P
M2_CT = M2_INNER // P
M2_PAD = M2_K - 1
M2_VEC = M2_K + 1
M2_BLOCKS = 3 * P
HALF_TOK = TOK // 2
M2_W = 2 * KD * P
M2_ROW = M2_W + D


def mamba2_setup(chip, outer):
    nc, dram = chip.nc, chip.dram
    kept = Part(chip, "m2", outer)
    chip.m2_sel = kept.sb("sel", [3 * 32, 32, P], BF16)
    chip.m2_mask = kept.sb("mask", [P, P], BF16)
    chip.m2_ident = kept.sb("ident", [P, P], BF16)
    chip.m2_cum_parts = kept.sb("cum_parts", [3 * 32, 2, TOK], BF16)
    chip.m2_dt_tok = kept.sb("dt_tok", [P, TILES, 2, 32])
    chip.m2_minus_cum_tok = kept.sb("minus_cum_tok", [P, TILES, 2, 32])
    chip.m2_cb = kept.sb("cb", [P, BATCH, M2_BLOCKS])
    chip.m2_vec = kept.sb("vec", [P, M2_CT + 2, M2_VEC])
    chip.m2_d = kept.sb("d", [P, M2_CT])
    chip.m2_nw = kept.sb("nw", [P, M2_CT])
    chip.m2_x_parts = [kept.sb(n, [P, KD, TOK], F32R) for n in ("x_high", "x_low")]
    with ExitStack() as held:
        part = Part(chip, "m2s", held)
        sb, ps, sem = part.sb, part.ps, part.sem
        w_dt = sb("w_dt", [P, KD, 2, 3 * 32])
        w_bc = sb("w_bc", [P, KD, 2, P])
        dt_bias = sb("dt_bias", [3 * 32, 2])
        a = sb("a", [3 * 32, 2])
        z = sb("z", [3 * 32, 2, TOK])
        soft = sb("soft", [3 * 32, 2, TOK])
        cum = sb("cum", [3 * 32, 2, TOK])
        mid = sb("mid", [3 * 32, 2, TOK], BF16)
        run_ones = sb("run_ones", [3 * 32, SEQ])
        mask_f = sb("mask_f", [P, P])
        pad = sb("pad", [P, 2, BATCH, M2_PAD + SEQ])
        conv = sb("conv", [P, 2, BATCH, SEQ])
        tanh = sb("tanh", [P, 2, TOK])
        ps_dt = ps("ps_dt", [P, 2, 2, 512])
        ps_bc = ps("ps_bc", [P, 2, 2, 512])

        loaded, vec_loaded, dt_made, bc_made = sem("loaded"), sem("vec_loaded"), sem("dt_made"), sem("bc_made")
        vec_ready, tables = sem("vec_ready"), sem("tables")
        x_high_ready = sem("x_high_ready")
        padded, evacuated, z_ready, abs_ready, e_ready, ln_ready, a_ready = (
            sem("padded"), sem("evacuated"), sem("z_ready"), sem("abs_ready"), sem("e_ready"), sem("ln_ready"), sem("a_ready"))
        turn, dt_ready, cum_ready, tok_made, conv_ready, tanh_ready, bc_ready, cb_made, cb_kept = (
            sem("turn"), sem("dt_ready"), sem("cum_ready"), sem("tok_made"), sem("conv_ready"), sem("tanh_ready"),
            sem("bc_ready"), sem("cb_made"), sem("cb_kept"))

        with nc.Block() as block:

            @block.sync
            def _(sp):
                sp.dma_start(w_dt[:, :, :, :], dram["m2_w_dt"]).then_inc(loaded, 16)
                sp.dma_start(w_bc[:, :, :, :], dram["m2_w_bc"]).then_inc(loaded, 16)
                sp.dma_start(dt_bias[:, :], dram["m2_dt_bias"]).then_inc(loaded, 16)
                sp.dma_start(a[:, :], dram["m2_a_log"]).then_inc(loaded, 16)
                sp.dma_start(chip.m2_vec[:, :, :], dram["m2_vec"]).then_inc(vec_loaded, 16)
                sp.dma_start(chip.m2_d[:, :], dram["m2_d"]).then_inc(vec_loaded, 16)
                sp.dma_start(chip.m2_nw[:, :], dram["m2_nw"]).then_inc(vec_loaded, 16)

            @block.gpsimd
            def _(pool):
                pool.memset(pad[:, :, :, 0:M2_PAD], 0.0).then_inc(padded, 1)
                pool.memset(run_ones[:, :], 1.0).then_inc(padded, 1)
                pool.memset(mask_f[:, :], 0.0).then_inc(tables, 1)
                pool.memset(chip.m2_sel[:, :, :], 0.0).then_inc(tables, 1)
                pool.wait_ge(tables, 2)
                pool.affine_select(out=mask_f[:, :], in_=mask_f[:, :], compare_op=ALU.is_ge, fill=-1e30, base=0,
                                   pattern=[[1, P]], channel_multiplier=-1).then_inc(tables, 1)
                for r in range(3):
                    pool.affine_select(out=chip.m2_sel[:, :, :], in_=chip.m2_sel[:, :, :], compare_op=ALU.not_equal,
                                       fill=1.0, base=-32 * r, pattern=[[-1, 32], [0, P]],
                                       channel_multiplier=1).then_inc(tables, 1)
                    pool.wait_ge(tables, 4 + r)
                pool.tensor_copy(chip.m2_mask[:, :], mask_f[:, :]).then_inc(tables, 1)
                pool.tensor_copy(chip.m2_ident[:, :], chip.ident[:, :]).then_inc(tables, 1)
                pool.wait_ge(vec_loaded, 48)
                pool.tensor_scalar(chip.m2_vec[:, :, :], chip.m2_vec[:, :, :], 0.5, None, ALU.mult).then_inc(vec_ready, 1)
                pool.tensor_scalar(chip.m2_nw[:, :], chip.m2_nw[:, :], 0.5, None, ALU.mult).then_inc(vec_ready, 1)

            @block.tensor
            def _(pe):
                pe.wait_ge(loaded, 64)
                for group in range(2):
                    for half in range(2):
                        for k in range(KD):
                            m = pe.matmul(ps_dt[0:96, group, half, :], w_dt[:, k, group, :],
                                          chip.x_feat[:, k, half * 512:(half + 1) * 512], start=(k == 0), stop=(k == KD - 1))
                m.then_inc(dt_made, 1)
                for which in range(2):
                    for half in range(2):
                        for k in range(KD):
                            m = pe.matmul(ps_bc[:, which, half, :], w_bc[:, k, which, :],
                                          chip.x_feat[:, k, half * 512:(half + 1) * 512], start=(k == 0), stop=(k == KD - 1))
                    m.then_inc(bc_made, 1)
                pe.wait_ge(z_ready, 2)
                for n, (source, ready) in enumerate(((soft, dt_ready), (cum, cum_ready))):
                    pe.wait_ge(ready, 1 if n == 0 else BATCH * 2)
                    for t in range(TILES):
                        for group in range(2):
                            at = (t * 2 + group) * 32
                            m = pe.transpose(ps_dt[:, 0, n, at:at + 32], source[0:32, group, t * P:(t + 1) * P],
                                             chip.ident[0:32, 0:32])
                    m.then_inc(tok_made, 1)
                pe.wait_ge(bc_ready, 2)
                for b in range(BATCH):
                    for j in range(HALVES):
                        m = pe.matmul(ps_bc[:, b // 2, b % 2, j * SEQ:j * P + SEQ],
                                      tanh[:, 0, b * SEQ + j * P:b * SEQ + (j + 1) * P],
                                      tanh[:, 1, b * SEQ + j * P:(b + 1) * SEQ], start=True, stop=True)
                m.then_inc(cb_made, 1)

            @block.scalar
            def _(act):
                act.wait_ge(loaded, 64)
                act.activation(a[:, :], a[:, :], ACT.Exp).then_inc(a_ready, 1)
                act.activation(chip.m2_x_parts[0][:, :, :], chip.x_feat[:, :, :], ACT.Copy).then_inc(x_high_ready, 1)
                act.wait_ge(dt_made, 1)
                for group in range(2):
                    act.activation(z[:, group, :], ps_dt[0:96, group, :, :].rearrange("p a t -> p (a t)"),
                                   ACT.Identity, bias=dt_bias[:, group:group + 1]).then_inc(z_ready, 1)
                act.wait_ge(z_ready, 2)
                act.wait_ge(bc_made, 2)
                act.wait_ge(padded, 2)
                for which in range(2):
                    for half in range(2):
                        act.activation(pad[:, which, 2 * half:2 * half + 2, M2_PAD:],
                                       ps_bc[:, which, half, :].rearrange("p (b t) -> p b t", b=2),
                                       ACT.Copy).then_inc(evacuated, 1)
                act.activation(soft[:, :, :], z[:, :, :], ACT.Abs).then_inc(abs_ready, 1)
                act.wait_ge(abs_ready, 1)
                act.activation(soft[:, :, :], soft[:, :, :], ACT.Exp, scale=-1.0).then_inc(e_ready, 1)
                act.wait_ge(e_ready, 1)
                act.activation(soft[:, :, :], soft[:, :, :], ACT.Ln, bias=1.0).then_inc(ln_ready, 1)
                act.wait_ge(conv_ready, 2)
                act.activation(tanh[:, :, :], conv[:, :, :, :].rearrange("p w b t -> p w (b t)"), ACT.Tanh).then_inc(tanh_ready, 1)
                act.wait_ge(tok_made, 2)
                act.activation(chip.m2_minus_cum_tok[:, :, :, :],
                               ps_dt[:, 0, 1, :].rearrange("p (t g n) -> p t g n", t=TILES, g=2), ACT.Copy,
                               scale=-1.0)
                act.activation(chip.m2_dt_tok[:, :, :, :],
                               ps_dt[:, 0, 0, :].rearrange("p (t g n) -> p t g n", t=TILES, g=2), ACT.Copy)
                act.wait_ge(cb_made, 1)
                act.activation(chip.m2_cb[:, :, :],
                               ps_bc[:, :, :, 0:M2_BLOCKS].rearrange("p a b t -> p (a b) t"), ACT.Copy).then_inc(cb_kept, 1)
                act.wait_ge(cb_kept, 1)

            @block.vector
            def _(dve):
                then_wait = in_turn(dve, turn)
                dve.wait_ge(x_high_ready, 1)
                dve.tensor_tensor(chip.m2_x_parts[1][:, :, :], chip.x_feat[:, :, :], chip.m2_x_parts[0][:, :, :], ALU.subtract)
                dve.wait_ge(vec_ready, 2)
                dve.wait_ge(evacuated, 4)
                for which in range(2):
                    vec = chip.m2_vec[:, M2_CT + which, :]
                    out = conv[:, which, :, :]
                    then_wait(dve.tensor_scalar(out, pad[:, which, :, M2_PAD:], vec[:, 3:4], vec[:, 4:5],
                                                ALU.mult, ALU.add))
                    for tap in range(M2_PAD):
                        m = dve.scalar_tensor_tensor(out=out, in0=pad[:, which, :, tap:tap + SEQ],
                                                     scalar=vec[:, tap:tap + 1], in1=out, op0=ALU.mult, op1=ALU.add)
                        if tap < M2_PAD - 1:
                            then_wait(m)
                    m.then_inc(conv_ready, 1)
                dve.wait_ge(ln_ready, 1)
                dve.scalar_tensor_tensor(out=soft[:, :, :], in0=z[:, :, :], scalar=0.0, in1=soft[:, :, :],
                                         op0=ALU.max, op1=ALU.add).then_inc(dt_ready, 1)
                dve.wait_ge(dt_ready, 1)
                dve.wait_ge(a_ready, 1)
                for group in range(2):
                    then_wait(dve.tensor_scalar(z[:, group, :], soft[:, group, :], a[:, group:group + 1], -1.0,
                                                ALU.mult, ALU.mult))
                for group in range(2):
                    for b in range(BATCH):
                        span = slice(b * SEQ, (b + 1) * SEQ)
                        dve.tensor_tensor_scan(cum[:, group, span], run_ones[:, :], z[:, group, span], 0.0,
                                               ALU.mult, ALU.add).then_inc(cum_ready, 1)
                dve.wait_ge(tanh_ready, 1)
                for which in range(2):
                    dve.scalar_tensor_tensor(out=tanh[:, which, :], in0=tanh[:, which, :], scalar=1.0,
                                             in1=conv[:, which, :, :].rearrange("p b t -> p (b t)"),
                                             op0=ALU.add, op1=ALU.mult).then_inc(bc_ready, 1)
                dve.wait_ge(cum_ready, 2 * BATCH)
                parts = chip.m2_cum_parts
                then_wait(dve.tensor_copy(parts[:, :, :], cum[:, :, :]))
                then_wait(dve.tensor_tensor(z[:, :, :], cum[:, :, :], parts[:, :, :], ALU.subtract))
                then_wait(dve.tensor_copy(mid[:, :, :], z[:, :, :]))
                then_wait(dve.tensor_tensor(z[:, :, :], z[:, :, :], mid[:, :, :], ALU.subtract))
                then_wait(dve.tensor_copy(parts[32:64, :, :], mid[32:64, :, :]))
                then_wait(dve.tensor_copy(parts[64:96, :, :], z[64:96, :, :]))


def mamba2_heads(chip):
    nc, dram = chip.nc, chip.dram
    STEPS = 2 * M2_CT
    with ExitStack() as held:
        part = Part(chip, "m2h", held)
        sb, ps, sem = part.sb, part.ps, part.sem
        w = sb("w", [P, 2, M2_ROW])
        w_parts = [sb(n, [P, 2, M2_W], F32R) for n in ("w_high", "w_low")]
        wo = sb("wo", [P, 2, D])
        pad = sb("pad", [P, 2, 2, M2_PAD + SEQ])
        conv = sb("conv", [P, 2, 2, SEQ])
        tanh_x = sb("tanh_x", [P, HALF_TOK])
        xs = sb("xs", [P, 2, HALF_TOK])
        xdt = sb("xdt", [P, 4, 2, M2_P])
        G = sb("G", [P, 2, 2, 2, M2_BLOCKS])
        tanh_g = sb("tanh_g", [P, HALF_TOK])
        gate = sb("gate", [P, 2, HALF_TOK])
        y = sb("y", [P, HALF_TOK])
        hidden = sb("hidden", [P, 2, HALF_TOK])
        square = sb("square", [P, HALF_TOK])
        squares = sb("squares", [P, HALF_TOK])
        zeros = sb("zeros", [P, 512], BF16)
        rms = sb("rms", [P, 4])
        rms_inv = sb("rms_inv", [P, 4])
        ps_x = ps("ps_x", [P, 512])
        ps_g = ps("ps_g", [P, 512])
        ps_turn = ps("ps_turn", [P, 512])
        ps_y = ps("ps_y", [P, 512])
        ps_diff = ps("ps_diff", [P, 2, 512])
        ps_out = ps("ps_out", [P, 2, 2, D])

        w_loaded = [sem("w_loaded0"), sem("w_loaded1")]
        w_high_ready, w_split = sem("w_high_ready"), sem("w_split")
        x_made, x_evac, conv_ready, tanh_x_ready, xs_ready, x_turned, xdt_ready = (
            sem("x_made"), sem("x_evac"), sem("conv_ready"), sem("tanh_x_ready"), sem("xs_ready"), sem("x_turned"),
            sem("xdt_ready"))
        g_made, tanh_g_ready, gate_ready = sem("g_made"), sem("tanh_g_ready"), sem("gate_ready")
        diff_made, exp_ready, G_ready, y_made, y_read, hidden_ready = (
            sem("diff_made"), sem("exp_ready"), sem("G_ready"), sem("y_made"), sem("y_read"), sem("hidden_ready"))
        square_ready, square_added, wo_ready, out_made = (
            sem("square_ready"), sem("square_added"), sem("wo_ready"), sem("out_made"))
        zeroed, sums_made, rms_ready, rms_inv_ready, out_read, turn = (
            sem("zeroed"), sem("sums_made"), sem("rms_ready"), sem("rms_inv_ready"), sem("out_read"), sem("turn"))

        def steps(eng, step):
            for g in (0, 1, 2):
                step(g, g % 2, g // 2, 0, 0)
            with eng.Fori(0, M2_CT // 2 - 2) as i:
                step(i * 2 + 3, 1, i + 1, 0, 0)
                step(i * 2 + 4, 0, i + 2, 0, 0)
            step(M2_CT - 1, 1, M2_CT // 2 - 1, 0, 0)
            step(M2_CT, 0, M2_CT // 2, 1, 0)
            step(M2_CT + 1, 1, M2_CT // 2, 1, 1)
            step(M2_CT + 2, 0, M2_CT // 2 + 1, 1, 1)
            with eng.Fori(0, M2_CT // 2 - 2) as i:
                step(i * 2 + M2_CT + 3, 1, i + M2_CT // 2 + 1, 1, 1)
                step(i * 2 + M2_CT + 4, 0, i + M2_CT // 2 + 2, 1, 1)
            step(STEPS - 1, 1, STEPS // 2 - 1, 1, 1)
            step(STEPS, 0, STEPS // 2, None, 1)

        with nc.Block() as block:

            @block.sync
            def _(sp):
                def step(g, q, u, half, _):
                    if half is None:
                        return
                    wait_if_positive(sp, w_split, g - 1)
                    wait_if_positive(sp, wo_ready, g - 1)
                    ct = g - M2_CT * half
                    src = dram["m2_w"][ct] if isinstance(ct, int) else dram["m2_w"][bass.ds(ct, 1), :, :].rearrange("a p n -> p (a n)")
                    sp.dma_start(w[:, q, :], src).then_inc(w_loaded[q], 16)

                steps(sp, step)

            @block.gpsimd
            def _(pool):
                pool.memset(zeros[:, :], 0.0).then_inc(zeroed, 1)
                pool.memset(pad[:, :, :, 0:M2_PAD], 0.0).then_inc(zeroed, 1)

                def step(g, q, u, half, prev):
                    if half is not None:
                        for b in range(2):
                            pool.wait_ge(exp_ready, g * 4 + 2 * b + 2)
                            pool.tensor_tensor(G[:, q, b, :, :], G[:, q, b, :, :],
                                               chip.m2_cb[:, 2 * half + b, :].unsqueeze(1).to_broadcast([P, 2, M2_BLOCKS]),
                                               ALU.mult).then_inc(G_ready, 1)
                    if isinstance(g, int) and g == 0:
                        return
                    pool.wait_ge(square_ready, g)
                    if isinstance(g, int) and g in (1, M2_CT + 1):
                        if g > 1:
                            pool.wait_ge(sums_made, 1)
                        pool.tensor_copy(squares[:, :], square[:, :]).then_inc(square_added, 1)
                    else:
                        pool.wait_ge(square_added, g - 1)
                        pool.tensor_tensor(squares[:, :], squares[:, :], square[:, :], ALU.add).then_inc(square_added, 1)
                    if isinstance(g, int) and g in (M2_CT, STEPS):
                        pool.wait_ge(rms_ready, g // M2_CT)
                        pool.tensor_tensor(rms_inv[:, :], rms[:, :], chip.minus_half[:, 0:1].to_broadcast([P, 4]),
                                           ALU.pow).then_inc(rms_inv_ready, 1)

                steps(pool, step)

            @block.scalar
            def _(act):
                def next_high(n, q, u):
                    act.wait_ge(w_loaded[q], (u + 1) * 16)
                    wait_if_positive(act, g_made, n - 1)
                    act.activation(w_parts[0][:, q, :], w[:, q, 0:M2_W], ACT.Copy).then_inc(w_high_ready, 1)

                act.wait_ge(zeroed, 2)
                next_high(0, 0, 0)

                def step(g, q, u, half, prev):
                    if half is not None:
                        ct = g - M2_CT * half

                        def exps(b):
                            for h in range(2):
                                n = 2 * b + h
                                act.wait_ge(diff_made, g * 4 + n + 1)
                                for j, (lo, hi) in enumerate(((0, SEQ), (SEQ, M2_BLOCKS))):
                                    e = act.activation(G[:, q, b, h, lo:hi], ps_diff[:, n % 2, lo:hi], ACT.Exp,
                                                       bias=chip.m2_minus_cum_tok[:, 4 * half + 2 * b + j, h, bass.ds(ct, 1)])
                                e.then_inc(exp_ready, 1)

                        act.wait_ge(w_loaded[q], (u + 1) * 16)
                        wait_if_positive(act, out_made, g - 1)
                        act.activation(wo[:, q, :], w[:, q, M2_W:M2_ROW], ACT.Copy,
                                       scale=chip.m2_nw[:, bass.ds(ct, 1)]).then_inc(wo_ready, 1)
                        wait_if_positive(act, y_made, g - 1)
                        exps(0)
                        act.wait_ge(x_made, g + 1)
                        wait_if_positive(act, conv_ready, g - 1)
                        act.activation(pad[:, q, :, M2_PAD:], ps_x[:, :].rearrange("p (b t) -> p b t", b=2),
                                       ACT.Copy).then_inc(x_evac, 1)
                        vec = chip.m2_vec[:, bass.ds(ct, 1), :].rearrange("p a v -> p (a v)")
                        act.activation(conv[:, q, :, :].rearrange("p b t -> p (b t)"), ps_x[:, :], ACT.Identity,
                                       scale=vec[:, 3:4], bias=vec[:, 4:5]).then_inc(x_evac, 1)
                        exps(1)
                        act.wait_ge(g_made, g + 1)
                        wait_if_positive(act, gate_ready, g)
                        act.activation(tanh_g[:, :], ps_g[:, :], ACT.Tanh, scale=0.5).then_inc(tanh_g_ready, 1)
                        if not (isinstance(g, int) and g == STEPS - 1):
                            next_high(g + 1, 1 - q, u + q)
                        act.wait_ge(conv_ready, g + 1)
                        wait_if_positive(act, xs_ready, g)
                        act.activation(tanh_x[:, :], conv[:, q, :, :].rearrange("p b t -> p (b t)"),
                                       ACT.Tanh).then_inc(tanh_x_ready, 1)
                    if isinstance(g, int) and g == 0:
                        return
                    act.wait_ge(hidden_ready, g)
                    wait_if_positive(act, square_added, g - 1)
                    act.activation(square[:, :], hidden[:, 1 - q, :], ACT.Square, scale=0.5).then_inc(square_ready, 1)

                steps(act, step)

            @block.tensor
            def _(pe):
                pe.wait_ge(zeroed, 2)

                def open_out():
                    for t in range(2):
                        pe.matmul(ps_out[:, t, :, :].rearrange("p a d -> p (a d)"), zeros[:, 0:P], zeros[:, :],
                                  start=True, stop=False)

                def diffs(n, half, b):
                    sel = chip.m2_sel[:, bass.ds(n - M2_CT * half, 1), :].rearrange("p a m -> p (a m)")
                    at = half * HALF_TOK + b * SEQ
                    for h in range(2):
                        wait_if_positive(pe, exp_ready, n * 4 + 2 * b + h - 1)
                        pe.matmul(ps_diff[:, h, P:SEQ], sel, chip.m2_cum_parts[:, h, at + P:at + SEQ],
                                  start=True, stop=True)
                        diagonal = ps_diff[:, h, :].rearrange("p (a i) -> p a i", a=2)[:, :, 0:P]
                        pe.matmul(diagonal, chip.m2_ident[:, :],
                                  chip.m2_mask[:, :].unsqueeze(1).to_broadcast([P, 2, P]), start=True, stop=False)
                        pe.matmul(diagonal, sel, chip.m2_cum_parts[:, h, at:at + SEQ].rearrange("p (a i) -> p a i", a=2),
                                  start=False, stop=True).then_inc(diff_made, 1)

                def step(g, q, u, half, prev):
                    is_first = isinstance(g, int) and g == 0
                    if half is not None:
                        ct = g - M2_CT * half
                        tokens = slice(half * HALF_TOK, (half + 1) * HALF_TOK)
                        def project(bank, which):
                            terms = [(w_part, x_part, k) for k in range(KD) for w_part, x_part in ((0, 0), (0, 1), (1, 0))]
                            for n, (w_part, x_part, k) in enumerate(terms):
                                at = (which * KD + k) * P
                                m = pe.matmul(bank[:, :], w_parts[w_part][:, q, at:at + P], chip.m2_x_parts[x_part][:, k, tokens],
                                              start=(n == 0), stop=(n == len(terms) - 1))
                            return m

                        pe.wait_ge(w_split, g + 1)
                        wait_if_positive(pe, x_evac, g * 2)
                        project(ps_x, 0).then_inc(x_made, 1)
                    if not is_first:
                        pe.wait_ge(G_ready, g * 2)
                        pe.wait_ge(xdt_ready, g)
                        wait_if_positive(pe, y_read, g - 1)
                        for b in range(2):
                            for h in range(2):
                                for j, (lo, hi) in enumerate(((0, SEQ), (SEQ, M2_BLOCKS))):
                                    m = pe.matmul(ps_y[h * M2_P:(h + 1) * M2_P, b * SEQ + j * P:(b + 1) * SEQ],
                                                  xdt[:, 2 * b + j, h, :], G[:, 1 - q, b, h, lo:hi],
                                                  start=(j == 0), stop=(j == 1))
                        m.then_inc(y_made, 1)
                    if half is not None:
                        diffs(g, half, 1)
                        wait_if_positive(pe, gate_ready, g)
                        project(ps_g, 1).then_inc(g_made, 1)
                    if not is_first:
                        pe.wait_ge(hidden_ready, g)
                        pe.wait_ge(wo_ready, g)
                        for t in range(4):
                            m = pe.matmul(ps_out[:, t // 2, t % 2, :], hidden[:, 1 - q, t * P:(t + 1) * P], wo[:, 1 - q, :],
                                          start=False, stop=False)
                        m.then_inc(out_made, 1)
                    if isinstance(g, int) and g in (M2_CT, STEPS):
                        n = g // M2_CT
                        for t in range(2):
                            pe.matmul(ps_out[:, t, :, :].rearrange("p a d -> p (a d)"), zeros[:, 0:P], zeros[:, :],
                                      start=False, stop=True)
                        pe.wait_ge(square_added, g)
                        pe.wait_ge(xdt_ready, g)
                        for t in range(4):
                            m = pe.matmul(ps_turn[:, t:t + 1], squares[:, t * P:(t + 1) * P], chip.ones[:, 0:1],
                                          start=True, stop=True)
                        m.then_inc(sums_made, 1)
                        if n == 1:
                            pe.wait_ge(out_read, 4)
                            open_out()
                    if half is not None:
                        if not (isinstance(g, int) and g == STEPS - 1):
                            diffs(g + 1, 1 if isinstance(g, int) and g == M2_CT - 1 else half, 0)
                        pe.wait_ge(xs_ready, g + 1)
                        wait_if_positive(pe, xdt_ready, g)
                        for t in range(4):
                            m = pe.transpose(ps_turn[:, t * P:(t + 1) * P], xs[:, q, t * P:(t + 1) * P], chip.ident[:, :])
                        m.then_inc(x_turned, 1)

                open_out()
                diffs(0, 0, 0)
                steps(pe, step)

            @block.vector
            def _(dve):
                def next_low(n, q):
                    dve.wait_ge(w_high_ready, n + 1)
                    wait_if_positive(dve, g_made, n - 1)
                    dve.tensor_tensor(w_parts[1][:, q, :], w[:, q, 0:M2_W], w_parts[0][:, q, :],
                                      ALU.subtract).then_inc(w_split, 1)

                next_low(0, 0)

                def step(g, q, u, half, prev):
                    has_prev = not (isinstance(g, int) and g == 0)
                    ct = None if half is None else g - M2_CT * half

                    def add_tap(tap):
                        if half is None:
                            return
                        if tap:
                            dve.wait_ge(turn, g * 2 + tap)
                        out = conv[:, q, :, :]
                        m = dve.scalar_tensor_tensor(out=out, in0=pad[:, q, :, tap:tap + SEQ],
                                                     scalar=chip.m2_vec[:, bass.ds(ct, 1), tap], in1=out,
                                                     op0=ALU.mult, op1=ALU.add)
                        m.then_inc(turn if tap < M2_PAD - 1 else conv_ready, 1)

                    if half is not None:
                        dve.wait_ge(x_evac, g * 2 + 2)
                    add_tap(0)
                    if has_prev:
                        before = g - 1 - M2_CT * prev
                        dve.wait_ge(y_made, g)
                        dve.scalar_tensor_tensor(out=y[:, :], in0=xs[:, 1 - q, :], scalar=chip.m2_d[:, bass.ds(before, 1)],
                                                 in1=ps_y[:, :], op0=ALU.mult, op1=ALU.add).then_inc(y_read, 1)
                    add_tap(1)
                    if has_prev:
                        dve.wait_ge(y_read, g)
                        wait_if_positive(dve, out_made, g - 2)
                        wait_if_positive(dve, square_ready, g - 2)
                        dve.tensor_tensor(hidden[:, 1 - q, :], y[:, :], gate[:, 1 - q, :], ALU.mult).then_inc(hidden_ready, 1)
                    add_tap(2)
                    if half is not None:
                        if not (isinstance(g, int) and g == STEPS - 1):
                            next_low(g + 1, 1 - q)
                        dve.wait_ge(tanh_x_ready, g + 1)
                        dve.scalar_tensor_tensor(out=xs[:, q, :], in0=tanh_x[:, :], scalar=1.0,
                                                 in1=conv[:, q, :, :].rearrange("p b t -> p (b t)"),
                                                 op0=ALU.add, op1=ALU.mult).then_inc(xs_ready, 1)
                        dve.wait_ge(tanh_g_ready, g + 1)
                        dve.scalar_tensor_tensor(out=gate[:, q, :], in0=tanh_g[:, :], scalar=1.0, in1=ps_g[:, :],
                                                 op0=ALU.add, op1=ALU.mult).then_inc(gate_ready, 1)
                    if isinstance(g, int) and g in (M2_CT, STEPS):
                        n = g // M2_CT
                        dve.wait_ge(sums_made, n)
                        dve.tensor_scalar(rms[:, :], ps_turn[:, 0:4], 1.0 / M2_INNER, 1e-5, ALU.mult,
                                          ALU.add).then_inc(rms_ready, 1)
                        dve.wait_ge(rms_inv_ready, n)
                        for t in range(4):
                            x = chip.x_tok[:, 4 * (n - 1) + t, :]
                            dve.scalar_tensor_tensor(out=x, in0=ps_out[:, t // 2, t % 2, :], scalar=rms_inv[:, t:t + 1],
                                                     in1=x, op0=ALU.mult, op1=ALU.add).then_inc(out_read, 1)
                    if half is not None:
                        dve.wait_ge(x_turned, g + 1)
                        dve.tensor_tensor(xdt[:, :, :, :], ps_turn[:, :].rearrange("p (t h c) -> p t h c", t=4, h=2),
                                          chip.m2_dt_tok[:, 4 * half:4 * half + 4, :, bass.ds(ct, 1)].to_broadcast([P, 4, 2, M2_P]),
                                          ALU.mult).then_inc(xdt_ready, 1)

                steps(dve, step)


def post_norm(chip, name):
    with ExitStack() as held:
        part = Part(chip, name, held)
        norm = PostNorm(part)
        turn = part.sem("turn")
        with chip.nc.Block() as block:

            @block.vector
            def _(dve):
                then_wait = in_turn(dve, turn)
                for b in range(BATCH):
                    norm.stats(dve, then_wait, b)
                    if b:
                        norm.scale(dve, b - 1)
                norm.scale(dve, BATCH - 1)

            @block.gpsimd
            def _(pool):
                norm.rstds(pool)

            @block.tensor
            def _(pe):
                norm.turn(pe)

            @block.scalar
            def _(act):
                norm.write_feat(act)


def mamba2(chip):
    with ExitStack() as outer:
        mamba2_setup(chip, outer)
        mamba2_heads(chip)
    post_norm(chip, "m2n")


def mamba2_inputs(given):
    import numpy as np

    w = given["L0_attn_in_proj_w"]
    conv_end = M2_INNER + M2_INNER + 2 * M2_N

    def tiles(m):
        return m.reshape(KD, P, -1, P).transpose(2, 1, 0, 3)

    gate, x, bc, dt = (w[:, :M2_INNER], w[:, M2_INNER:2 * M2_INNER], w[:, 2 * M2_INNER:conv_end], w[:, conv_end:])
    by_group = lambda v: np.stack([np.concatenate([v[..., g::2]] * 3, axis=-1) for g in range(2)], axis=-2)
    vec = np.concatenate([given["L0_attn_conv_w"], given["L0_attn_conv_b"][:, None]], axis=1)
    return {
        "m2_w": np.concatenate([tiles(x).reshape(M2_CT, P, -1), tiles(gate).reshape(M2_CT, P, -1),
                                given["L0_attn_out_proj_w"].reshape(M2_CT, P, D)], axis=2),
        "m2_w_bc": tiles(bc).transpose(1, 2, 0, 3),
        "m2_w_dt": by_group(dt.reshape(KD, P, M2_HEADS)).transpose(1, 0, 2, 3),
        "m2_dt_bias": by_group(given["L0_attn_dt_bias"]).T,
        "m2_a_log": by_group(given["L0_attn_A_log"]).T,
        "m2_vec": vec.reshape(M2_CT + 2, P, M2_VEC).transpose(1, 0, 2),
        "m2_d": np.repeat(given["L0_attn_D_param"], M2_P).reshape(M2_CT, P).T,
        "m2_nw": given["L0_attn_norm_w"].reshape(M2_CT, P).T,
    }


MORE = [mamba2_inputs]



BM_DI, BM_DS, BM_K, BM_R = 512, 16, 4, 128
BM_CT = BM_DI // P
BM_PAD = BM_K - 1
BM_BC = 3 * 2 * BM_DS


class BiWeights:

    def __init__(self, chip, part):
        self.chip = chip
        self.w_xz = part.sb("w_xz", [P, KD, 2 * BM_DI])
        self.w_proj = part.sb("w_proj", [P, BM_CT, BM_R + BM_BC])
        self.w_dt = part.sb("w_dt", [P, BM_DI])
        self.vec = part.sb("vec", [P, BM_CT, BM_K + 1])
        self.dt_b = part.sb("dt_b", [P, BM_CT])
        self.A = part.sb("A", [P, 2, BM_DS, BM_CT])
        self.skip = part.sb("skip", [P, 2, BM_CT])
        self.w_out = part.sb("w_out", [P, 2, BM_CT, D])
        self.twice = part.sb("twice", [P, KD, D])
        self.diag_skip = part.sb("diag_skip", [P, BM_CT, P])
        self.loaded, self.out_loaded, self.vec_loaded = (
            part.sem("way_loaded"), part.sem("way_out_loaded"), part.sem("way_vec_loaded"))

    def load(self, sp, back, way):
        dram = self.chip.dram
        sp.dma_start(self.w_xz[:, :, :], dram[f"{way}_w_xz"]).then_inc(self.loaded, 16)
        sp.dma_start(self.w_proj[:, :, :], dram[f"{way}_w_proj"]).then_inc(self.loaded, 16)
        sp.dma_start(self.w_dt[:, :], dram[f"{way}_w_dt"]).then_inc(self.loaded, 16)
        sp.dma_start(self.vec[:, :, :], dram[f"{way}_vec"]).then_inc(self.vec_loaded, 16)
        sp.dma_start(self.dt_b[:, :], dram[f"{way}_dt_b"]).then_inc(self.vec_loaded, 16)
        sp.dma_start(self.A[:, back, :, :], dram[f"{way}_a_log"]).then_inc(self.vec_loaded, 16)
        sp.dma_start(self.skip[:, back, :], dram[f"{way}_d"]).then_inc(self.vec_loaded, 16)
        sp.dma_start(self.w_out[:, back, :, :], dram[f"{way}_w_out"]).then_inc(self.out_loaded, 16)


def bi_head(chip, part, h_feat, sel, weights):
    nc, dram = chip.nc, chip.dram
    w_in = part.sb("w_in", [P, KD, D])
    b_in = part.sb("b_in", [P, KD])
    loaded, made, h_ready = part.sem("head_loaded"), part.sem("head_made"), part.sem("h_ready")
    with ExitStack() as held:
        ps_h = Part(chip, "bmh", held).ps("ps_h", [P, KD, 2, 512])
        sel_ready = part.sem("sel_ready")
        with nc.Block() as block:

            @block.gpsimd
            def _(pool):
                pool.memset(sel[:, :, :], 0.0).then_inc(sel_ready, 1)
                for r in range(3):
                    pool.wait_ge(sel_ready, 1 + r)
                    pool.affine_select(out=sel[:, :, :], in_=sel[:, :, :], compare_op=ALU.not_equal, fill=1.0,
                                       base=-32 * r, pattern=[[-1, 32], [0, P]], channel_multiplier=1).then_inc(sel_ready, 1)
                twice = weights.twice
                pool.memset(twice[:, :, :], 0.0).then_inc(sel_ready, 1)
                pool.wait_ge(sel_ready, 5)
                for k in range(KD):
                    pool.tensor_scalar(twice[:, k, k * P:(k + 1) * P], chip.ident[:, :], 2.0, None, ALU.mult)

            @block.sync
            def _(sp):
                sp.dma_start(w_in[:, :, :], dram["bm_w_in"]).then_inc(loaded, 16)
                sp.dma_start(b_in[:, :], dram["bm_b_in"]).then_inc(loaded, 16)
                weights.load(sp, 0, "fm")

            @block.tensor
            def _(pe):
                pe.wait_ge(loaded, 32)
                for m in range(KD):
                    for half in range(2):
                        for k in range(KD):
                            o = pe.matmul(ps_h[:, m, half, :], w_in[:, k, m * P:(m + 1) * P],
                                          chip.x_feat[:, k, half * 512:(half + 1) * 512], start=(k == 0), stop=(k == KD - 1))
                    o.then_inc(made, 1)

            @block.scalar
            def _(act):
                for m in range(KD):
                    act.wait_ge(made, m + 1)
                    act.activation(h_feat[:, m, :], ps_h[:, m, :, :].rearrange("p a t -> p (a t)"), ACT.Gelu,
                                   bias=b_in[:, m:m + 1]).then_inc(h_ready, 1)


def bi_setup(chip, name, back, bufs, weights):
    nc = chip.nc
    xi, z, dt, u, h_feat, bc_parts, _ = bufs
    A = weights.A[:, back, :, :]
    w_xz, w_proj, w_dt, vec, dt_b = weights.w_xz, weights.w_proj, weights.w_dt, weights.vec, weights.dt_b
    with ExitStack() as held:
        part = Part(chip, name, held)
        sb, ps, sem = part.sb, part.ps, part.sem
        pad = sb("pad", [P, 2, BATCH, SEQ + BM_PAD])
        tanh = sb("tanh", [P, TOK])
        rank = sb("rank", [P, TOK])
        bc = sb("bc", [BM_BC, TOK])
        bc_mid = sb("bc_mid", [BM_BC, TOK], BF16)
        ln = sb("ln", [P, BM_CT, TOK])
        series_ready = sem("series_ready")
        is_small = sb("is_small", [P, TOK], mybir.dt.int32)
        ps_a = ps("ps_a", [P, 2, 2, 512])
        ps_rank = ps("ps_rank", [P, 2, 512])
        ps_bc = ps("ps_bc", [BM_BC, 2, 512])
        vec_ready, padded, a_ready = (
            sem("vec_ready"), sem("padded"), sem("a_ready"))
        made, evac, conv_ready, tanh_ready, silu_ready = (
            sem("made"), sem("evac"), sem("conv_ready"), sem("tanh_ready"), sem("silu_ready"))
        proj_made, rank_ready, bc_ready, dt_made, dt_evac = (
            sem("proj_made"), sem("rank_ready"), sem("bc_ready"), sem("dt_made"), sem("dt_evac"))
        abs_ready, soft_ready, dt_ready, u_ready, turn, exp_ready = (
            sem("abs_ready"),
            sem("soft_ready"), sem("dt_ready"), sem("u_ready"), sem("turn"), sem("exp_ready"))
        own = 0 if back else BM_PAD
        tap_at = lambda tap: BM_PAD - tap if back else tap

        with nc.Block() as block:

            @block.gpsimd
            def _(pool):
                zeros = slice(SEQ, SEQ + BM_PAD) if back else slice(0, BM_PAD)
                pool.memset(pad[:, :, :, zeros], 0.0).then_inc(padded, 1)
                pool.wait_ge(weights.vec_loaded, (back + 1) * 64)
                pool.tensor_scalar(vec[:, :, :], vec[:, :, :], 0.5, None, ALU.mult).then_inc(vec_ready, 1)
                pool.wait_ge(a_ready, 1)
                pool.tensor_scalar(A[:, :, :], A[:, :, :], -1.0, None, ALU.mult).then_inc(vec_ready, 1)
                for ct in range(BM_CT):
                    pool.tensor_scalar(weights.diag_skip[:, ct, :], chip.ident[:, :], weights.skip[:, back, ct:ct + 1], None, ALU.mult)

            @block.tensor
            def _(pe):
                pe.wait_ge(weights.loaded, (back + 1) * 48)
                pe.wait_ge(weights.out_loaded, (back + 1) * 16)
                def xz(m, slot):
                    for half in range(2):
                        for k in range(KD):
                            o = pe.matmul(ps_a[:, slot, half, :], w_xz[:, k, m * P:(m + 1) * P],
                                          h_feat[:, k, half * 512:(half + 1) * 512], start=(k == 0), stop=(k == KD - 1))
                    o.then_inc(made, 1)

                for m in range(BM_CT):
                    if m >= 2:
                        pe.wait_ge(evac, 2 * (m - 1))
                    xz(m, m % 2)
                for k in range(BM_CT):
                    pe.wait_ge(silu_ready, k + 1)
                    for half in range(2):
                        span = slice(half * 512, (half + 1) * 512)
                        pe.matmul(ps_rank[:, half, :], w_proj[:, k, 0:BM_R], xi[:, k, span], start=(k == 0), stop=(k == BM_CT - 1))
                        o = pe.matmul(ps_bc[:, half, :], w_proj[:, k, BM_R:], xi[:, k, span], start=(k == 0), stop=(k == BM_CT - 1))
                o.then_inc(proj_made, 1)
                pe.wait_ge(rank_ready, 1)
                for m in range(BM_CT):
                    if m >= 2:
                        pe.wait_ge(dt_evac, m - 1)
                    for half in range(2):
                        o = pe.matmul(ps_a[:, m % 2, half, :], w_dt[:, m * P:(m + 1) * P], rank[:, half * 512:(half + 1) * 512],
                                      start=True, stop=True)
                    o.then_inc(dt_made, 1)
                for m in range(BM_CT):
                    if m < 2:
                        pe.wait_ge(dt_evac, m + 3)
                    else:
                        pe.wait_ge(silu_ready, BM_CT + m - 1)
                    xz(BM_CT + m, m % 2)

            @block.scalar
            def _(act):
                act.wait_ge(padded, 1)
                act.wait_ge(weights.vec_loaded, (back + 1) * 64)
                act.activation(A[:, :, :], A[:, :, :], ACT.Exp).then_inc(a_ready, 1)
                act.wait_ge(vec_ready, 1)

                def x_tile(m):
                    flat = ps_a[:, m % 2, :, :].rearrange("p a t -> p (a t)")
                    act.wait_ge(made, m + 1)
                    if m >= 2:
                        act.wait_ge(conv_ready, m - 1)
                    act.activation(pad[:, m % 2, :, own:own + SEQ], flat.rearrange("p (b t) -> p b t", b=BATCH),
                                   ACT.Copy).then_inc(evac, 1)
                    act.activation(xi[:, m, :], flat, ACT.Identity, scale=vec[:, m, BM_K - 1:BM_K],
                                   bias=vec[:, m, BM_K:BM_K + 1]).then_inc(evac, 1)

                def tanh_x(m):
                    act.wait_ge(conv_ready, m + 1)
                    if m:
                        act.wait_ge(silu_ready, m)
                    act.activation(tanh[:, :], xi[:, m, :], ACT.Tanh).then_inc(tanh_ready, 1)

                x_tile(0)
                for m in range(1, BM_CT):
                    x_tile(m)
                    tanh_x(m - 1)
                tanh_x(BM_CT - 1)
                act.wait_ge(proj_made, 1)
                act.activation(rank[:, :], ps_rank[:, :, :].rearrange("p a t -> p (a t)"), ACT.Copy).then_inc(rank_ready, 1)
                act.activation(bc[:, :], ps_bc[:, :, :].rearrange("p a t -> p (a t)"), ACT.Copy).then_inc(bc_ready, 1)
                for m in range(BM_CT):
                    act.wait_ge(dt_made, m + 1)
                    act.activation(dt[:, m, :], ps_a[:, m % 2, :, :].rearrange("p a t -> p (a t)"), ACT.Identity,
                                   bias=dt_b[:, m:m + 1]).then_inc(dt_evac, 1)
                    act.wait_ge(dt_evac, m + 1)
                    act.activation(u[:, m, :], dt[:, m, :], ACT.Abs).then_inc(abs_ready, 1)
                    act.wait_ge(abs_ready, m + 1)
                    act.activation(u[:, m, :], u[:, m, :], ACT.Exp, scale=-1.0).then_inc(exp_ready, 1)
                act.wait_ge(exp_ready, BM_CT)
                for m in range(BM_CT):
                    act.activation(ln[:, m, :], u[:, m, :], ACT.Ln, bias=1.0).then_inc(soft_ready, 1)
                for m in range(BM_CT):
                    act.wait_ge(made, BM_CT + m + 1)
                    act.wait_ge(silu_ready, BM_CT + m)
                    act.activation(tanh[:, :], ps_a[:, m % 2, :, :].rearrange("p a t -> p (a t)"), ACT.Tanh,
                                   scale=0.5).then_inc(tanh_ready, 1)

            @block.vector
            def _(dve):
                then_wait = in_turn(dve, turn)
                dve.wait_ge(vec_ready, 1)
                def conv(m):
                    dve.wait_ge(evac, 2 * (m + 1))
                    out = xi[:, m, :].rearrange("p (b t) -> p b t", b=BATCH)
                    for tap in range(BM_PAD):
                        at = tap_at(tap)
                        c = dve.scalar_tensor_tensor(out=out, in0=pad[:, m % 2, :, at:at + SEQ], scalar=vec[:, m, tap:tap + 1],
                                                     in1=out, op0=ALU.mult, op1=ALU.add)
                        if tap < BM_PAD - 1:
                            then_wait(c)
                    c.then_inc(conv_ready, 1)

                def silu_x(m):
                    dve.wait_ge(tanh_ready, m + 1)
                    dve.scalar_tensor_tensor(out=xi[:, m, :], in0=tanh[:, :], scalar=1.0, in1=xi[:, m, :],
                                             op0=ALU.add, op1=ALU.mult).then_inc(silu_ready, 1)

                conv(0)
                for m in range(1, BM_CT):
                    conv(m)
                    silu_x(m - 1)
                silu_x(BM_CT - 1)
                dve.wait_ge(bc_ready, 1)
                then_wait(dve.tensor_copy(bc_parts[:, :], bc[:, :]))
                then_wait(dve.tensor_tensor(bc[:, :], bc[:, :], bc_parts[:, :], ALU.subtract))
                then_wait(dve.tensor_copy(bc_mid[:, :], bc[:, :]))
                then_wait(dve.tensor_tensor(bc[:, :], bc[:, :], bc_mid[:, :], ALU.subtract))
                then_wait(dve.tensor_copy(bc_parts[32:64, :], bc_mid[32:64, :]))
                then_wait(dve.tensor_copy(bc_parts[64:96, :], bc[64:96, :]))
                for m in range(BM_CT):
                    dve.wait_ge(exp_ready, m + 1)
                    e, series = u[:, m, :], z[:, m, :]
                    then_wait(dve.tensor_scalar(series, e, 1.0 / 3.0, -0.5, ALU.mult, ALU.add))
                    then_wait(dve.tensor_tensor(series, series, e, ALU.mult))
                    dve.scalar_tensor_tensor(out=series, in0=series, scalar=1.0, in1=e, op0=ALU.add,
                                             op1=ALU.mult).then_inc(series_ready, 1)
                dve.wait_ge(series_ready, BM_CT)
                for m in range(BM_CT):
                    then_wait(dve.tensor_scalar(is_small[:, :], u[:, m, :], 1.0 / 128.0, None, ALU.is_lt))
                    dve.wait_ge(soft_ready, m + 1)
                    then_wait(dve.copy_predicated(ln[:, m, :], is_small[:, :], z[:, m, :]))
                    dve.scalar_tensor_tensor(out=dt[:, m, :], in0=dt[:, m, :], scalar=0.0, in1=ln[:, m, :],
                                             op0=ALU.max, op1=ALU.add).then_inc(dt_ready, 1)
                    dve.wait_ge(tanh_ready, BM_CT + m + 1)
                    dve.scalar_tensor_tensor(out=z[:, m, :], in0=tanh[:, :], scalar=1.0,
                                             in1=ps_a[:, m % 2, :, :].rearrange("p a t -> p (a t)"),
                                             op0=ALU.add, op1=ALU.mult).then_inc(silu_ready, 1)
                    dve.wait_ge(dt_ready, m + 1)
                    dve.tensor_tensor(u[:, m, :], dt[:, m, :], xi[:, m, :], ALU.mult).then_inc(u_ready, 1)
                dve.wait_ge(u_ready, BM_CT)


def bi_scan(chip, name, back, bufs, weights):
    nc = chip.nc
    xi, z, dt, u, _, bc_parts, sel = bufs
    A = weights.A[:, back, :, :]
    GROUPS, LAST = 2 * (BM_CT // 2), BM_DS - 1
    with ExitStack() as held:
        part = Part(chip, name, held)
        sb, ps, sem = part.sb, part.ps, part.sem
        decay = sb("decay", [P, 4, HALF_TOK])
        state = sb("state", [P, 4, HALF_TOK])
        read = sb("read", [P, 4, HALF_TOK])
        c_row = sb("c_row", [P, 2, HALF_TOK])
        zeros = sb("zeros", [P, 512], BF16)
        ps_y = ps("ps_y", [P, 2, 512])
        ps_b = ps("ps_b", [P, 2, 512])
        ps_c = ps("ps_c", [P, 512])
        ps_inp = ps("ps_inp", [P, 2, 512])
        cleared, b_made, c_made, c_kept, decay_ready, inp_ready, state_ready, read_ready, added = (
            sem("cleared"), sem("b_made"), sem("c_made"), sem("c_kept"), sem("decay_ready"), sem("inp_ready"), sem("state_ready"),
            sem("read_ready"), sem("added"))
        closed, gated = sem("closed"), sem("gated")
        first = SEQ - 1 if back else 0
        rest = slice(0, SEQ - 1) if back else slice(1, SEQ)
        by_batch = lambda ap: ap.rearrange("p (b t) -> p b t", b=2)
        order = (lambda ap: ap[:, ::-1]) if back else (lambda ap: ap)
        tokens = lambda group: slice(group // 2 * HALF_TOK, (group // 2 + 1) * HALF_TOK)
        tile = lambda group, c: group % 2 * 2 + c

        def over_states(eng, body):
            for group in range(GROUPS):
                base = group * BM_DS
                body(base, 0, 0, group)
                body(base + 1, 1, 1, group)
                with eng.Fori(0, BM_DS // 2 - 2) as i:
                    body(i * 2 + base + 2, i * 2 + 2, 0, group)
                    body(i * 2 + base + 3, i * 2 + 3, 1, group)
                body(base + LAST - 1, LAST - 1, 0, group)
                body(base + LAST, LAST, 1, group)

        def two_on(S, s, group):
            if isinstance(s, int) and s + 2 > LAST:
                return (S + 2, s + 2 - BM_DS, group + 1) if group + 1 < GROUPS else None
            return S + 2, s + 2, group

        with nc.Block() as block:

            @block.sync
            def _(sp):
                if not back:
                    weights.load(sp, 1, "bm")

            @block.gpsimd
            def _(pool):
                pool.memset(decay[:, :, :].rearrange("p a (b t) -> p a b t", b=2)[:, :, :, first:first + 1], 0.0).then_inc(cleared, 1)
                pool.memset(zeros[:, :], 0.0).then_inc(cleared, 1)

                def body(S, s, q, group):
                    pool.wait_ge(c_kept, S + 1)
                    for c in range(2):
                        n = S * 2 + c
                        pool.wait_ge(state_ready, n + 1)
                        wait_if_positive(pool, added, n - 3)
                        pool.tensor_tensor(read[:, 2 * q + c, :], state[:, 2 * q + c, :], c_row[:, q, :], ALU.mult).then_inc(read_ready, 1)

                over_states(pool, body)

            @block.scalar
            def _(act):
                act.wait_ge(cleared, 2)

                def body(S, s, q, group):
                    act.wait_ge(c_made, S + 1)
                    wait_if_positive(act, read_ready, S * 2 - 2)
                    act.activation(c_row[:, q, :], ps_c[:, :], ACT.Copy).then_inc(c_kept, 1)
                    for c in range(2):
                        n = S * 2 + c
                        wait_if_positive(act, state_ready, n - 3)
                        act.activation(by_batch(decay[:, 2 * q + c, :])[:, :, rest],
                                       by_batch(dt[:, tile(group, c), tokens(group)])[:, :, rest], ACT.Exp,
                                       scale=A[:, bass.ds(s, 1), tile(group, c)]).then_inc(decay_ready, 1)

                over_states(act, body)

            @block.vector
            def _(dve):
                def make_input(S, q, group, c):
                    n = S * 2 + c
                    dve.wait_ge(b_made, S + 1)
                    wait_if_positive(dve, state_ready, n - 1)
                    dve.tensor_tensor(ps_inp[:, c, :], u[:, tile(group, c), tokens(group)], ps_b[:, q, :],
                                      ALU.mult).then_inc(inp_ready, 1)

                def scan(S, q, c):
                    slot = 2 * q + c
                    n = S * 2 + c
                    dve.wait_ge(inp_ready, n + 1)
                    dve.wait_ge(decay_ready, n + 1)
                    wait_if_positive(dve, read_ready, n - 3)
                    dve.tensor_tensor_scan(order(state[:, slot, :]), order(decay[:, slot, :]), order(ps_inp[:, c, :]),
                                           0.0, ALU.mult, ALU.add).then_inc(state_ready, 1)

                def gate(group):
                    dve.wait_ge(closed, group + 1)
                    for c in range(2):
                        ct = tile(group, c)
                        dve.tensor_tensor(z[:, ct, tokens(group)], z[:, ct, tokens(group)], ps_y[:, c, :],
                                          ALU.mult).then_inc(gated, 1)

                def body(S, s, q, group):
                    make_input(S, q, group, 0)
                    make_input(S, q, group, 1)
                    scan(S, q, 0)
                    scan(S, q, 1)
                    if group and isinstance(s, int) and s == 0:
                        gate(group - 1)

                over_states(dve, body)
                gate(GROUPS - 1)

            @block.tensor
            def _(pe):
                def spread(what, S, s, q, group):
                    if what == 0:
                        wait_if_positive(pe, inp_ready, S * 2 - 2)
                    else:
                        wait_if_positive(pe, c_kept, S)
                    pe.matmul(ps_b[:, q, :] if what == 0 else ps_c[:, :],
                              sel[:, bass.ds(s * 2 + what, 1), :].rearrange("p a m -> p (a m)"), bc_parts[:, tokens(group)],
                              start=True, stop=True).then_inc(c_made if what else b_made, 1)

                def body(S, s, q, group):
                    following = two_on(S, s, group)
                    if following:
                        spread(0, following[0], following[1], q, following[2])
                    if isinstance(s, int) and s == 0:
                        wait_if_positive(pe, gated, group * 2)
                        for c in range(2):
                            pe.matmul(ps_y[:, c, :], weights.diag_skip[:, tile(group, c), :], xi[:, tile(group, c), tokens(group)],
                                      start=True, stop=False)
                    for c in range(2):
                        n = S * 2 + c
                        pe.wait_ge(read_ready, n + 1)
                        pe.matmul(ps_y[:, c, :], chip.ident[:, :], read[:, 2 * q + c, :], start=False, stop=False).then_inc(added, 1)
                        if c == 0 and following:
                            spread(1, following[0], following[1], q, following[2])
                    if isinstance(s, int) and s == LAST:
                        for c in range(2):
                            m = pe.matmul(ps_y[:, c, :], zeros[:, 0:P], zeros[:, :], start=False, stop=True)
                        m.then_inc(closed, 1)

                pe.wait_ge(cleared, 2)
                for S in range(2):
                    for what in range(2):
                        spread(what, S, S, S, 0)
                over_states(pe, body)


def bi_out(chip, name, back, bufs, weights, total):
    nc = chip.nc
    z, h_feat = bufs[1], bufs[4]
    with ExitStack() as held:
        part = Part(chip, name, held)
        w_out, twice = weights.w_out[:, back, :, :], weights.twice
        ps_out = part.ps("ps_out", [P, BATCH, 2, D])
        made, summed = part.sem("made"), part.sem("summed")
        with nc.Block() as block:

            @block.tensor
            def _(pe):
                for t in range(TILES):
                    for k in range(BM_CT):
                        o = pe.matmul(ps_out[:, t // 2, t % 2, :], z[:, k, t * P:(t + 1) * P], w_out[:, k, :],
                                      start=(k == 0), stop=(k == BM_CT - 1 and bool(back)))
                    if not back:
                        for k in range(KD):
                            o = pe.matmul(ps_out[:, t // 2, t % 2, :], h_feat[:, k, t * P:(t + 1) * P], twice[:, k, :],
                                          start=False, stop=(k == KD - 1))
                    o.then_inc(made, 1)

            @block.vector
            def _(dve):
                for b in range(BATCH):
                    dve.wait_ge(made, 2 * (b + 1))
                    out = total[:, 2 * b:2 * b + 2, :]
                    if back:
                        dve.scalar_tensor_tensor(out=out, in0=ps_out[:, b, :, :], scalar=0.5, in1=out,
                                                 op0=ALU.mult, op1=ALU.add).then_inc(summed, 1)
                    else:
                        dve.tensor_scalar(out, ps_out[:, b, :, :], 0.5, None, ALU.mult).then_inc(summed, 1)


def bi_tail(chip, name, total):
    nc, dram = chip.nc, chip.dram
    with ExitStack() as held:
        part = Part(chip, name, held)
        sb, ps, sem = part.sb, part.ps, part.sem
        norm = PostNorm(part)
        w_out = sb("w_out", [P, KD, D])
        gain = sb("gain", [P, KD])
        shift = sb("shift", [P, KD])
        b_out = sb("b_out", [P, D])
        raw = sb("raw", [P, TILES, 6])
        mean_var = sb("mean_var", [P, TILES, 2])
        var_eps = sb("var_eps", [P, TILES])
        rstd = sb("rstd", [P, TILES])
        feat = sb("feat", [P, KD, TOK])
        ps_turn = ps("ps_turn", [P, 2, 512])
        ps_out = ps("ps_out", [P, BATCH, 2, D])
        loaded, tables, turn, stats_ready, eps_added, rstd_ready, normed, turned, feat_ready, made = (
            sem("loaded"), sem("tables"), sem("turn"), sem("stats_ready"), sem("eps_added"), sem("rstd_ready"),
            sem("normed"), sem("turned"), sem("feat_ready"), sem("made"))
        with nc.Block() as block:

            @block.sync
            def _(sp):
                sp.dma_start(w_out[:, :, :], dram["bm_w_last"]).then_inc(loaded, 16)
                sp.dma_start(gain[:, :], dram["bm_ln_g"]).then_inc(tables, 16)
                sp.dma_start(shift[:, :], dram["bm_ln_b"]).then_inc(tables, 16)
                sp.dma_start(b_out[:, :], dram["bm_b_out"].partition_broadcast(P)).then_inc(tables, 16)

            @block.gpsimd
            def _(pool):
                for b in range(BATCH):
                    two = slice(2 * b, 2 * b + 2)
                    pool.wait_ge(stats_ready, 2 * (b + 1))
                    pool.tensor_scalar(var_eps[:, two], mean_var[:, two, 1], LN_EPS, None, ALU.add).then_inc(eps_added, 1)
                    pool.wait_ge(eps_added, b + 1)
                    pool.tensor_tensor(rstd[:, two], var_eps[:, two], chip.minus_half[:, 0:2],
                                       ALU.pow).then_inc(rstd_ready, 1)
                norm.rstds(pool)

            @block.tensor
            def _(pe):
                for b in range(BATCH):
                    pe.wait_ge(normed, 2 * (b + 1))
                    if b >= 2:
                        pe.wait_ge(feat_ready, KD * (b - 1))
                    for k in range(KD):
                        for h in range(HALVES):
                            at = (k * HALVES + h) * P
                            m = pe.transpose(ps_turn[:, b % 2, at:at + P], total[:, 2 * b + h, k * P:(k + 1) * P],
                                             chip.ident[:, :])
                    m.then_inc(turned, 1)
                pe.wait_ge(loaded, 16)
                for t in range(TILES):
                    pe.wait_ge(feat_ready, KD * (t // 2 + 1))
                    for k in range(KD):
                        m = pe.matmul(ps_out[:, t // 2, t % 2, :], feat[:, k, t * P:(t + 1) * P], w_out[:, k, :],
                                      start=(k == 0), stop=(k == KD - 1))
                    m.then_inc(made, 1)
                norm.turn(pe)

            @block.scalar
            def _(act):
                act.wait_ge(tables, 48)
                for b in range(BATCH):
                    act.wait_ge(turned, b + 1)
                    for k in range(KD):
                        act.activation(feat[:, k, b * SEQ:(b + 1) * SEQ], ps_turn[:, b % 2, k * SEQ:(k + 1) * SEQ],
                                       ACT.Identity, scale=gain[:, k:k + 1], bias=shift[:, k:k + 1]).then_inc(feat_ready, 1)
                norm.write_feat(act)

            @block.vector
            def _(dve):
                then_wait = in_turn(dve, turn)
                for b in range(BATCH):
                    for t in (2 * b, 2 * b + 1):
                        then_wait(dve.bn_stats(raw[:, t, :], total[:, t, :]))
                        dve.bn_aggr(mean_var[:, t, :], raw[:, t, :]).then_inc(stats_ready, 1)
                for b in range(BATCH):
                    dve.wait_ge(rstd_ready, b + 1)
                    for t in (2 * b, 2 * b + 1):
                        dve.tensor_scalar(total[:, t, :], total[:, t, :], mean_var[:, t, 0:1], rstd[:, t:t + 1],
                                          ALU.subtract, ALU.mult).then_inc(normed, 1)
                dve.wait_ge(tables, 48)
                for b in range(BATCH):
                    x = chip.x_tok[:, 2 * b:2 * b + 2, :]
                    then_wait(dve.tensor_tensor(x, x, b_out[:, :].unsqueeze(1).to_broadcast([P, 2, D]), ALU.add))
                    dve.wait_ge(made, 2 * (b + 1))
                    then_wait(dve.tensor_tensor(x, x, ps_out[:, b, :, :], ALU.add))
                    norm.stats(dve, then_wait, b)
                    if b:
                        norm.scale(dve, b - 1)
                norm.scale(dve, BATCH - 1)


def bi_mamba(chip):
    with ExitStack() as outer:
        part = Part(chip, "bm", outer)
        h_feat = part.sb("h_feat", [P, KD, TOK])
        total = part.sb("total", [P, TILES, D])
        bufs = tuple(part.sb(n, [P, BM_CT, TOK]) for n in ("xi", "z", "dt", "u")) + (
            h_feat,
            part.sb("bc_parts", [BM_BC, TOK], BF16), part.sb("sel", [BM_BC, 2 * BM_DS, P], BF16))
        weights = BiWeights(chip, part)
        bi_head(chip, part, h_feat, bufs[-1], weights)
        for back, way in enumerate(("fm", "bm")):
            bi_setup(chip, f"{way}s", back, bufs, weights)
            bi_scan(chip, f"{way}r", back, bufs, weights)
            bi_out(chip, f"{way}o", back, bufs, weights, total)
        bi_tail(chip, "bmt", total)


def bi_mamba_inputs(given):
    import numpy as np

    def halves(w):
        return w.reshape(w.shape[0] // P, P, -1).transpose(1, 0, 2)

    columns = lambda v: v.reshape(-1, P).T
    g = lambda n: given[f"L1_attn_{n}"]
    out = {"bm_w_in": halves(g("w_in").T), "bm_b_in": columns(g("b_in")), "bm_w_last": halves(g("w_out").T),
           "bm_ln_g": columns(g("ln_g")), "bm_ln_b": columns(g("ln_b")), "bm_b_out": g("b_out").reshape(1, D)}
    turn = list(range(BM_R)) + [BM_R + which * BM_DS + s for s in range(BM_DS) for which in range(2)] * 3
    for way in ("fm", "bm"):
        h = lambda n: g(f"{way}_{n}")
        out[f"{way}_w_xz"] = halves(h("in_w").T)
        out[f"{way}_w_proj"] = halves(h("xproj_w")[turn].T)
        out[f"{way}_w_dt"] = h("dt_w").T
        out[f"{way}_vec"] = np.concatenate([h("conv_w"), h("conv_b")[:, None]], axis=1).reshape(BM_CT, P, -1).transpose(1, 0, 2)
        out[f"{way}_dt_b"] = columns(h("dt_b"))
        out[f"{way}_a_log"] = h("A_log").reshape(BM_CT, P, BM_DS).transpose(1, 2, 0)
        out[f"{way}_d"] = columns(h("D"))
        out[f"{way}_w_out"] = halves(h("out_w").T)
    return out


MORE.append(bi_mamba_inputs)



RA_HEADS, RA_K, RA_CQ, RA_R = 16, 128, 192, 64
RA_HQ = RA_CQ // 2
RA_WIDE = D + RA_CQ + CTX + D


def rope_attention(chip, name="ra"):
    nc, dram = chip.nc, chip.dram
    STEPS = 2 * RA_HEADS
    with ExitStack() as outer:
        kept = Part(chip, name, outer)
        kv_tok = kept.sb("kv_tok", [P, TILES, CTX])
        kv_feat = kept.sb("kv_feat", [CTX, TOK])
        cos_q = kept.sb("cos_q", [RA_HQ, 2, SEQ])
        sin_q = kept.sb("sin_q", [RA_HQ, 2, SEQ])
        q_tables = kept.sem("q_tables")
        x_parts = [kept.sb(n, [P, KD, TOK], F32R) for n in ("x_high", "x_low")]
        x_high_ready = kept.sem("x_high_ready")

        with ExitStack() as held:
            part = Part(chip, f"{name}s", held)
            ctx_tok = part.sb("ctx_tok", [P, TILES, CTX])
            cos_k = part.sb("cos_k", [P, HALVES, CTX])
            sin_k = part.sb("sin_k", [P, HALVES, CTX])
            crossed = part.sb("crossed", [P, TILES, CTX])
            ps_kv = part.ps("ps_kv", [CTX, 2, 512])
            loaded, turn, kv_ready, turned, kept_feat = (part.sem("loaded"), part.sem("turn"), part.sem("kv_ready"),
                                                         part.sem("turned"), part.sem("kept_feat"))
            with nc.Block() as block:

                @block.sync
                def _(sp):
                    sp.dma_start(ctx_tok[:, :, :], dram["ctx_tok"]).then_inc(loaded, 16)
                    sp.dma_start(cos_k[:, :, :], dram["rope_cos_k"]).then_inc(loaded, 16)
                    sp.dma_start(sin_k[:, :, :], dram["rope_sin_k"]).then_inc(loaded, 16)
                    sp.dma_start(cos_q[:, :, :], dram["rope_cos_q"]).then_inc(q_tables, 16)
                    sp.dma_start(sin_q[:, :, :], dram["rope_sin_q"]).then_inc(q_tables, 16)

                @block.vector
                def _(dve):
                    then_wait = in_turn(dve, turn)
                    dve.wait_ge(loaded, 48)
                    by_seq = lambda ap: ap.rearrange("p (b h) c -> p b h c", h=HALVES)
                    for to, of in ((slice(0, 32), slice(32, 64)), (slice(32, 64), slice(0, 32))):
                        for h in range(HALVES):
                            then_wait(dve.tensor_tensor(by_seq(crossed[:, :, :])[:, :, h, to], by_seq(ctx_tok[:, :, :])[:, :, h, of],
                                                        sin_k[:, h, to].unsqueeze(1).to_broadcast([P, BATCH, 32]), ALU.mult))
                    for h in range(HALVES):
                        then_wait(dve.tensor_tensor(by_seq(kv_tok[:, :, :])[:, :, h, :], by_seq(ctx_tok[:, :, :])[:, :, h, :],
                                                    cos_k[:, h, :].unsqueeze(1).to_broadcast([P, BATCH, CTX]), ALU.mult))
                    dve.tensor_tensor(kv_tok[:, :, :], kv_tok[:, :, :], crossed[:, :, :], ALU.add).then_inc(kv_ready, 1)
                    dve.wait_ge(x_high_ready, 1)
                    dve.tensor_tensor(x_parts[1][:, :, :], chip.x_feat[:, :, :], x_parts[0][:, :, :], ALU.subtract)

                @block.tensor
                def _(pe):
                    pe.wait_ge(kv_ready, 1)
                    for t in range(TILES):
                        m = pe.transpose(ps_kv[:, t // 4, (t % 4) * P:(t % 4 + 1) * P], kv_tok[:, t, :], chip.ident[:, :])
                    m.then_inc(turned, 1)

                @block.scalar
                def _(act):
                    act.activation(x_parts[0][:, :, :], chip.x_feat[:, :, :], ACT.Copy).then_inc(x_high_ready, 1)
                    act.wait_ge(turned, 1)
                    act.activation(kv_feat[:, :], ps_kv[:, :, :].rearrange("p a t -> p (a t)"), ACT.Copy).then_inc(kept_feat, 1)
                    act.wait_ge(kept_feat, 1)

        with ExitStack() as held:
            part = Part(chip, f"{name}h", held)
            sb, ps, sem = part.sb, part.ps, part.sem
            w = sb("w", [P, 2, RA_WIDE])
            w_r = sb("w_r", [RA_R, 2, RA_CQ + CTX])
            M_parts = [sb(n, [P, KD, RA_CQ], F32R) for n in ("M_high", "M_low")]
            Z = sb("Z", [RA_HQ, 2, CTX])
            N = sb("N", [P, 2, D])
            straight = sb("straight", [RA_HQ, 2, HALF_TOK])
            crossed = sb("crossed", [RA_HQ, 2, HALF_TOK])
            zq = sb("zq", [CTX, HALF_TOK])
            attn = sb("attn", [P, 2, 2, SEQ])
            attn_t = sb("attn_t", [P, 2, SEQ])
            minus_max = sb("minus_max", [P, 2, 2])
            total = sb("total", [P, 2, 2])
            share = sb("share", [P, 2, 2])
            mixed = sb("mixed", [P, HALF_TOK])
            zeros = sb("zeros", [P, 512], BF16)
            ps_lo = ps("ps_lo", [P, 512])
            ps_hi = ps("ps_hi", [P, 512])
            ps_z = ps("ps_z", [P, 512])
            ps_s = ps("ps_s", [P, 512])
            ps_t = ps("ps_t", [P, 512])
            ps_c = ps("ps_c", [P, 512])
            ps_out = ps("ps_out", [P, 2, 2, D])
            w_loaded = [sem("w_loaded0"), sem("w_loaded1")]
            q_lo_made, m_high_ready = sem("q_lo_made"), sem("m_high_ready")
            m_made, m_kept, zn_made, zn_kept, q_made, rope_read, hi_parts, hi_roped, lo_roped = (
                sem("m_made"), sem("m_kept"), sem("zn_made"), sem("zn_kept"), sem("q_made"), sem("rope_read"),
                sem("hi_parts"), sem("hi_roped"), sem("lo_roped"))
            zq_made, zq_kept, scored, max_ready, exp_ready, share_ready, normed = (
                sem("zq_made"), sem("zq_kept"), sem("scored"), sem("max_ready"), sem("exp_ready"), sem("share_ready"),
                sem("normed"))
            t_made, t_kept, ctx_made, c_kept, out_made, zeroed, closed, out_read = (
                sem("t_made"), sem("t_kept"), sem("ctx_made"), sem("c_kept"), sem("out_made"), sem("zeroed"),
                sem("closed"), sem("out_read"))

            def steps(eng, step):
                for half in range(2):
                    base = half * RA_HEADS
                    for r in range(4):
                        step(base + r, r, (base + r) // 2, half)
                    with eng.Fori(0, RA_HEADS // 4 - 1) as i:
                        for r in range(4):
                            step(i * 4 + (base + 4 + r), r, i * 2 + (base + 4 + r) // 2, half)
                step(STEPS, 0, STEPS // 2, None)

            with nc.Block() as block:

                @block.sync
                def _(sp):
                    def step(g, r, pair, half):
                        if half is None:
                            return
                        q = r % 2
                        wait_if_positive(sp, zn_made, g - 1)
                        head = g - half * RA_HEADS
                        sp.dma_start(w[:, q, :], dram["ra_w"][bass.ds(head, 1), :, :].rearrange("a p n -> p (a n)")).then_inc(w_loaded[q], 16)
                        sp.dma_start(w_r[:, q, :], dram["ra_w_r"][bass.ds(head, 1), :, :].rearrange("a p n -> p (a n)")).then_inc(w_loaded[q], 16)

                    steps(sp, step)

                @block.gpsimd
                def _(pool):
                    pool.memset(zeros[:, :], 0.0).then_inc(zeroed, 1)

                    def step(g, r, pair, half):
                        if half is None:
                            return
                        pool.wait_ge(hi_parts, g + 1)
                        pool.tensor_tensor(straight[:, 1, :], straight[:, 1, :], crossed[:, 1, :], ALU.add).then_inc(hi_roped, 1)

                    steps(pool, step)

                @block.tensor
                def _(pe):
                    pe.wait_ge(zeroed, 1)

                    def zero_products(start, stop):
                        for t in range(2):
                            m = pe.matmul(ps_out[:, t, :, :].rearrange("p a d -> p (a d)"), zeros[:, 0:P], zeros[:, :],
                                          start=start, stop=stop)
                        return m

                    def scores(p, b, half_p):
                        pe.wait_ge(zq_kept, p + 1)
                        wait_if_positive(pe, exp_ready, p * 4 + 2 * b)
                        tokens = slice(half_p * HALF_TOK + b * SEQ, half_p * HALF_TOK + (b + 1) * SEQ)
                        for t in range(2):
                            m = pe.matmul(ps_s[:, t * SEQ:(t + 1) * SEQ], zq[:, b * SEQ + t * P:b * SEQ + (t + 1) * P],
                                          kv_feat[:, tokens], start=True, stop=True)
                        m.then_inc(scored, 1)

                    def turn_attn(p, b):
                        pe.wait_ge(normed, p * 2 + b + 1)
                        wait_if_positive(pe, t_kept, p * 2 + b)
                        for l in range(2):
                            for t in range(2):
                                m = pe.transpose(ps_t[:, l * SEQ + t * P:l * SEQ + (t + 1) * P], attn[:, b, t, l * P:(l + 1) * P],
                                                 chip.ident[:, :])
                        m.then_inc(t_made, 1)

                    def context(p, b, rows, half_p):
                        pe.wait_ge(t_kept, p * 2 + b + 1)
                        wait_if_positive(pe, c_kept, p)
                        for l in range(2):
                            m = pe.matmul(ps_c[rows, b * SEQ:(b + 1) * SEQ], kv_tok[:, 4 * half_p + 2 * b + l, :],
                                          attn_t[:, l, :], start=(l == 0), stop=(l == 1))
                        m.then_inc(ctx_made, 1)

                    def output(slot, heads_kept):
                        pe.wait_ge(c_kept, heads_kept)
                        for t in range(4):
                            m = pe.matmul(ps_out[:, t // 2, t % 2, :], mixed[:, t * P:(t + 1) * P], N[:, slot, :],
                                          start=False, stop=False)
                        m.then_inc(out_made, 1)

                    def step(g, r, pair, half):
                        q = r % 2
                        has_back = not (isinstance(g, int) and g == 0)
                        p = g - 1
                        new_half = isinstance(g, int) and g in (RA_HEADS, STEPS)
                        half_p = (g // RA_HEADS - 1) if new_half else half
                        back_rows = slice((1 - q) * CTX, (2 - q) * CTX)

                        def q_part(n, bank):
                            tokens = slice(half * HALF_TOK, (half + 1) * HALF_TOK)
                            terms = [(m_part, x_part, k) for k in range(KD) for m_part, x_part in ((0, 0), (0, 1), (1, 0))]
                            for i, (m_part, x_part, k) in enumerate(terms):
                                m = pe.matmul(bank[0:RA_HQ, :], M_parts[m_part][:, k, n * RA_HQ:(n + 1) * RA_HQ],
                                              x_parts[x_part][:, k, tokens], start=(i == 0), stop=(i == len(terms) - 1))
                            return m

                        if half is not None:
                            pe.wait_ge(w_loaded[q], (pair + 1) * 32)
                            wait_if_positive(pe, rope_read, g)
                            for k in range(KD):
                                m = pe.matmul(ps_lo[:, k * RA_CQ:(k + 1) * RA_CQ], w[:, q, k * P:(k + 1) * P],
                                              w[:, q, D:D + RA_CQ], start=True, stop=True)
                            m.then_inc(m_made, 1)
                        if has_back:
                            scores(p, 0, half_p)
                        if half is not None:
                            wait_if_positive(pe, zq_kept, g)
                            for k in range(2):
                                pe.matmul(ps_z[0:RA_HQ, k * CTX:(k + 1) * CTX], w_r[:, q, k * RA_HQ:(k + 1) * RA_HQ],
                                          w_r[:, q, RA_CQ:], start=True, stop=True)
                            m = pe.matmul(ps_z[q * CTX:(q + 1) * CTX, SEQ:2 * SEQ], w[:, q, D + RA_CQ:D + RA_CQ + CTX],
                                          w[:, q, D + RA_CQ + CTX:], start=True, stop=True)
                            m.then_inc(zn_made, 1)
                            pe.wait_ge(m_kept, g + 1)
                            q_part(0, ps_lo).then_inc(q_lo_made, 1)
                        if has_back:
                            scores(p, 1, half_p)
                            turn_attn(p, 0)
                        if half is not None:
                            q_part(1, ps_hi).then_inc(q_made, 1)
                        if has_back:
                            context(p, 0, back_rows, half_p)
                            turn_attn(p, 1)
                            if q == 1 and not (isinstance(g, int) and g % RA_HEADS == 1):
                                output(1 if r == 1 else 0, g - 1)
                            context(p, 1, back_rows, half_p)
                        if half is not None:
                            pe.wait_ge(zn_kept, g + 1)
                            pe.wait_ge(hi_roped, g + 1)
                            pe.wait_ge(lo_roped, g + 1)
                            for k in range(2):
                                m = pe.matmul(ps_z[0:CTX, :], Z[:, k, :], straight[:, k, :], start=(k == 0), stop=(k == 1))
                            m.then_inc(zq_made, 1)
                        if new_half:
                            output(1, g)
                        if new_half:
                            zero_products(False, True).then_inc(closed, 1)
                            if g < STEPS:
                                pe.wait_ge(out_read, 2)
                                zero_products(True, False)

                    zero_products(True, False)
                    steps(pe, step)

                @block.scalar
                def _(act):
                    def exps(p, b):
                        act.wait_ge(max_ready, p * 2 + b + 1)
                        wait_if_positive(act, t_made, p * 2 + b - 1)
                        for t in range(2):
                            act.activation(attn[:, b, t, :], ps_s[:, t * SEQ:(t + 1) * SEQ], ACT.Exp,
                                           bias=minus_max[:, b, t:t + 1], accum_out=total[:, b, t:t + 1]).then_inc(exp_ready, 1)

                    def keep_turned(p, b):
                        act.wait_ge(t_made, p * 2 + b + 1)
                        wait_if_positive(act, ctx_made, p * 2 + b)
                        act.activation(attn_t[:, :, :], ps_t[:, :].rearrange("p (l s) -> p l s", l=2), ACT.Copy).then_inc(t_kept, 1)

                    def step(g, r, pair, half):
                        q = r % 2
                        has_back = not (isinstance(g, int) and g == 0)
                        p = g - 1
                        if half is not None:
                            act.wait_ge(m_made, g + 1)
                            wait_if_positive(act, q_made, g)
                            act.activation(M_parts[0][:, :, :], ps_lo[:, 0:KD * RA_CQ].rearrange("p (k n) -> p k n", k=KD),
                                           ACT.Copy).then_inc(m_high_ready, 1)
                        if has_back:
                            exps(p, 0)
                        if half is not None:
                            act.wait_ge(zn_made, g + 1)
                            wait_if_positive(act, zq_made, g)
                            act.activation(Z[:, :, :], ps_z[0:RA_HQ, 0:2 * CTX].rearrange("p (k n) -> p k n", k=2), ACT.Copy)
                            wait_if_positive(act, out_made, pair - 1)
                            act.activation(N[q * CTX:(q + 1) * CTX, r // 2, :], ps_z[q * CTX:(q + 1) * CTX, SEQ:2 * SEQ],
                                           ACT.Copy).then_inc(zn_kept, 1)
                        if has_back:
                            keep_turned(p, 0)
                            exps(p, 1)
                            keep_turned(p, 1)
                            rows = slice((1 - q) * CTX, (2 - q) * CTX)
                            act.wait_ge(ctx_made, p * 2 + 2)
                            wait_if_positive(act, out_made, pair - 1 if q == 0 else pair)
                            act.activation(mixed[rows, :], ps_c[rows, :], ACT.Copy).then_inc(c_kept, 1)
                        if half is not None:
                            act.wait_ge(zq_made, g + 1)
                            wait_if_positive(act, scored, g * 2)
                            act.activation(zq[:, :], ps_z[0:CTX, :], ACT.Copy).then_inc(zq_kept, 1)

                    steps(act, step)

                @block.vector
                def _(dve):
                    dve.wait_ge(q_tables, 32)

                    def maxima(p, b):
                        dve.wait_ge(scored, p * 2 + b + 1)
                        wait_if_positive(dve, exp_ready, p * 4 + 2 * b - 2)
                        dve.tensor_reduce(minus_max[:, b, :], ps_s[:, :].rearrange("p (t l) -> p t l", t=2), AX.X, ALU.max,
                                          negate=True).then_inc(max_ready, 1)

                    def normalise(p, b):
                        dve.wait_ge(exp_ready, p * 4 + 2 * b + 2)
                        dve.reciprocal(share[:, b, :], total[:, b, :]).then_inc(share_ready, 1)
                        dve.wait_ge(share_ready, p * 2 + b + 1)
                        for t in range(2):
                            m = dve.tensor_scalar(attn[:, b, t, :], attn[:, b, t, :], share[:, b, t:t + 1], None, ALU.mult)
                        m.then_inc(normed, 1)

                    def step(g, r, pair, half):
                        has_back = not (isinstance(g, int) and g == 0)
                        p = g - 1
                        if half is not None:
                            dve.wait_ge(m_high_ready, g + 1)
                            wait_if_positive(dve, q_made, g)
                            dve.tensor_tensor(M_parts[1][:, :, :], ps_lo[:, 0:KD * RA_CQ].rearrange("p (k n) -> p k n", k=KD),
                                              M_parts[0][:, :, :], ALU.subtract).then_inc(m_kept, 1)
                        if has_back:
                            maxima(p, 0)
                            normalise(p, 0)
                            maxima(p, 1)
                        if half is not None:
                            by_batch = lambda ap: ap.rearrange("p (b t) -> p b t", b=2)
                            spread = lambda table: table.unsqueeze(1).to_broadcast([RA_HQ, 2, SEQ])
                            lo, hi = by_batch(ps_lo[0:RA_HQ, :]), by_batch(ps_hi[0:RA_HQ, :])
                            dve.wait_ge(q_lo_made, g + 1)
                            wait_if_positive(dve, zq_made, g)
                            wait_if_positive(dve, hi_roped, g)
                            wait_if_positive(dve, lo_roped, g)
                            dve.tensor_tensor(by_batch(crossed[:, 1, :]), lo, spread(sin_q[:, 1, :]), ALU.mult)
                            dve.tensor_tensor(by_batch(straight[:, 0, :]), lo, spread(cos_q[:, 0, :]), ALU.mult)
                        if has_back:
                            normalise(p, 1)
                        if half is not None:
                            dve.wait_ge(q_made, g + 1)
                            dve.tensor_tensor(by_batch(straight[:, 1, :]), hi, spread(cos_q[:, 1, :]), ALU.mult).then_inc(hi_parts, 1)
                            dve.tensor_tensor(by_batch(crossed[:, 0, :]), hi, spread(sin_q[:, 0, :]), ALU.mult).then_inc(rope_read, 1)
                            dve.wait_ge(rope_read, g + 1)
                            dve.tensor_tensor(straight[:, 0, :], straight[:, 0, :], crossed[:, 0, :], ALU.add).then_inc(lo_roped, 1)
                        if isinstance(g, int) and g in (RA_HEADS, STEPS):
                            n = g // RA_HEADS
                            dve.wait_ge(closed, n)
                            for b in range(2):
                                x = chip.x_tok[:, 4 * (n - 1) + 2 * b:4 * (n - 1) + 2 * b + 2, :]
                                dve.tensor_tensor(x, ps_out[:, b, :, :], x, ALU.add).then_inc(out_read, 1)

                    steps(dve, step)
    post_norm(chip, "ran")


def rope_inputs(given):
    import numpy as np

    def tables(width):
        inv = (np.float32(1.0) / np.float32(10000.0) ** (np.arange(0, width, 2, dtype=np.float32) / np.float32(width))).astype(np.float32)
        f = np.arange(SEQ, dtype=np.float32)[:, None] * inv[None, :]
        sin, cos = np.repeat(np.sin(f), 2, axis=-1), np.repeat(np.cos(f), 2, axis=-1)
        signed = np.concatenate([-sin[:, :width // 2], sin[:, width // 2:]], axis=-1)
        return signed.astype(np.float32), cos.astype(np.float32)

    g = lambda n: given[f"L1_xattn_{n}"]
    sin_q, cos_q = tables(RA_CQ)
    sin_k, cos_k = tables(CTX)
    by_half = lambda t: t.T.reshape(2, RA_HQ, SEQ).transpose(1, 0, 2)
    by_tile = lambda t: t.reshape(HALVES, P, CTX).transpose(1, 0, 2)
    return {
        "ctx_tok": given["ctx_512"].reshape(TILES, P, CTX).transpose(1, 0, 2),
        "rope_cos_q": by_half(cos_q), "rope_sin_q": by_half(sin_q),
        "rope_cos_k": by_tile(cos_k), "rope_sin_k": by_tile(sin_k),
        "ra_w": np.concatenate([g("Wq").reshape(RA_HEADS, RA_K, D), g("w_kc_q"), g("w_kc_kv"),
                                g("Wo").T.reshape(RA_HEADS, RA_K, D)], axis=2),
        "ra_w_r": np.concatenate([g("W_qr").transpose(0, 2, 1), g("W_kr").transpose(0, 2, 1)], axis=2),
    }


MORE.append(rope_inputs)



def load_and_constants(chip):
    nc, dram = chip.nc, chip.dram
    chip.x_tok = chip.keep("x_tok", [P, TILES, D])
    chip.x_feat = chip.keep("x_feat", [P, KD, TOK])
    chip.ident = chip.keep("ident", [P, P])
    chip.ones = chip.keep("ones", [P, P])
    chip.minus_half = chip.keep("minus_half", [P, 2])
    chip.constants_ready = chip.sem("constants_ready")
    chip.x_loaded = chip.sem("x_loaded")
    chip.CONSTANTS = 4
    with nc.Block() as block:

        @block.sync
        def _(sp):
            sp.dma_start(chip.x_feat[:, :, :], dram["x_feat"]).then_inc(chip.x_loaded, 16)
            sp.dma_start(chip.x_tok[:, :, :], dram["x_tok"]).then_inc(chip.x_loaded, 16)
            sp.wait_ge(chip.x_loaded, 32)

        @block.gpsimd
        def _(pool):
            pool.memset(chip.ident[:, :], 0.0).then_inc(chip.constants_ready, 1)
            pool.memset(chip.ones[:, :], 1.0).then_inc(chip.constants_ready, 1)
            pool.memset(chip.minus_half[:, :], -0.5).then_inc(chip.constants_ready, 1)
            pool.wait_ge(chip.constants_ready, 3)
            pool.affine_select(out=chip.ident[:, :], in_=chip.ident[:, :], compare_op=ALU.not_equal, fill=1.0,
                               base=0, pattern=[[-1, P]], channel_multiplier=1).then_inc(chip.constants_ready, 1)
            pool.wait_ge(chip.constants_ready, 4)


PARTS = [mamba2, ctx_attention, factor_ffn, bi_mamba, rope_attention, expert_ffn]


def decoder(nc, dram, parts):
    chip = Chip(nc, dram)
    with chip.kept:
        load_and_constants(chip)
        for part in parts:
            part(chip)
            chip.end_part()


def laid_out(inputs):
    import numpy as np

    def halves(w):
        k = w.shape[0] // P
        return w.reshape(k, P, -1).transpose(1, 0, 2)

    given = {n: np.asarray(a) for n, a in inputs.items()}
    x = given["x"].reshape(TOK, D)
    out = {
        "x_tok": x.reshape(TILES, P, D).transpose(1, 0, 2),
        "x_feat": halves(x.T),
        "ctx_feat": given["ctx_512"].reshape(TOK, CTX).T,
        "L0_xattn_W_k_t": given["L0_xattn_W_k"].T,
        "L0_xattn_b_k": given["L0_xattn_b_k"].reshape(CTX, 1),
        "L0_xattn_ln_gamma": given["L0_xattn_ln_gamma"].reshape(1, SEQ),
        "L0_xattn_ln_beta": given["L0_xattn_ln_beta"].reshape(1, SEQ),
        "L0_ffn_factors": given["L0_ffn_factors"].reshape(8, KD, P, D).transpose(2, 0, 1, 3),
        "L0_ffn_bias": given["L0_ffn_bias"].reshape(1, D),
        "L1_ffn_imp_center": given["L1_ffn_imp_center"].reshape(1, 8),
        "L1_ffn_imp_slope": given["L1_ffn_imp_slope"].reshape(1, 8),
        "expert_in": halves(np.concatenate([
            given["L1_ffn_select_weight"].transpose(1, 0, 2).reshape(D, 64),
            given["L1_ffn_lora_update"].transpose(1, 0, 2).reshape(D, 64),
            given["L1_ffn_select_mean_diff"].T], axis=1)),
        "expert_away": np.stack([given["L1_ffn_select_mean_diff"].T.reshape(KD, P, 8),
                                 given["L1_ffn_debias_w"].T.reshape(KD, P, 8)], axis=2).transpose(1, 0, 2, 3),
        "expert_down": np.concatenate([given["L1_ffn_lora_degen"].transpose(0, 2, 1).reshape(64, D),
                                       given["L1_ffn_bias_w"]], axis=0),
    }
    for more in MORE:
        out.update(more(given))
    return {n: np.ascontiguousarray(a) for n, a in out.items()}


def kernel(**inputs):
    import numpy as np
    import concourse.bacc as bacc
    from concourse.bass_utils import run_bass_kernel_spmd

    nc = bacc.Bacc("TRN2", target_bir_lowering=False, num_devices=1)
    arrays = laid_out(inputs)
    dram = {n: nc.dram_tensor(f"in_{n}", a.shape, mybir.dt.from_np(a.dtype), kind="ExternalInput").ap()
            for n, a in arrays.items()}
    out = nc.dram_tensor("out", (TILES, P, D), F32, kind="ExternalOutput").ap()
    dram["out"] = out.rearrange("t p d -> p t d")
    decoder(nc, dram, PARTS)
    result = run_bass_kernel_spmd(nc, [{f"in_{n}": a for n, a in arrays.items()}], core_ids=[0])
    return result.results[0]["out"].reshape(BATCH, SEQ, D)
```
